# Optimizing a Trainium2 kernel written in Bass

```python
import numpy as np
import jax
import jax.numpy as jnp

def _softmax(x, axis=-1):
    return jax.nn.softmax(x, axis=axis)

def _gelu(x):
    return jax.nn.gelu(x, approximate=True)

def _silu(x):
    return jax.nn.silu(x)

def _sigmoid(x):
    return jax.nn.sigmoid(x)

def _layernorm(x, axis=-1, eps=1e-05):
    m = jnp.mean(x, axis=axis, keepdims=True)
    v = jnp.var(x, axis=axis, keepdims=True)
    return (x - m) / jnp.sqrt(v + eps)

def _scatter_add(tgt, idx, src, axis=0):
    return tgt.at[idx].add(src)

def _segment_sum(src, seg, n):
    return jax.ops.segment_sum(src, seg, n)
kernel_name = 'mk_xattn_ffn_d4_seqx_r8_e5bb70'

def setup_inputs(seed: int=0):
    np.random.seed(seed)
    _w = jnp.asarray

    def _rec_inputs():
        import jax
        import jax.numpy as jnp
        _rk = jax.random.key(seed)
        x = 7.22e-05 + 1 * jax.random.normal(jax.random.fold_in(_rk, 1), (8, 56, 128), jnp.float32)
        _lenS = 56 - jax.random.randint(jax.random.fold_in(_rk, 7), (8,), 0, max(1, 56 // 4) + 1, jnp.int32)
        _lenS2 = 1500 - jax.random.randint(jax.random.fold_in(_rk, 8), (8,), 0, max(1, 1500 // 4) + 1, jnp.int32)
        _ctx_1024P = jax.random.normal(jax.random.fold_in(_rk, 11), (8, 16, 128), jnp.float32)
        _ctx_1024c = jax.random.dirichlet(jax.random.fold_in(_rk, 511), 0.3 * jnp.ones((16,), jnp.float32), (8, 1500))
        _ctx_1024t = jnp.einsum('bsk,bkd->bsd', _ctx_1024c, _ctx_1024P)
        _ctx_1024t = _ctx_1024t * jax.lax.rsqrt(jnp.mean(jnp.square(_ctx_1024t)) + 1e-12) * 0.953939
        ctx_1024 = 4.13588e-05 + 0.999923 * (_ctx_1024t + 0.3 * jax.random.normal(jax.random.fold_in(_rk, 611), (8, 1500, 128), jnp.float32))
        _validS = jnp.arange(56)[None, :] < _lenS[:, None]
        _validS2 = jnp.arange(1500)[None, :] < _lenS2[:, None]
        _causal = jnp.tril(jnp.ones((56, 56), dtype=bool))
        mask_BxSxS2_bf0 = jnp.logical_not(jnp.ones((8, 56, 1500), dtype=bool))
        mask_SxS2_bk0 = jnp.logical_not(jnp.broadcast_to(_validS2[0:1, :], (56, 1500)))
        mask_BxS2_bk1 = jnp.broadcast_to(_validS2[:, :], (8, 1500))
        return (x, ctx_1024, mask_BxSxS2_bf0, mask_SxS2_bk0, mask_BxS2_bk1)
    x, ctx_1024, mask_BxSxS2_bf0, mask_SxS2_bk0, mask_BxS2_bk1 = _rec_inputs()

    def _L0_xattn_setup():
        import jax, jax.numpy as jnp
        import numpy as np
        D_MODEL = 128
        NUM_HEADS = 16
        D_K = D_MODEL // NUM_HEADS
        B, S = (4, 256)
        key = jax.random.key(seed)
        ks = jax.random.split(key, 11)
        scale = 1.0 / np.sqrt(D_MODEL)
        inp = {'query': jax.random.normal(ks[0], (B, S, D_MODEL), dtype=jnp.float32), 'key': jax.random.normal(ks[1], (B, S, D_MODEL), dtype=jnp.float32), 'value': jax.random.normal(ks[2], (B, S, D_MODEL), dtype=jnp.float32), 'Wq': jax.random.normal(ks[3], (D_MODEL, D_MODEL), dtype=jnp.float32) * scale, 'bq': jnp.zeros((D_MODEL,), dtype=jnp.float32), 'Wk': jax.random.normal(ks[4], (D_MODEL, D_MODEL), dtype=jnp.float32) * scale, 'bk': jnp.zeros((D_MODEL,), dtype=jnp.float32), 'Wv': jax.random.normal(ks[5], (D_MODEL, D_MODEL), dtype=jnp.float32) * scale, 'bv': jnp.zeros((D_MODEL,), dtype=jnp.float32), 'Wo': jax.random.normal(ks[6], (D_MODEL, D_MODEL), dtype=jnp.float32) * scale, 'bo': jnp.zeros((D_MODEL,), dtype=jnp.float32)}
        return inp
    _L0_xattn_all = _L0_xattn_setup()
    _L0_xattn_in = {k: v for k, v in _L0_xattn_all.items() if k in ('Wq', 'bq', 'Wk', 'bk', 'Wv', 'bv', 'Wo', 'bo')}
    del _L0_xattn_all

    def _L0_ffn_setup():
        import jax, jax.numpy as jnp
        import numpy as np
        from jax import lax
        N_HEADS = 16
        TOP_K = 2
        N_EXPERTS = 8

        def layer_norm(x, w, b, eps=1e-05):
            mu = jnp.mean(x, axis=-1, keepdims=True)
            var = jnp.mean(jnp.square(x - mu), axis=-1, keepdims=True)
            return (x - mu) * lax.rsqrt(var + eps) * w + b

        def attention(x, w_qkv, b_qkv, w_o, b_o):
            B, T, D = x.shape
            dh = D // N_HEADS
            qkv = x @ w_qkv + b_qkv
            q, k, v = jnp.split(qkv, 3, axis=-1)
            q = q.reshape(B, T, N_HEADS, dh)
            k = k.reshape(B, T, N_HEADS, dh)
            v = v.reshape(B, T, N_HEADS, dh)
            scores = jnp.einsum('bqhd,bkhd->bhqk', q, k) / jnp.sqrt(jnp.float32(dh)).astype(x.dtype)
            probs = jax.nn.softmax(scores, axis=-1)
            ctx = jnp.einsum('bhqk,bkhd->bqhd', probs, v).reshape(B, T, D)
            return ctx @ w_o + b_o

        def moe_ff(x, w_gate, w1, b1, w2, b2):
            B, T, D = x.shape
            t = x.reshape(B * T, D)
            probs = jax.nn.softmax(t @ w_gate, axis=-1)
            tw, ti = lax.top_k(probs, TOP_K)
            tw = tw / jnp.sum(tw, axis=-1, keepdims=True)
            out = jnp.zeros_like(t)
            for e in range(N_EXPERTS):
                we = jnp.sum(jnp.where(ti == e, tw, 0.0), axis=-1)
                h = jax.nn.gelu(t @ w1[e] + b1[e]) @ w2[e] + b2[e]
                out = out + we[:, None] * h
            return out.reshape(B, T, D)
        key = jax.random.key(seed)
        ks = jax.random.split(key, 8)
        B, T, D, H, E = (4, 64, 128, 512, 8)
        s = lambda d: 1.0 / np.sqrt(d)
        return {'x': jax.random.normal(ks[0], (B, T, D), jnp.float32), 'ln1_w': jnp.ones((D,), jnp.float32), 'ln1_b': jnp.zeros((D,), jnp.float32), 'ln2_w': jnp.ones((D,), jnp.float32), 'ln2_b': jnp.zeros((D,), jnp.float32), 'w_qkv': jax.random.normal(ks[1], (D, 3 * D), jnp.float32) * s(D), 'b_qkv': jnp.zeros((3 * D,), jnp.float32), 'w_o': jax.random.normal(ks[2], (D, D), jnp.float32) * s(D), 'b_o': jnp.zeros((D,), jnp.float32), 'w_gate': jax.random.normal(ks[3], (D, E), jnp.float32) * s(D), 'w1': jax.random.normal(ks[4], (E, D, H), jnp.float32) * s(D), 'b1': jnp.zeros((E, H), jnp.float32), 'w2': jax.random.normal(ks[5], (E, H, D), jnp.float32) * s(H), 'b2': jnp.zeros((E, D), jnp.float32)}
    _L0_ffn_all = _L0_ffn_setup()
    _L0_ffn_in = {k: v for k, v in _L0_ffn_all.items() if k in ('ln1_w', 'ln1_b', 'ln2_w', 'ln2_b', 'w_qkv', 'b_qkv', 'w_o', 'b_o', 'w_gate', 'w1', 'b1', 'w2', 'b2')}
    del _L0_ffn_all

    def _L1_xattn_setup():
        import jax, jax.numpy as jnp
        import numpy as np
        D_MODEL = 128
        NUM_HEADS = 16
        D_K = D_MODEL // NUM_HEADS

        def _split_heads(x):
            B, S, _ = x.shape
            return x.reshape(B, S, NUM_HEADS, D_K).transpose(0, 2, 1, 3)
        key = jax.random.key(seed)
        ks = jax.random.split(key, 8)
        B, S = (2, 256)
        scale = 1.0 / np.sqrt(D_MODEL)
        return {'query': jax.random.normal(ks[0], (B, S, D_MODEL), jnp.float32), 'key': jax.random.normal(ks[1], (B, S, D_MODEL), jnp.float32), 'value': jax.random.normal(ks[2], (B, S, D_MODEL), jnp.float32), 'mask': jnp.zeros((B, S, S), dtype=bool), 'W_Q': jax.random.normal(ks[3], (D_MODEL, D_MODEL), jnp.float32) * scale, 'W_K': jax.random.normal(ks[4], (D_MODEL, D_MODEL), jnp.float32) * scale, 'W_V': jax.random.normal(ks[5], (D_MODEL, D_MODEL), jnp.float32) * scale, 'W_O': jax.random.normal(ks[6], (D_MODEL, D_MODEL), jnp.float32) * scale}
    _L1_xattn_all = _L1_xattn_setup()
    _L1_xattn_in = {k: v for k, v in _L1_xattn_all.items() if k in ('W_Q', 'W_K', 'W_V', 'W_O')}
    del _L1_xattn_all

    def _L1_ffn_setup():
        import jax, jax.numpy as jnp
        import numpy as np
        B, N, C, F, E, K = (2, 256, 128, 512, 8, 2)
        key = jax.random.key(seed)
        k = jax.random.split(key, 6)
        xavier1 = float(np.sqrt(6.0 / (C + F)))
        xavier2 = float(np.sqrt(6.0 / (F + C)))
        return {'x': jax.random.normal(k[0], (B, N, C), dtype=jnp.float32), 'router_w': jax.random.normal(k[1], (E, C), dtype=jnp.float32) * 0.01, 'w1': jax.random.uniform(k[2], (E, F, C), dtype=jnp.float32, minval=-xavier1, maxval=xavier1), 'b1': jnp.zeros((E, F), dtype=jnp.float32), 'w2': jax.random.uniform(k[3], (E, C, F), dtype=jnp.float32, minval=-xavier2, maxval=xavier2), 'b2': jnp.zeros((E, C), dtype=jnp.float32)}
    _L1_ffn_all = _L1_ffn_setup()
    _L1_ffn_in = {k: v for k, v in _L1_ffn_all.items() if k in ('router_w', 'w1', 'b1', 'w2', 'b2')}
    del _L1_ffn_all

    def _L2_xattn_setup():
        import jax, jax.numpy as jnp
        import numpy as np
        B, S, DIM, EMBED, HEAD = (2, 256, 128, 128, 16)
        HEAD_DIM = EMBED // HEAD
        key = jax.random.key(seed)
        ks = jax.random.split(key, 11)
        std = 1.0 / np.sqrt(DIM)
        inp = {'q': jax.random.normal(ks[0], (B, S, DIM), jnp.float32), 'k': jax.random.normal(ks[1], (B, S, DIM), jnp.float32), 'v': jax.random.normal(ks[2], (B, S, DIM), jnp.float32), 'tri_mask': jnp.tril(jnp.ones((S, S), dtype=bool)), 'padding_mask': jnp.arange(S)[None, :] < jnp.array([S, S - 32])[:, None], 'Wq': jax.random.normal(ks[3], (EMBED, DIM), jnp.float32) * std, 'bq': jnp.zeros((EMBED,), jnp.float32), 'Wk': jax.random.normal(ks[4], (EMBED, DIM), jnp.float32) * std, 'bk': jnp.zeros((EMBED,), jnp.float32), 'Wv': jax.random.normal(ks[5], (EMBED, DIM), jnp.float32) * std, 'bv': jnp.zeros((EMBED,), jnp.float32), 'Wo': jax.random.normal(ks[6], (EMBED, EMBED), jnp.float32) * std, 'bo': jnp.zeros((EMBED,), jnp.float32)}
        return inp
    _L2_xattn_all = _L2_xattn_setup()
    _L2_xattn_in = {k: v for k, v in _L2_xattn_all.items() if k in ('Wq', 'bq', 'Wk', 'bk', 'Wv', 'bv', 'Wo', 'bo')}
    del _L2_xattn_all

    def _L2_ffn_setup():
        import jax, jax.numpy as jnp
        import numpy as np
        HIDDEN = 128
        HEAD_DIM = 64
        N_EXPERTS = 16
        MIN_EXPERTS = 2
        B, T = (4, 256)

        def _normalize(x, axis):
            n = jnp.sqrt(jnp.sum(x * x, axis=axis, keepdims=True))
            return x / jnp.maximum(n, 1e-12)

        def _ste(x):
            hard = jax.lax.stop_gradient((x > 0).astype(x.dtype))
            return hard + x - jax.lax.stop_gradient(x)

        def _gating(hidden_states, sim_matrix, gates):
            b, t, c = hidden_states.shape
            flat = hidden_states.reshape(b * t, c)
            logits = _normalize(flat, -1) @ _normalize(sim_matrix, 0) - jax.nn.sigmoid(gates)
            gated = jax.nn.relu(logits)
            mask = _ste(gated)
            inactive = jnp.sum(mask, axis=1) == 0
            _, fb_idx = jax.lax.top_k(logits, MIN_EXPERTS)
            fb = jnp.zeros_like(mask).at[jnp.arange(b * t)[:, None], fb_idx].set(1.0)
            fb_applied = inactive[:, None] & (fb > 0)
            mask = jnp.where(fb_applied, 1.0, mask)
            masked_logits = jnp.where(mask > 0, gated, -jnp.inf)
            return jax.nn.softmax(masked_logits, axis=-1).reshape(b, t, -1)
        key = jax.random.key(seed)
        ks = jax.random.split(key, 6)
        xav_qkv = float(np.sqrt(6.0 / (HIDDEN + HEAD_DIM)))
        return {'hidden_states': jax.random.normal(ks[0], (B, T, HIDDEN), dtype=jnp.float32), 'sim_matrix': jax.random.normal(ks[1], (HIDDEN, N_EXPERTS), dtype=jnp.float32), 'gates': jnp.zeros((N_EXPERTS,), dtype=jnp.float32), 'q_proj': jax.random.uniform(ks[2], (N_EXPERTS, HIDDEN, HEAD_DIM), jnp.float32, -xav_qkv, xav_qkv), 'k_proj': jax.random.uniform(ks[3], (N_EXPERTS, HIDDEN, HEAD_DIM), jnp.float32, -xav_qkv, xav_qkv), 'v_proj': jax.random.uniform(ks[4], (N_EXPERTS, HIDDEN, HEAD_DIM), jnp.float32, -xav_qkv, xav_qkv), 'o_proj': jax.random.uniform(ks[5], (N_EXPERTS, HEAD_DIM, HIDDEN), jnp.float32, -xav_qkv, xav_qkv)}
    _L2_ffn_all = _L2_ffn_setup()
    _L2_ffn_in = {k: v for k, v in _L2_ffn_all.items() if k in ('sim_matrix', 'gates', 'q_proj', 'k_proj', 'v_proj', 'o_proj')}
    del _L2_ffn_all

    def _L3_xattn_setup():
        import jax, jax.numpy as jnp
        import numpy as np
        B, SQ, SKV, E, H = (4, 256, 256, 128, 16)
        D = E // H
        key = jax.random.key(seed)
        ks = jax.random.split(key, 8)
        s = 1.0 / np.sqrt(D)
        return {'query': jax.random.normal(ks[0], (B, SQ, E), jnp.float32), 'key_value': jax.random.normal(ks[1], (B, SKV, E), jnp.float32), 'wq': jax.random.normal(ks[2], (H, D, D), jnp.float32) * s, 'bq': jnp.zeros((H, D), jnp.float32), 'wk': jax.random.normal(ks[3], (H, D, D), jnp.float32) * s, 'bk': jnp.zeros((H, D), jnp.float32), 'wv': jax.random.normal(ks[4], (H, D, D), jnp.float32) * s, 'bv': jnp.zeros((H, D), jnp.float32), 'wo': jax.random.normal(ks[5], (E, E), jnp.float32) * (1.0 / np.sqrt(E)), 'bo': jnp.zeros((E,), jnp.float32)}
    _L3_xattn_all = _L3_xattn_setup()
    _L3_xattn_in = {k: v for k, v in _L3_xattn_all.items() if k in ('wq', 'bq', 'wk', 'bk', 'wv', 'bv', 'wo', 'bo')}
    del _L3_xattn_all

    def _L3_ffn_setup():
        import jax, jax.numpy as jnp
        import numpy as np
        B, T, D, E, H, K = (2, 256, 128, 8, 512, 2)
        key = jax.random.key(seed)
        ks = jax.random.split(key, 8)
        s = 0.02
        return {'x': jax.random.normal(ks[0], (B, T, D), jnp.float32), 'rw1': jax.random.normal(ks[1], (D, D), jnp.float32) * s, 'rb1': jnp.zeros((D,), jnp.float32), 'rw2': jax.random.normal(ks[2], (D, E), jnp.float32) * s, 'rb2': jnp.zeros((E,), jnp.float32), 'we1': jax.random.normal(ks[3], (E, D, H), jnp.float32) * s, 'be1': jnp.zeros((E, H), jnp.float32), 'we2': jax.random.normal(ks[4], (E, H, D), jnp.float32) * s, 'be2': jnp.zeros((E, D), jnp.float32)}
    _L3_ffn_all = _L3_ffn_setup()
    _L3_ffn_in = {k: v for k, v in _L3_ffn_all.items() if k in ('rw1', 'rb1', 'rw2', 'rb2', 'we1', 'be1', 'we2', 'be2')}
    del _L3_ffn_all
    return {'x': x, 'ctx_1024': ctx_1024, 'mask_BxSxS2_bf0': mask_BxSxS2_bf0, 'mask_SxS2_bk0': mask_SxS2_bk0, 'mask_BxS2_bk1': mask_BxS2_bk1, 'L0_xattn_Wq': _L0_xattn_in['Wq'], 'L0_xattn_bq': _L0_xattn_in['bq'], 'L0_xattn_Wk': _L0_xattn_in['Wk'], 'L0_xattn_bk': _L0_xattn_in['bk'], 'L0_xattn_Wv': _L0_xattn_in['Wv'], 'L0_xattn_bv': _L0_xattn_in['bv'], 'L0_xattn_Wo': _L0_xattn_in['Wo'], 'L0_xattn_bo': _L0_xattn_in['bo'], 'L0_ffn_ln1_w': _L0_ffn_in['ln1_w'], 'L0_ffn_ln1_b': _L0_ffn_in['ln1_b'], 'L0_ffn_ln2_w': _L0_ffn_in['ln2_w'], 'L0_ffn_ln2_b': _L0_ffn_in['ln2_b'], 'L0_ffn_w_qkv': _L0_ffn_in['w_qkv'], 'L0_ffn_b_qkv': _L0_ffn_in['b_qkv'], 'L0_ffn_w_o': _L0_ffn_in['w_o'], 'L0_ffn_b_o': _L0_ffn_in['b_o'], 'L0_ffn_w_gate': _L0_ffn_in['w_gate'], 'L0_ffn_w1': _L0_ffn_in['w1'], 'L0_ffn_b1': _L0_ffn_in['b1'], 'L0_ffn_w2': _L0_ffn_in['w2'], 'L0_ffn_b2': _L0_ffn_in['b2'], 'L1_xattn_W_Q': _L1_xattn_in['W_Q'], 'L1_xattn_W_K': _L1_xattn_in['W_K'], 'L1_xattn_W_V': _L1_xattn_in['W_V'], 'L1_xattn_W_O': _L1_xattn_in['W_O'], 'L1_ffn_router_w': _L1_ffn_in['router_w'], 'L1_ffn_w1': _L1_ffn_in['w1'], 'L1_ffn_b1': _L1_ffn_in['b1'], 'L1_ffn_w2': _L1_ffn_in['w2'], 'L1_ffn_b2': _L1_ffn_in['b2'], 'L2_xattn_Wq': _L2_xattn_in['Wq'], 'L2_xattn_bq': _L2_xattn_in['bq'], 'L2_xattn_Wk': _L2_xattn_in['Wk'], 'L2_xattn_bk': _L2_xattn_in['bk'], 'L2_xattn_Wv': _L2_xattn_in['Wv'], 'L2_xattn_bv': _L2_xattn_in['bv'], 'L2_xattn_Wo': _L2_xattn_in['Wo'], 'L2_xattn_bo': _L2_xattn_in['bo'], 'L2_ffn_sim_matrix': _L2_ffn_in['sim_matrix'], 'L2_ffn_gates': _L2_ffn_in['gates'], 'L2_ffn_q_proj': _L2_ffn_in['q_proj'], 'L2_ffn_k_proj': _L2_ffn_in['k_proj'], 'L2_ffn_v_proj': _L2_ffn_in['v_proj'], 'L2_ffn_o_proj': _L2_ffn_in['o_proj'], 'L3_xattn_wq': _L3_xattn_in['wq'], 'L3_xattn_bq': _L3_xattn_in['bq'], 'L3_xattn_wk': _L3_xattn_in['wk'], 'L3_xattn_bk': _L3_xattn_in['bk'], 'L3_xattn_wv': _L3_xattn_in['wv'], 'L3_xattn_bv': _L3_xattn_in['bv'], 'L3_xattn_wo': _L3_xattn_in['wo'], 'L3_xattn_bo': _L3_xattn_in['bo'], 'L3_ffn_rw1': _L3_ffn_in['rw1'], 'L3_ffn_rb1': _L3_ffn_in['rb1'], 'L3_ffn_rw2': _L3_ffn_in['rw2'], 'L3_ffn_rb2': _L3_ffn_in['rb2'], 'L3_ffn_we1': _L3_ffn_in['we1'], 'L3_ffn_be1': _L3_ffn_in['be1'], 'L3_ffn_we2': _L3_ffn_in['we2'], 'L3_ffn_be2': _L3_ffn_in['be2']}

def reference(x, ctx_1024, mask_BxSxS2_bf0, mask_SxS2_bk0, mask_BxS2_bk1, L0_xattn_Wq, L0_xattn_bq, L0_xattn_Wk, L0_xattn_bk, L0_xattn_Wv, L0_xattn_bv, L0_xattn_Wo, L0_xattn_bo, L0_ffn_ln1_w, L0_ffn_ln1_b, L0_ffn_ln2_w, L0_ffn_ln2_b, L0_ffn_w_qkv, L0_ffn_b_qkv, L0_ffn_w_o, L0_ffn_b_o, L0_ffn_w_gate, L0_ffn_w1, L0_ffn_b1, L0_ffn_w2, L0_ffn_b2, L1_xattn_W_Q, L1_xattn_W_K, L1_xattn_W_V, L1_xattn_W_O, L1_ffn_router_w, L1_ffn_w1, L1_ffn_b1, L1_ffn_w2, L1_ffn_b2, L2_xattn_Wq, L2_xattn_bq, L2_xattn_Wk, L2_xattn_bk, L2_xattn_Wv, L2_xattn_bv, L2_xattn_Wo, L2_xattn_bo, L2_ffn_sim_matrix, L2_ffn_gates, L2_ffn_q_proj, L2_ffn_k_proj, L2_ffn_v_proj, L2_ffn_o_proj, L3_xattn_wq, L3_xattn_bq, L3_xattn_wk, L3_xattn_bk, L3_xattn_wv, L3_xattn_bv, L3_xattn_wo, L3_xattn_bo, L3_ffn_rw1, L3_ffn_rb1, L3_ffn_rw2, L3_ffn_rb2, L3_ffn_we1, L3_ffn_be1, L3_ffn_we2, L3_ffn_be2):
    import jax
    import jax.numpy as jnp

    def _L0_xattn_ref(query, key, value, Wq, bq, Wk, bk, Wv, bv, Wo, bo):
        import jax, jax.numpy as jnp
        import numpy as np
        D_MODEL = 128
        NUM_HEADS = 16
        D_K = D_MODEL // NUM_HEADS
        B, S = (4, 256)
        b, sq, _ = query.shape
        sk = key.shape[1]
        Q = query @ Wq + bq
        K = key @ Wk + bk
        V = value @ Wv + bv
        Q = Q.reshape(b, sq, NUM_HEADS, D_K).transpose(0, 2, 1, 3)
        K = K.reshape(b, sk, NUM_HEADS, D_K).transpose(0, 2, 1, 3)
        V = V.reshape(b, sk, NUM_HEADS, D_K).transpose(0, 2, 1, 3)
        scores = jnp.einsum('bhqd,bhkd->bhqk', Q, K) / jnp.sqrt(jnp.float32(D_K))
        attn = jax.nn.softmax(scores, axis=-1)
        out = jnp.einsum('bhqk,bhkd->bhqd', attn, V)
        out = out.transpose(0, 2, 1, 3).reshape(b, sq, D_MODEL)
        return out @ Wo + bo

    def _L0_ffn_ref(x, ln1_w, ln1_b, ln2_w, ln2_b, w_qkv, b_qkv, w_o, b_o, w_gate, w1, b1, w2, b2):
        import jax, jax.numpy as jnp
        import numpy as np
        from jax import lax
        N_HEADS = 16
        TOP_K = 2
        N_EXPERTS = 8

        def layer_norm(x, w, b, eps=1e-05):
            mu = jnp.mean(x, axis=-1, keepdims=True)
            var = jnp.mean(jnp.square(x - mu), axis=-1, keepdims=True)
            return (x - mu) * lax.rsqrt(var + eps) * w + b

        def attention(x, w_qkv, b_qkv, w_o, b_o):
            B, T, D = x.shape
            dh = D // N_HEADS
            qkv = x @ w_qkv + b_qkv
            q, k, v = jnp.split(qkv, 3, axis=-1)
            q = q.reshape(B, T, N_HEADS, dh)
            k = k.reshape(B, T, N_HEADS, dh)
            v = v.reshape(B, T, N_HEADS, dh)
            scores = jnp.einsum('bqhd,bkhd->bhqk', q, k) / jnp.sqrt(jnp.float32(dh)).astype(x.dtype)
            probs = jax.nn.softmax(scores, axis=-1)
            ctx = jnp.einsum('bhqk,bkhd->bqhd', probs, v).reshape(B, T, D)
            return ctx @ w_o + b_o

        def moe_ff(x, w_gate, w1, b1, w2, b2):
            B, T, D = x.shape
            t = x.reshape(B * T, D)
            probs = jax.nn.softmax(t @ w_gate, axis=-1)
            tw, ti = lax.top_k(probs, TOP_K)
            tw = tw / jnp.sum(tw, axis=-1, keepdims=True)
            out = jnp.zeros_like(t)
            for e in range(N_EXPERTS):
                we = jnp.sum(jnp.where(ti == e, tw, 0.0), axis=-1)
                h = jax.nn.gelu(t @ w1[e] + b1[e]) @ w2[e] + b2[e]
                out = out + we[:, None] * h
            return out.reshape(B, T, D)
        h = x + attention(layer_norm(x, ln1_w, ln1_b), w_qkv, b_qkv, w_o, b_o)
        return h + moe_ff(layer_norm(h, ln2_w, ln2_b), w_gate, w1, b1, w2, b2)

    def _L1_xattn_ref(query, key, value, mask, W_Q, W_K, W_V, W_O):
        import jax, jax.numpy as jnp
        import numpy as np
        D_MODEL = 128
        NUM_HEADS = 16
        D_K = D_MODEL // NUM_HEADS

        def _split_heads(x):
            B, S, _ = x.shape
            return x.reshape(B, S, NUM_HEADS, D_K).transpose(0, 2, 1, 3)
        Q = _split_heads(jnp.einsum('bsd,ed->bse', query, W_Q))
        K = _split_heads(jnp.einsum('bsd,ed->bse', key, W_K))
        V = _split_heads(jnp.einsum('bsd,ed->bse', value, W_V))
        scores = jnp.einsum('bhqd,bhkd->bhqk', Q, K) / jnp.sqrt(jnp.float32(D_K))
        m = mask[:, None, :, :]
        scores = jnp.where(m, -jnp.inf, scores)
        attn = jax.nn.softmax(scores, axis=-1)
        attn = jnp.where(jnp.isnan(attn), 0.0, attn)
        out = jnp.einsum('bhqk,bhkd->bhqd', attn, V)
        B, H, S, _ = out.shape
        out = out.transpose(0, 2, 1, 3).reshape(B, S, D_MODEL)
        return jnp.einsum('bsd,ed->bse', out, W_O)

    def _L1_ffn_ref(x, router_w, w1, b1, w2, b2):
        import jax, jax.numpy as jnp
        import numpy as np
        B, N, C, F, E, K = (2, 256, 128, 512, 8, 2)
        Bb, Nn, Cc = x.shape
        x_flat = x.reshape(-1, Cc)
        logits = jnp.einsum('tc,ec->te', x_flat, router_w)
        probs = jax.nn.softmax(logits, axis=-1)
        top_w, top_idx = jax.lax.top_k(probs, K)
        top_w = top_w / (jnp.sum(top_w, axis=-1, keepdims=True) + 1e-09)
        h = jnp.einsum('tc,efc->tef', x_flat, w1) + b1[None]
        h = jax.nn.relu(h)
        y = jnp.einsum('tef,ecf->tec', h, w2) + b2[None]
        sel = jnp.take_along_axis(y, top_idx[:, :, None], axis=1)
        out = jnp.einsum('tkc,tk->tc', sel, top_w)
        return out.reshape(Bb, Nn, Cc)

    def _L2_xattn_ref(q, k, v, tri_mask, padding_mask, Wq, bq, Wk, bk, Wv, bv, Wo, bo):
        import jax, jax.numpy as jnp
        import numpy as np
        B, S, DIM, EMBED, HEAD = (2, 256, 128, 128, 16)
        HEAD_DIM = EMBED // HEAD
        scale = EMBED ** (-0.5)
        neg = jnp.finfo(q.dtype).min

        def split_heads(x):
            b, s, _ = x.shape
            return x.reshape(b, s, HEAD, HEAD_DIM).transpose(0, 2, 1, 3)
        qh = split_heads(q @ Wq.T + bq)
        kh = split_heads(k @ Wk.T + bk)
        vh = split_heads(v @ Wv.T + bv)
        energy = jnp.einsum('bhse,bhke->bhsk', qh, kh) * scale
        keep = padding_mask[:, None, None, :] & tri_mask[None, None, :, :]
        energy = jnp.where(keep, energy, neg)
        attn = jax.nn.softmax(energy, axis=-1)
        out = jnp.einsum('bhsk,bhke->bhse', attn, vh)
        out = out.transpose(0, 2, 1, 3).reshape(q.shape[0], q.shape[1], EMBED)
        return out @ Wo.T + bo

    def _L2_ffn_ref(hidden_states, sim_matrix, gates, q_proj, k_proj, v_proj, o_proj):
        import jax, jax.numpy as jnp
        import numpy as np
        HIDDEN = 128
        HEAD_DIM = 64
        N_EXPERTS = 16
        MIN_EXPERTS = 2
        B, T = (4, 256)

        def _normalize(x, axis):
            n = jnp.sqrt(jnp.sum(x * x, axis=axis, keepdims=True))
            return x / jnp.maximum(n, 1e-12)

        def _ste(x):
            hard = jax.lax.stop_gradient((x > 0).astype(x.dtype))
            return hard + x - jax.lax.stop_gradient(x)

        def _gating(hidden_states, sim_matrix, gates):
            b, t, c = hidden_states.shape
            flat = hidden_states.reshape(b * t, c)
            logits = _normalize(flat, -1) @ _normalize(sim_matrix, 0) - jax.nn.sigmoid(gates)
            gated = jax.nn.relu(logits)
            mask = _ste(gated)
            inactive = jnp.sum(mask, axis=1) == 0
            _, fb_idx = jax.lax.top_k(logits, MIN_EXPERTS)
            fb = jnp.zeros_like(mask).at[jnp.arange(b * t)[:, None], fb_idx].set(1.0)
            fb_applied = inactive[:, None] & (fb > 0)
            mask = jnp.where(fb_applied, 1.0, mask)
            masked_logits = jnp.where(mask > 0, gated, -jnp.inf)
            return jax.nn.softmax(masked_logits, axis=-1).reshape(b, t, -1)
        b, t, c = hidden_states.shape
        rw = _gating(hidden_states, sim_matrix, gates)
        q = jnp.einsum('bte,bted->btd', rw, jnp.einsum('btc,ecd->bted', hidden_states, q_proj))
        k = jnp.einsum('bte,bted->btd', rw, jnp.einsum('btc,ecd->bted', hidden_states, k_proj))
        v = jnp.einsum('bte,bted->btd', rw, jnp.einsum('btc,ecd->bted', hidden_states, v_proj))
        scale = 1.0 / jnp.sqrt(jnp.asarray(HEAD_DIM, dtype=q.dtype))
        scores = jnp.einsum('bqd,bkd->bqk', q, k) * scale
        causal = jnp.tril(jnp.ones((t, t), dtype=bool))
        scores = jnp.where(causal, scores, -jnp.inf)
        attn = jnp.einsum('bqk,bkd->bqd', jax.nn.softmax(scores, axis=-1), v)
        mixed = attn[:, :, None, :] * rw[..., None]
        return jnp.einsum('bted,edc->btc', mixed, o_proj)

    def _L3_xattn_ref(query, key_value, wq, bq, wk, bk, wv, bv, wo, bo):
        import jax, jax.numpy as jnp
        import numpy as np
        B, SQ, SKV, E, H = (4, 256, 256, 128, 16)
        D = E // H
        b, sq, e = query.shape
        skv = key_value.shape[1]
        h, d = (wq.shape[0], wq.shape[1])
        q = query.reshape(b, sq, h, d)
        kv = key_value.reshape(b, skv, h, d)
        qh = jnp.einsum('bshd,hed->bshe', q, wq) + bq
        kh = jnp.einsum('bthd,hed->bthe', kv, wk) + bk
        vh = jnp.einsum('bthd,hed->bthe', kv, wv) + bv
        scores = jnp.einsum('bshd,bthd->bhst', qh, kh) / jnp.sqrt(jnp.asarray(d, qh.dtype))
        attn = jax.nn.softmax(scores, axis=-1)
        ctx = jnp.einsum('bhst,bthd->bshd', attn, vh)
        out = ctx.reshape(b, sq, e)
        return out @ wo.T + bo

    def _L3_ffn_ref(x, rw1, rb1, rw2, rb2, we1, be1, we2, be2):
        import jax, jax.numpy as jnp
        import numpy as np
        B, T, D, E, H, K = (2, 256, 128, 8, 512, 2)
        b, t, d = x.shape
        xt = x.reshape(b * t, d)
        n = xt.shape[0]
        logits = jax.nn.silu(xt @ rw1 + rb1) @ rw2 + rb2
        _, idx = jax.lax.top_k(logits, K)
        mask = jnp.zeros((n, E), bool).at[jnp.arange(n)[:, None], idx].set(True)
        w = jax.nn.softmax(jnp.where(mask, logits, -jnp.inf), axis=1)
        h = jax.nn.silu(jnp.einsum('nd,edh->enh', xt, we1) + be1[:, None, :])
        eo = jnp.einsum('enh,ehd->end', h, we2) + be2[:, None, :]
        y = xt + jnp.einsum('ne,end->nd', w, eo)
        return y.reshape(b, t, d)
    x = x + _L0_xattn_ref(_layernorm(x, axis=-1), ctx_1024, ctx_1024, L0_xattn_Wq, L0_xattn_bq, L0_xattn_Wk, L0_xattn_bk, L0_xattn_Wv, L0_xattn_bv, L0_xattn_Wo, L0_xattn_bo)
    x = x + _L0_ffn_ref(_layernorm(x, axis=-1), L0_ffn_ln1_w, L0_ffn_ln1_b, L0_ffn_ln2_w, L0_ffn_ln2_b, L0_ffn_w_qkv, L0_ffn_b_qkv, L0_ffn_w_o, L0_ffn_b_o, L0_ffn_w_gate, L0_ffn_w1, L0_ffn_b1, L0_ffn_w2, L0_ffn_b2)
    x = x + _L1_xattn_ref(_layernorm(x, axis=-1), ctx_1024, ctx_1024, mask_BxSxS2_bf0, L1_xattn_W_Q, L1_xattn_W_K, L1_xattn_W_V, L1_xattn_W_O)
    x = x + _L1_ffn_ref(_layernorm(x, axis=-1), L1_ffn_router_w, L1_ffn_w1, L1_ffn_b1, L1_ffn_w2, L1_ffn_b2)
    x = x + _L2_xattn_ref(_layernorm(x, axis=-1), ctx_1024, ctx_1024, mask_SxS2_bk0, mask_BxS2_bk1, L2_xattn_Wq, L2_xattn_bq, L2_xattn_Wk, L2_xattn_bk, L2_xattn_Wv, L2_xattn_bv, L2_xattn_Wo, L2_xattn_bo)
    x = x + _L2_ffn_ref(_layernorm(x, axis=-1), L2_ffn_sim_matrix, L2_ffn_gates, L2_ffn_q_proj, L2_ffn_k_proj, L2_ffn_v_proj, L2_ffn_o_proj)
    x = x + _L3_xattn_ref(_layernorm(x, axis=-1), ctx_1024, L3_xattn_wq, L3_xattn_bq, L3_xattn_wk, L3_xattn_bk, L3_xattn_wv, L3_xattn_bv, L3_xattn_wo, L3_xattn_bo)
    x = x + _L3_ffn_ref(_layernorm(x, axis=-1), L3_ffn_rw1, L3_ffn_rb1, L3_ffn_rw2, L3_ffn_rb2, L3_ffn_we1, L3_ffn_be1, L3_ffn_we2, L3_ffn_be2)
    return x

_drawn_inputs = setup_inputs


def setup_inputs(seed=0):
    import zlib

    import numpy as np

    out = dict(_drawn_inputs(seed))
    spreads = {'L0_xattn_bq': (0.0, 0.1),
     'L0_xattn_bk': (0.0, 0.8),
     'L0_xattn_bv': (0.0, 0.1),
     'L0_xattn_bo': (0.0, 0.1),
     'L0_ffn_ln1_w': (1.0, 0.2),
     'L0_ffn_ln1_b': (0.0, 0.1),
     'L0_ffn_ln2_w': (1.0, 0.2),
     'L0_ffn_ln2_b': (0.0, 0.1),
     'L0_ffn_b_qkv': (0.0, 0.1),
     'L0_ffn_b_o': (0.0, 0.1),
     'L0_ffn_b1': (0.0, 0.1),
     'L0_ffn_b2': (0.0, 0.1),
     'L1_ffn_b1': (0.0, 0.1),
     'L1_ffn_b2': (0.0, 0.1),
     'L2_xattn_bq': (0.0, 0.1),
     'L2_xattn_bk': (0.0, 0.1),
     'L2_xattn_bv': (0.0, 0.1),
     'L2_xattn_bo': (0.0, 0.1),
     'L2_ffn_gates': (0.0, 0.1),
     'L3_xattn_bq': (0.0, 0.64),
     'L3_xattn_bk': (0.0, 0.8),
     'L3_xattn_bv': (0.0, 0.1),
     'L3_xattn_bo': (0.0, 0.1),
     'L3_ffn_rb1': (0.0, 0.8),
     'L3_ffn_rb2': (0.0, 0.337),
     'L3_ffn_be1': (0.0, 0.8),
     'L3_ffn_be2': (0.0, 0.417)}
    factors = {'L3_ffn_rw1': 4.621, 'L3_ffn_rw2': 4.498, 'L3_ffn_we1': 5.526, 'L3_ffn_we2': 5.096}
    for name, (base, spread) in spreads.items():
        noise = np.random.default_rng([zlib.crc32(name.encode()), seed]).standard_normal(out[name].shape)
        drawn = base * np.exp(spread * noise) if base else spread * noise
        out[name] = jnp.asarray(drawn.astype(out[name].dtype))
    for name, factor in factors.items():
        out[name] = (out[name] * factor).astype(out[name].dtype)
    return out
```

```python
from contextlib import ExitStack

import concourse.bass as bass
from concourse import mybir
import numpy as np

F32 = mybir.dt.float32
F16 = mybir.dt.float16
BF16 = mybir.dt.bfloat16
U8 = mybir.dt.uint8
ALU = mybir.AluOpType
ACT = mybir.ActivationFunctionType
AX = mybir.AxisListType

P = 128
B, S, D = 8, 56, 128
H, DH = 16, 8
KV = 1500
KT = 12
KK = KV // KT
KPAD = 1504
L = 4
G = L * B
T = 2 * S
NT = B // 2
TOK = B * S
QUADS, HQ = 4, 4
HC = H * S
CH = HC // P
KS = 3
KP = KV // KS
E, F, FC = 8, 512, 4
SLOTS = 3
MASKED = (1, 2)
MASK = -32768.0
NEG = -(2.0 ** 100)
E2, HD2 = 16, 64

C_ID, C_PERM, C_BM, C_M4, C_SEL, C_BLK, C_CAU, C_RANK, C_HOT = 0, 128, 256, 272, 276, 278, 390, 502, 518
C_W = C_HOT + HC
R_LN1W, R_LN1B, R_LN2W, R_LN2B, R_BO, R_FBO, R_FBV, R_RB2, R_GATE = 0, 1, 2, 3, 4, 8, 9, 10, 11
R_N = 12


def aux_slots(g):
    slots = [[] for _ in range(KT)]
    if (g + 1) % B and g + 1 < G:
        n = 0
        for s in range(10):
            for _ in range(3 if s == 0 else 2):
                slots[s].append(("S", g + 1, n))
                n += 1
        slots[10] += [("M", g + 1, 0), ("M", g + 1, 1)]
    if g + 1 < G:
        for i, s in enumerate((1, 4, 7)):
            slots[s].append(("V", g + 1, i))
    if g + 2 < G:
        for i, s in enumerate((2, 5, 8)):
            slots[s].append(("K", g + 2, i))
    return slots


def head_items(g):
    return [("S", g, n) for n in range(CH * KS)] + [("M", g, 0), ("M", g, 1)]


FIRST_ITEMS = [("K", 0, i) for i in range(KS)] + [("V", 0, i) for i in range(3)] + [("K", 1, i) for i in range(KS)]


def all_items():
    items = list(FIRST_ITEMS)
    for g in range(G):
        if g % B == 0:
            items += head_items(g)
        for slot in aux_slots(g):
            items += slot
    return items


TOP2 = ["v1", "eq1", "sc1", "m1", "oh1", "p2", "v2", "eq2", "sc2", "m2", "oh2"]
PAIRS, FOURS = NT * E2 // 2, NT * E2 // 4


def phase_steps(phase):
    kind, n = phase
    if kind == "ln":
        return {"dve": ["stats", "aggr", "var", "norm"], "pool": ["rstd"]}
    if kind == "affine":
        return {"dve": ["mul", "add"]}
    if kind == "turn":
        return {"pe": ["turned"], "act": ["copied"]}
    if kind == "count":
        return {"pe": ["count"], "dve": ["keep"]}
    if kind == "q":
        return {"pe": ["q"], "dve": ["scaled"] + ["kept"] * (n == 2) + ["q16", "lo"], "act": ["hi", "hi_lo"]}
    if kind == "out":
        return {"dve": ["biased", "with_bo", "added"], "pe": ["projected"]}
    if kind == "moe":
        pe = ["r1"] * (n == 2) + ["gate", "h0"]
        for e in range(E):
            pe += [f"h{e + 1}"] * (e + 1 < E) + [f"y{e}"]
        softmax = ["max", "shift", "sum", "recip", "probs"] * (n != 2)
        weigh = ["gap", "plus", "inv", "second", "w1", "w2", "W"] if n == 2 else ["chosen", "den", "inv", "cp", "W"]
        return {"pe": pe + ["w_turned", "b2"],
                "act": ["r1"] * (n == 2) + ["exp"] + [f"h{e}_{c}" for e in range(E) for c in range(FC)] + ["w_copied"],
                "dve": ["logits"] + softmax + TOP2 + weigh + ["base"] * (n != 1) + [f"acc{e}" for e in range(E)] + ["b2"]}
    if kind == "self":
        return {"pe": ["qk", "v"] + [f"{s}{t}" for t in range(NT) for s in ("s", "t", "o")] + ["o_turned", "proj"],
                "act": [f"{s}{t}" for t in range(NT) for s in ("exp", "pt")] + ["o_copied"],
                "dve": ["q", "k", "v"] + [f"{s}{t}" for t in range(NT) for s in ("kb", "max", "shift", "sum", "recip", "o")]
                + ["hb", "h"]}
    assert kind == "gated"
    return {"pe": ["sim2", "logits"] + [f"p{i}" for i in range(PAIRS)] + ["qk_turned"]
            + [f"{s}{t}" for t in range(NT) for s in ("s", "t", "o")] + ["a_turned"] + [f"f{i}" for i in range(FOURS)],
            "act": ["gate_exp", "exp", "qk_copied"] + [f"{s}{t}" for t in range(NT) for s in ("exp", "pt")] + ["a_copied"],
            "pool": ["sim_norm", "y_norm"],
            "dve": ["sim2", "y2", "y2_sum", "y2_max", "sim2_max", "sim_unit", "gate1", "gate", "cos", "logits", "pos", "any",
                    "gated", "gmax"] + TOP2 + ["two", "none", "fallback", "active", "shift", "em", "sum", "recip", "rw"]
            + [f"p{i}{k}" for i in range(PAIRS) for k in "ab"]
            + [f"{s}{t}" for t in range(NT) for s in ("mask", "max", "shift", "sum", "recip", "o")]
            + [f"f{i}_{k}" for i in range(FOURS) for k in range(4)]}


def program_order():
    seq = []
    turn = ln = moe = 0
    for l in range(L):
        if l in MASKED:
            seq.append(("count", l))
        seq += [("ln", ln), ("turn", turn), ("q", l), ("out", l), ("ln", ln + 1)]
        ln, turn = ln + 2, turn + 1
        if l == 0:
            seq += [("ln", ln), ("affine", 0), ("turn", turn), ("self", 0), ("ln", ln + 1), ("affine", 1)]
            ln, turn = ln + 2, turn + 1
        seq.append(("turn", turn))
        turn += 1
        if l == 2:
            seq.append(("gated", 0))
        else:
            seq.append(("moe", moe))
            moe += 1
    return seq


def step_counts():
    n = {"pe": 0, "act": 0, "dve": 0, "pool": 0}
    at = {}
    for phase in program_order():
        for who, names in phase_steps(phase).items():
            for step in names:
                n[who] += 1
                at[(who, phase, step)] = n[who]
    return at


def build(nc, a, out):
    at = step_counts()
    items = all_items()
    place = {item: n for n, item in enumerate(items)}

    with ExitStack() as ctx:
        def sb(name, shape, dt):
            return ctx.enter_context(nc.sbuf_tensor(name, shape, dt))

        def sem(name):
            return ctx.enter_context(nc.semaphore(name))

        ps = ctx.enter_context(nc.psum_tensor("ps", [P, 8, 512], F32))
        BANK_PV, BANK_AUX = 4, 6

        ctxT = sb("ctxT", [P, 3, KV], F32)
        khi = sb("khi", [P, 2, KV], F16)
        klo = sb("klo", [P, 2, KV], F16)
        kq = sb("kq", [P, 2, QUADS, KPAD], F16)
        v_aug = sb("v_aug", [P, 2, KT, 8, 32], F32)
        probs = sb("probs", [P, 2, HC], F32)
        qn = sb("qn", [P, 2, H, S], F16)
        qb = sb("qb", [P, 2, QUADS, HQ, S], F16)
        mx_part = sb("mx_part", [P, 2, CH, KS], F32)
        mx = sb("mx", [P, 2, 8], F32)
        oc_t = sb("oc_t", [P, 2, S], F32)
        oc = sb("oc", [P, 2, S], F32)
        rden = sb("rden", [P, 2, S], F32)
        o_all = sb("o_all", [P, 2, TOK], F32)
        mask_u8 = sb("mask_u8", [S, 2, KV], U8)
        tri_u8 = sb("tri_u8", [S, KV], U8)
        mask_q = sb("mask_q", [P, 2, KV], BF16)
        maskT_u8 = sb("maskT_u8", [P, B, KT, S], U8)
        triT_u8 = sb("triT_u8", [P, KT, S], U8)
        padT_u8 = sb("padT_u8", [P, B, KT], U8)
        mask_t = sb("mask_t", [P, B, KT, S], BF16)
        keep = sb("keep", [P, TOK], F32)
        weights = sb("weights", [P, 5120], F32)
        big1 = sb("big1", [P, 4, TOK], F32)
        big2 = sb("big2", [P, 4, TOK], F32)
        big0 = probs[:, :, :].rearrange("p a c -> p (a c)").rearrange("p (a c) -> p a c", a=4)
        kvw = sb("kvw", [P, L, 256], F32)
        xw = sb("xw", [P, 7 * D], F32)
        xb = sb("xb", [P, L, 8], F32)
        rows = sb("rows", [T, R_N, D], F32)
        cst = sb("cst", [P, C_W - HC], F32)
        hot_f = big1[:, 0:2, :].rearrange("p a c -> p (a c)")
        hot = sb("hot", [P, HC], BF16)
        id_mask = sb("id_mask", [P, P], BF16)
        id_b = sb("id_b", [P, P], BF16)
        blk_b = sb("blk_b", [P, T], BF16)
        ones_b = sb("ones_b", [P, P], BF16)
        ones_f = sb("ones_f", [P, P], F32)
        bm16 = sb("bm16", [P, H], F16)
        m4 = sb("m4", [P, HQ], F16)
        x = sb("x", [T, NT, D], F32)
        y = sb("y", [T, NT, D], F32)
        z = sb("z", [T, NT, D], F32)
        hbuf = sb("hbuf", [T, NT, D], F32)
        yT = sb("yT", [P, TOK], F32)
        qnf = sb("qnf", [P, TOK], F32)
        qn16 = sb("qn16", [P, TOK], F16)
        st = sb("st", [T, NT, 6], F32)
        mv = sb("mv", [T, NT, 2], F32)
        ve = sb("ve", [T, NT], F32)
        rstd = sb("rstd", [T, NT], F32)
        mhalf = sb("mhalf", [P, NT * 8], F32)
        sm = sb("sm", [T, 16, NT * E2], F32)
        s1 = sb("s1", [T, 12, NT], F32)
        rw1 = sb("rw1", [P, D], F32)
        rb1 = sb("rb1", [P, 1], F32)
        b1 = sb("b1", [P, 3, E, FC], F32)
        b2 = sb("b2", [E, 3, D], F32)
        wg = sb("wg", [P, 3, E], F32)
        fw = sb("fw", [P, 4 * D], F32)
        fb = sb("fb", [P, 2], F32)
        sim = sb("sim", [P, E2], F32)
        sim2 = sb("sim2", [P, 4, E2], F32)
        sumh = sb("sumh", [T, 4, H], F32)

        ident = cst[:, C_ID:C_ID + P]
        perm = cst[:, C_PERM:C_PERM + P]

        qs = big1
        qv = big2[:, 0:2, :].rearrange("p a c -> p (a c)").bitcast(F16).rearrange("p (a c) -> p a c", a=4)
        qv_hi = big2[:, 2:4, :].rearrange("p a c -> p (a c)").bitcast(F16).rearrange("p (a c) -> p a c", a=4)

        ctx_in = [sem(f"ctx_in{i}") for i in range(3)]
        const_in = sem("const_in")
        kvw_in = sem("kvw_in")
        x_in = sem("x_in")
        xw_in = sem("xw_in")
        weights_in = [sem(f"weights_in{i}") for i in range(SLOTS)]
        gated_in = sem("gated_in")
        mask_in = [sem(f"mask_in{i}") for i in range(2)]
        consts_ready = sem("consts_ready")
        pool_ready = sem("pool_ready")
        aux_filled = sem("aux_filled")
        khi_done = sem("khi_done")
        klo_done = sem("klo_done")
        v_done = sem("v_done")
        smax_done = sem("smax_done")
        mx_done = sem("mx_done")
        mrow_done = sem("mrow_done")
        kq_in = [sem(f"kq_in{i}") for i in range(2)]
        qn_done = sem("qn_done")
        qb_done = sem("qb_done")
        maskq_done = sem("maskq_done")
        maskt_done = sem("maskt_done")
        scores_done = sem("scores_done")
        exp_done = sem("exp_done")
        pv_done = sem("pv_done")
        oc_half = sem("oc_half")
        oc_done = sem("oc_done")
        den_done = sem("den_done")
        rden_done = sem("rden_done")
        o_done = sem("o_done")
        out_done = sem("out_done")
        steps = {w: sem(f"{w}_step") for w in ("pe", "act", "dve", "pool")}
        pe_step, act_step, dve_step, pool_step = (steps[w] for w in ("pe", "act", "dve", "pool"))

        block = ctx.enter_context(nc.Block())

        def after(eng, who, phase, step):
            eng.wait_ge(steps[who], at[(who, phase, step)])

        def bank(item):
            return BANK_AUX + place[item] % 2

        def masks_before(g):
            return sum(1 for k in range(g + 1) if k // B in MASKED)

        def weights_count(mi, e):
            per = [len([k for k in range(E) if k % SLOTS == s]) for s in range(SLOTS)]
            return 16 * (mi * per[e % SLOTS] + e // SLOTS + 1)

        def prior(ph, kind):
            seq = program_order()
            return [p for p in seq[:seq.index(ph)] if p[0] == kind][-1]

        def turn_sources():
            seq, out_ = program_order(), []
            for i, p in enumerate(seq):
                if p[0] == "turn":
                    q = seq[i - 1]
                    out_.append(("z" if q[0] == "affine" else "y", q))
            return out_

        hbuf_T = keep
        qkv = big1[0:T, :, :].rearrange("p a c -> p (a c)")[:, 0:768].rearrange("p (t c) -> p t c", t=NT)
        N_FILLS = 7
        N_CONST = 15

        def ln_io(n):
            lns = [(x, y), (x, y), (y, z), (hbuf, z)] + [(x, y)] * 6
            return lns[n]

        @block.sync
        def _(sp):
            sp.dma_start(kvw[:, :, :], a["kvw"]).then_inc(kvw_in, 16)
            sp.dma_start(ctxT[:, 0, :], a["ctxT"][0]).then_inc(ctx_in[0], 16)
            sp.dma_start(xb[:, :, :], a["xb"]).then_inc(kvw_in, 16)
            sp.dma_start(cst[:, :], a["cst"][:, 0:C_W - HC]).then_inc(const_in, 16)
            sp.dma_start(x[:, :, :], a["x"].rearrange("(t p) d -> p t d", p=T)).then_inc(x_in, 16)
            sp.dma_start(ctxT[:, 1, :], a["ctxT"][1]).then_inc(ctx_in[1], 16)
            sp.dma_start(hot_f, a["cst"][:, C_W - HC:C_W]).then_inc(const_in, 16)
            sp.dma_start(ctxT[:, 2, :], a["ctxT"][2]).then_inc(ctx_in[2], 16)
            sp.dma_start(rows[:, :, :], a["rows"].rearrange("r d -> (r d)").partition_broadcast(T)
                         .rearrange("p (r d) -> p r d", d=D)).then_inc(const_in, 16)
            sp.dma_start(rw1[:, :], a["rw1"]).then_inc(const_in, 16)
            sp.dma_start(rb1[:, :], a["rb1"]).then_inc(const_in, 16)
            sp.dma_start(b1[:, :, :, :], a["b1"]).then_inc(const_in, 16)
            sp.dma_start(b2[:, :, :], a["b2"]).then_inc(const_in, 16)
            sp.dma_start(wg[:, :, :], a["wg"]).then_inc(const_in, 16)
            sp.dma_start(fw[:, :], a["fw"]).then_inc(const_in, 16)
            sp.dma_start(fb[:, :], a["fb"]).then_inc(const_in, 16)
            sp.dma_start(sim[:, :], a["sim"]).then_inc(const_in, 16)
            sp.dma_start(tri_u8[:, :], a["tri"]).then_inc(const_in, 16)
            sp.dma_start(maskT_u8[0:KK, :, :, :], a["maskT"]).then_inc(const_in, 16)
            sp.dma_start(triT_u8[0:KK, :, :], a["triT"]).then_inc(const_in, 16)
            sp.dma_start(padT_u8[0:KK, :, :], a["padT"]).then_inc(const_in, 16)

            def spread_keys(g):
                sp.wait_ge(klo_done, KS * (g + 1))
                if g >= 2:
                    sp.wait_ge(scores_done, KT * (g - 1))
                else:
                    sp.wait_ge(pool_ready, N_FILLS)
                for quad in range(QUADS):
                    r = slice(32 * quad, 32 * quad + 32)
                    for blk, part in enumerate((khi, klo, khi)):
                        sp.dma_start(kq[32 * blk:32 * blk + 32, g % 2, quad, 0:KV], part[r, g % 2, :])\
                            .then_inc(kq_in[g % 2], 16)

            def load_mask(g):
                if masks_before(g) > 2:
                    sp.wait_ge(maskq_done, masks_before(g) - 2)
                b = g % B
                src = a["mask"][:, b, :] if g // B == 1 else a["pad"][b, :].partition_broadcast(S)
                sp.dma_start(mask_u8[:, g % 2, :], src).then_inc(mask_in[g % 2], 16)

            spread_keys(0)
            spread_keys(1)
            for l in range(L):
                if l:
                    after(sp, "pe", ("out", l - 1), "projected")
                sp.dma_start(xw[:, :], a["xw"][l]).then_inc(xw_in, 16)
                mi = {0: 0, 1: 1, 3: 2}.get(l)
                if l:
                    former = ("gated", 0) if l == 3 else ("moe", l - 1)
                    after(sp, "pe", former, f"f{FOURS - 1}" if l == 3 else "b2")
                if mi is None:
                    sp.dma_start(weights[:, 0:3072], a["qkv2"]).then_inc(gated_in, 16)
                    sp.dma_start(weights[0:HD2, 3072:5120], a["o2"]).then_inc(gated_in, 16)
                else:
                    for e in range(SLOTS):
                        sp.dma_start(weights[:, e * 1024:(e + 1) * 1024], a["moe"][mi * E + e])\
                            .then_inc(weights_in[e], 16)
                for g in range(l * B, (l + 1) * B):
                    if g + 3 < G:
                        sp.wait_ge(v_done, 3 * (g + 1))
                        sp.dma_start(ctxT[:, g % 3, :], a["ctxT"][(g + 3) % B]).then_inc(ctx_in[g % 3], 16)
                    if g + 3 < G and (g + 3) // B in MASKED:
                        load_mask(g + 3)
                    if g + 2 < G:
                        spread_keys(g + 2)
                if mi is not None:
                    for e in range(SLOTS, E):
                        after(sp, "pe", ("moe", mi), f"y{e - SLOTS}")
                        k = e % SLOTS
                        sp.dma_start(weights[:, k * 1024:(k + 1) * 1024], a["moe"][mi * E + e])\
                            .then_inc(weights_in[k], 16)
            after(sp, "dve", ("moe", 2), "b2")
            sp.dma_start(out.rearrange("(t p) d -> p t d", p=T), x[:, :, :]).then_inc(out_done, 16)
            sp.wait_ge(out_done, 16)

        @block.gpsimd
        def _(pool):
            fills = [(mhalf[:, :], -0.5), (kq[:, :, :, KV:KPAD], 0.0), (kq[96:128, :, :, 0:KV], 0.0),
                     (kq[96:97, :, :, 0:KV], 1.0), (v_aug[:, :, :, :, :], 1.0), (qb[96:128, :, :, :, :], 0.0),
                     (ones_f[:, :], 1.0)]
            for n, (dst, value) in enumerate(fills):
                if n:
                    pool.wait_ge(pool_ready, n)
                nc.gpsimd.memset(dst, value).then_inc(pool_ready, 1)

            def rsqrt(ph):
                after(pool, "dve", ph, "var")
                pool.wait_ge(pool_ready, N_FILLS)
                nc.gpsimd.tensor_tensor(rstd[:, :], ve[:, :], mhalf[0:T, 0:NT], ALU.pow).then_inc(pool_step, 1)

            for ph in program_order():
                kind, n = ph
                if kind == "ln":
                    rsqrt(ph)
                elif kind == "gated":
                    after(pool, "dve", ph, "sim2_max")
                    nc.gpsimd.tensor_tensor(sim2[:, 2, :], sim2[:, 1, :], mhalf[:, 0:E2], ALU.pow).then_inc(pool_step, 1)
                    after(pool, "dve", ph, "y2_max")
                    nc.gpsimd.tensor_tensor(s1[:, 1, :], s1[:, 0, :], mhalf[0:T, 0:NT], ALU.pow).then_inc(pool_step, 1)
                elif kind == "q":
                    for b in range(B):
                        g = n * B + b
                        if b == 0:
                            pool.wait_ge(consts_ready, 1)
                            after(pool, "dve", ph, "lo")
                            after(pool, "act", ph, "hi")
                        if g >= 2:
                            pool.wait_ge(smax_done, CH * KS * (g - 1))
                        src = qn16[:, b * S:(b + 1) * S].unsqueeze(1).broadcast_to([P, H, S])
                        nc.gpsimd.tensor_tensor(qn[:, g % 2, :, :], src,
                                                bm16[:, :].unsqueeze(2).broadcast_to([P, H, S]), ALU.mult)\
                            .then_inc(qn_done, 1)
                        if g >= 2:
                            pool.wait_ge(scores_done, KT * (g - 1))
                        src = qv[0:96, :, b * S:(b + 1) * S].unsqueeze(2).broadcast_to([96, QUADS, HQ, S])
                        sel = m4[0:96, :].unsqueeze(1).unsqueeze(3).broadcast_to([96, QUADS, HQ, S])
                        nc.gpsimd.tensor_tensor(qb[0:96, g % 2, :, :, :], src, sel, ALU.mult).then_inc(qb_done, 1)

        @block.tensor
        def _(pe):
            mm = nc.tensor.matmul

            def gated_pe(pe, ph):
                mm = nc.tensor.matmul
                after(pe, "dve", ph, "sim2")
                after(pe, "act", prior(ph, "turn"), "copied")
                mm(ps[:, 1, 0:E2], ones_f[:, :], sim2[:, 0, :], start=True, stop=True).then_inc(pe_step, 1)
                after(pe, "dve", ph, "sim_unit")
                for t in range(NT):
                    last = mm(ps[0:T, 2, t * E2:(t + 1) * E2], yT[:, t * T:(t + 1) * T], sim2[:, 3, :], start=True, stop=True)
                last.then_inc(pe_step, 1)
                pe.wait_ge(gated_in, 32)
                for i in range(PAIRS):
                    t, p = divmod(i, E2 // 2)
                    if i >= 2:
                        after(pe, "dve", ph, f"p{i - 2}b")
                    mm(ps[0:T, 4 + i % 2, 0:384], yT[:, t * T:(t + 1) * T], weights[:, p * 384:(p + 1) * 384],
                       start=True, stop=True).then_inc(pe_step, 1)
                after(pe, "dve", ph, f"p{PAIRS - 1}b")
                for t in range(NT):
                    nc.tensor.transpose(ps[0:HD2, 0, t * T:(t + 1) * T], qkv[:, t, 0:64], ident[0:T, 0:T])
                    last = nc.tensor.transpose(ps[0:HD2, 1, t * T:(t + 1) * T], qkv[:, t, 64:128], ident[0:T, 0:T])
                last.then_inc(pe_step, 1)
                after(pe, "act", ph, "qk_copied")
                for t in range(NT):
                    mm(ps[0:T, 2, 0:T], big2[0:HD2, 0, t * T:(t + 1) * T], big2[0:HD2, 1, t * T:(t + 1) * T],
                       start=True, stop=True).then_inc(pe_step, 1)
                    after(pe, "act", ph, f"exp{t}")
                    nc.tensor.transpose(ps[0:T, 3, 0:T], big2[0:T, 2, 0:T], ident[0:T, 0:T]).then_inc(pe_step, 1)
                    after(pe, "act", ph, f"pt{t}")
                    mm(ps[0:T, 4, 0:HD2], big2[0:T, 2, T:2 * T], qkv[:, t, 128:192], start=True, stop=True).then_inc(pe_step, 1)
                    after(pe, "dve", ph, f"o{t}")
                for t in range(NT):
                    last = nc.tensor.transpose(ps[0:HD2, 0, t * T:(t + 1) * T], hbuf[:, t, 0:HD2], ident[0:T, 0:T])
                last.then_inc(pe_step, 1)
                after(pe, "act", ph, "a_copied")
                for i in range(FOURS):
                    t, p = divmod(i, E2 // 4)
                    if i >= 2:
                        after(pe, "dve", ph, f"f{i - 2}_3")
                    mm(ps[0:T, 4 + i % 2, :], big2[0:HD2, 0, t * T:(t + 1) * T], weights[0:HD2, 3072 + p * 512:3072 + (p + 1) * 512],
                       start=True, stop=True).then_inc(pe_step, 1)

            def wait_evacuated(item):
                kind, g, i = item
                if kind == "K":
                    pe.wait_ge(khi_done, KS * g + i + 1)
                    pe.wait_ge(klo_done, KS * g + i + 1)
                elif kind == "V":
                    pe.wait_ge(v_done, 3 * g + i + 1)
                elif kind == "S":
                    pe.wait_ge(smax_done, CH * KS * g + i + 1)
                else:
                    pe.wait_ge(mrow_done, 2 * g + i + 1)

            def side(item):
                kind, g, i = item
                l, bk = g // B, bank(item)
                if place[item] >= 2:
                    wait_evacuated(items[place[item] - 2])
                if kind == "K":
                    if i == 0:
                        pe.wait_ge(ctx_in[g % 3], 16 * (g // 3 + 1))
                    last = mm(ps[:, bk, 0:KP], kvw[:, l, 0:D], ctxT[:, g % 3, i * KP:(i + 1) * KP], start=True, stop=True)
                elif kind == "V":
                    for j in range(4):
                        kt = 4 * i + j
                        last = mm(ps[0:KK, bk, j * D:(j + 1) * D], ctxT[:, g % 3, kt * KK:(kt + 1) * KK],
                                  kvw[:, l, D:2 * D], start=True, stop=True)
                elif kind == "S":
                    c, k = divmod(i, KS)
                    if i == 0:
                        pe.wait_ge(qn_done, g + 1)
                        if l in MASKED:
                            pe.wait_ge(maskq_done, masks_before(g))
                    cols = slice(c * P, (c + 1) * P)
                    q2 = qn[:, g % 2, :, :].rearrange("p h s -> p (h s)")
                    masked = l in MASKED
                    last = mm(ps[:, bk, 0:KP], q2[:, cols], khi[:, g % 2, k * KP:(k + 1) * KP], start=True, stop=not masked)
                    if masked:
                        last = mm(ps[:, bk, 0:KP], hot[:, cols], mask_q[:, g % 2, k * KP:(k + 1) * KP], start=False, stop=True)
                else:
                    if i == 0:
                        pe.wait_ge(mx_done, g + 1)
                    for j, c in enumerate(range(4 * i, min(4 * i + 4, CH))):
                        last = mm(ps[0:1, bk, j * P:(j + 1) * P], mx[:, g % 2, c:c + 1], ident, start=True, stop=True)
                last.then_inc(aux_filled, 1)

            def scores(g, kt):
                n = g * KT + kt
                if kt == 0:
                    pe.wait_ge(kq_in[g % 2], 16 * 12 * (g // 2 + 1))
                    pe.wait_ge(qb_done, g + 1)
                    pe.wait_ge(mrow_done, 2 * (g + 1))
                if n >= 2:
                    pe.wait_ge(exp_done, n - 1)
                masked = g // B in MASKED
                for quad in range(QUADS):
                    dst = ps[:, 2 * (kt % 2) + quad // 2, (quad % 2) * 224:(quad % 2 + 1) * 224]
                    last = mm(dst, kq[:, g % 2, quad, kt * KK:kt * KK + P],
                              qb[:, g % 2, quad, :, :].rearrange("p h s -> p (h s)"), start=True, stop=not masked)
                    if masked:
                        mt = mask_t[:, g % B, kt, :].unsqueeze(1).broadcast_to([P, HQ, S])
                        last = mm(dst.rearrange("p (h s) -> p h s", s=S), id_mask[:, :], mt, start=False, stop=True)
                last.then_inc(scores_done, 1)

            def values(g, kt):
                n = g * KT + kt
                if kt == 0:
                    pe.wait_ge(v_done, 3 * (g + 1))
                    if g >= 2:
                        pe.wait_ge(o_done, g - 1)
                pe.wait_ge(exp_done, n + 1)
                for t8 in range(8):
                    r, j = divmod(t8, 4)
                    last = mm(ps[32 * j:32 * j + 32, BANK_PV + g % 2, r * T:(r + 1) * T],
                              v_aug[0:KK, g % 2, kt, t8, :], probs[0:KK, kt % 2, t8 * T:(t8 + 1) * T],
                              start=(kt == 0 and r == 0), stop=(kt == KT - 1), skip_group_check=True)
                last.then_inc(pv_done, 1)

            def denominators(g):
                pe.wait_ge(oc_done, g + 1)
                mm(ps[:, BANK_PV + g % 2, 256:256 + 2 * S], perm, oc[:, :, :].rearrange("p r s -> p (r s)"),
                   start=True, stop=True).then_inc(den_done, 1)

            def attention(l):
                for g in range(l * B, (l + 1) * B):
                    last_of_layer = g % B == B - 1
                    if g % B == 0:
                        for item in head_items(g):
                            side(item)
                        scores(g, 0)
                    for kt, slot in enumerate(aux_slots(g)):
                        for item in slot[:1]:
                            side(item)
                        if kt + 1 < KT:
                            scores(g, kt + 1)
                        for item in slot[1:]:
                            side(item)
                        if kt == KT - 1 and not last_of_layer:
                            scores(g + 1, 0)
                        values(g, kt)
                        if kt == 2 and g % B:
                            denominators(g - 1)
                denominators((l + 1) * B - 1)

            pe.wait_ge(kvw_in, 32)
            for item in FIRST_ITEMS:
                side(item)
            pe.wait_ge(const_in, 16 * N_CONST)
            pe.wait_ge(consts_ready, 1)
            pe.wait_ge(pool_ready, N_FILLS)
            src_of_turn = turn_sources()
            for ph in program_order():
                kind, n = ph
                if kind == "turn":
                    src, before = src_of_turn[n]
                    after(pe, "dve", before, "add" if before[0] == "affine" else "norm")
                    for t in range(NT):
                        last = nc.tensor.transpose(ps[:, 0, t * T:(t + 1) * T], (y if src == "y" else z)[:, t, :], ident[0:T, 0:T])
                    last.then_inc(pe_step, 1)
                elif kind == "count":
                    pe.wait_ge(consts_ready, 1)
                    pe.wait_ge(maskt_done, MASKED.index(n) + 1)
                    after(pe, "dve", ("moe", n - 1), "b2")
                    for kt in range(KT):
                        last = mm(ps[:, 5, 0:TOK].rearrange("p (b s) -> p b s", s=S), ones_b[0:KK, :], mask_t[0:KK, :, kt, :], start=kt == 0, stop=kt == KT - 1)
                    last.then_inc(pe_step, 1)
                elif kind == "q":
                    pe.wait_ge(xw_in, 16 * (n + 1))
                    after(pe, "act", prior(ph, "turn"), "copied")
                    for quad in range(QUADS):
                        mm(ps[:, quad, 0:TOK], xw[:, D * (1 + quad):D * (2 + quad)], yT[:, :], start=True, stop=True)
                    mm(ps[:, 4, 0:TOK], xw[:, 0:D], yT[:, :], start=True, stop=True).then_inc(pe_step, 1)
                    attention(n)
                elif kind == "out":
                    after(pe, "dve", ph, "biased")
                    for t in range(NT):
                        for r in range(2):
                            last = mm(ps[0:T, 3, t * D:(t + 1) * D], o_all[:, r, t * T:(t + 1) * T],
                                      xw[:, D * (5 + r):D * (6 + r)], start=r == 0, stop=r == 1)
                    last.then_inc(pe_step, 1)
                elif kind == "moe":
                    after(pe, "act", prior(ph, "turn"), "copied")
                    rT = yT
                    if n == 2:
                        mm(ps[:, 1, 0:TOK], rw1[:, :], yT[:, :], start=True, stop=True).then_inc(pe_step, 1)
                        after(pe, "act", ph, "r1")
                        rT = hbuf_T
                    for t in range(NT):
                        last = mm(ps[0:T, 5, t * E:(t + 1) * E], rT[:, t * T:(t + 1) * T], wg[:, n, :], start=True, stop=True)
                    last.then_inc(pe_step, 1)

                    def hidden(e):
                        pe.wait_ge(weights_in[e % SLOTS], weights_count(n, e))
                        for c in range(FC):
                            if e:
                                after(pe, "act", ph, f"h{e - 1}_{c}")
                            w = (e % SLOTS) * 1024 + c * P
                            last = mm(ps[:, c, 0:TOK], weights[:, w:w + P], yT[:, :], start=True, stop=True)
                        last.then_inc(pe_step, 1)

                    def down(e):
                        after(pe, "act", ph, f"h{e}_{FC - 1}")
                        if e >= 2:
                            after(pe, "dve", ph, f"acc{e - 2}")
                        else:
                            after(pe, "dve", ph, "logits")
                        hT = (big0, big1)[e % 2]
                        for t in range(NT):
                            for c in range(FC):
                                w = (e % SLOTS) * 1024 + F + c * D
                                last = mm(ps[0:T, 4 + e % 2, t * D:(t + 1) * D], hT[:, c, t * T:(t + 1) * T],
                                          weights[:, w:w + D], start=c == 0, stop=c == FC - 1)
                        last.then_inc(pe_step, 1)

                    hidden(0)
                    for e in range(E):
                        if e + 1 < E:
                            hidden(e + 1)
                        down(e)
                    after(pe, "dve", ph, "W")
                    after(pe, "act", ph, f"h{E - 1}_{FC - 1}")
                    for t in range(NT):
                        last = nc.tensor.transpose(ps[0:E, 0, t * T:(t + 1) * T], sm[:, 8, t * E:(t + 1) * E], ident[0:T, 0:T])
                    last.then_inc(pe_step, 1)
                    after(pe, "act", ph, "w_copied")
                    after(pe, "dve", ph, f"acc{E - 2}")
                    for t in range(NT):
                        last = mm(ps[0:T, 4, t * D:(t + 1) * D], keep[0:E, t * T:(t + 1) * T], b2[:, n, :], start=True, stop=True)
                    last.then_inc(pe_step, 1)
                elif kind == "self":
                    after(pe, "act", prior(ph, "turn"), "copied")
                    mm(ps[:, 4, 0:TOK], fw[:, 0:D], yT[:, :], start=True, stop=True)
                    mm(ps[:, 5, 0:TOK], fw[:, D:2 * D], yT[:, :], start=True, stop=True).then_inc(pe_step, 1)
                    for t in range(NT):
                        last = mm(ps[0:T, 3, t * D:(t + 1) * D], yT[:, t * T:(t + 1) * T], fw[:, 2 * D:3 * D], start=True, stop=True)
                    last.then_inc(pe_step, 1)
                    after(pe, "dve", ph, "v")
                    for t in range(NT):
                        after(pe, "dve", ph, f"kb{t}")
                        if t:
                            after(pe, "act", ph, f"pt{t - 1}")
                        for c in range(4):
                            mm(ps[0:T, c, 0:448], qnf[:, t * T:(t + 1) * T], big0[:, c, :], start=True, stop=False)
                            last = mm(ps[0:T, c, 0:448].rearrange("p (h k) -> p h k", k=T), id_b[0:T, 0:T], blk_b[0:T, :].unsqueeze(1).broadcast_to([T, 4, T]),
                                      start=False, stop=True)
                        last.then_inc(pe_step, 1)
                        after(pe, "act", ph, f"exp{t}")
                        for h in range(H):
                            last = nc.tensor.transpose(ps[0:T, h // 4, (h % 4) * T:(h % 4 + 1) * T],
                                                       big1[0:T, h // 4, (h % 4) * T:(h % 4 + 1) * T], ident[0:T, 0:T])
                        last.then_inc(pe_step, 1)
                        after(pe, "act", ph, f"pt{t}")
                        if t >= 2:
                            after(pe, "dve", ph, f"o{t - 2}")
                        for h in range(H):
                            last = mm(ps[0:T, 4 + t % 2, h * DH:(h + 1) * DH], big2[0:T, h // 4, (h % 4) * T:(h % 4 + 1) * T],
                                      z[:, t, h * DH:(h + 1) * DH], start=True, stop=True)
                        last.then_inc(pe_step, 1)
                    after(pe, "dve", ph, f"o{NT - 1}")
                    for t in range(NT):
                        last = nc.tensor.transpose(ps[:, 0, t * T:(t + 1) * T], hbuf[:, t, :], ident[0:T, 0:T])
                    last.then_inc(pe_step, 1)
                    after(pe, "act", ph, "o_copied")
                    for t in range(NT):
                        last = mm(ps[0:T, 3, t * D:(t + 1) * D], yT[:, t * T:(t + 1) * T], fw[:, 3 * D:4 * D], start=True, stop=True)
                    last.then_inc(pe_step, 1)
                elif kind == "gated":
                    gated_pe(pe, ph)

        @block.scalar
        def _(act):
            A = nc.scalar.activation

            def side(item):
                kind, g, i = item
                bk = bank(item)
                if kind == "S":
                    return
                act.wait_ge(aux_filled, place[item] + 1)
                if kind == "K":
                    if g >= 2 and i == 0:
                        act.wait_ge(kq_in[g % 2], 16 * 12 * (g // 2))
                    A(khi[:, g % 2, i * KP:(i + 1) * KP], ps[:, bk, 0:KP], ACT.Identity,
                      bias=xb[:, g // B, 0:1]).then_inc(khi_done, 1)
                elif kind == "V":
                    if g >= 2 and i == 0:
                        act.wait_ge(pv_done, KT * (g - 1))
                    dst = v_aug[0:KK, g % 2, 4 * i:4 * i + 4, :, 0:16].rearrange("p k t c -> p (k t) c")
                    A(dst, ps[0:KK, bk, :].rearrange("p (k c) -> p k c", c=16), ACT.Copy).then_inc(v_done, 1)
                else:
                    n = 512 if i == 0 else HC - 512
                    row = qb[96:97, g % 2, :, :, :].rearrange("p a h s -> p (a h s)")
                    if i == 0 and g >= 2:
                        act.wait_ge(scores_done, KT * (g - 1))
                    A(row[:, i * 512:i * 512 + n], ps[0:1, bk, 0:n], ACT.Copy, scale=-1.0).then_inc(mrow_done, 1)

            def attention(l):
                for g in range(l * B, (l + 1) * B):
                    if g % B == 0:
                        for item in head_items(g):
                            side(item)
                    for kt, slot in enumerate(aux_slots(g)):
                        n = g * KT + kt
                        act.wait_ge(scores_done, n + 1)
                        if n >= 2:
                            act.wait_ge(pv_done, n - 1)
                        A(probs[0:KK, kt % 2, :].rearrange("p (a c) -> p a c", a=2),
                          ps[0:KK, 2 * (kt % 2):2 * (kt % 2) + 2, 0:448], ACT.Exp).then_inc(exp_done, 1)
                        for item in slot:
                            side(item)

            act.wait_ge(kvw_in, 32)
            act.wait_ge(pool_ready, N_FILLS)
            for item in FIRST_ITEMS:
                side(item)
            for ph in program_order():
                kind, n = ph
                if kind == "turn":
                    after(act, "pe", ph, "turned")
                    A(yT[:, :], ps[:, 0, 0:TOK], ACT.Copy).then_inc(act_step, 1)
                elif kind == "q":
                    after(act, "dve", ph, "kept" if n == 2 else "scaled")
                    A(qv[0:64, :, :], qs[0:64, :, :], ACT.Copy).then_inc(act_step, 1)
                    A(qv_hi[64:96, :, :], qs[64:96, :, :], ACT.Copy).then_inc(act_step, 1)
                    attention(n)
                elif kind == "moe":
                    func = (ACT.Gelu_apprx_tanh, ACT.Relu, ACT.Silu)[n]
                    if n == 2:
                        act.wait_ge(const_in, 16 * N_CONST)
                        after(act, "pe", ph, "r1")
                        A(hbuf_T[:, :], ps[:, 1, 0:TOK], ACT.Silu, bias=rb1[:, 0:1]).then_inc(act_step, 1)
                        after(act, "dve", ph, "gap")
                        A(s1[:, 8, :], s1[:, 7, :], ACT.Exp).then_inc(act_step, 1)
                    else:
                        after(act, "dve", ph, "shift")
                        A(sm[:, 2, 0:32], sm[:, 1, 0:32], ACT.Exp).then_inc(act_step, 1)
                    act.wait_ge(const_in, 16 * N_CONST)
                    for e in range(E):
                        after(act, "pe", ph, f"h{e}")
                        if e >= 2:
                            after(act, "pe", ph, f"y{e - 2}")
                        for c in range(FC):
                            A((big0, big1)[e % 2][:, c, :], ps[:, c, 0:TOK], func, bias=b1[:, n, e, c:c + 1])\
                                .then_inc(act_step, 1)
                    after(act, "pe", ph, "w_turned")
                    A(keep[0:E, :], ps[0:E, 0, 0:TOK], ACT.Copy).then_inc(act_step, 1)
                elif kind == "self":
                    for t in range(NT):
                        after(act, "dve", ph, f"shift{t}")
                        A(big1[0:T, :, :], big1[0:T, :, :], ACT.Exp).then_inc(act_step, 1)
                        after(act, "pe", ph, f"t{t}")
                        if t:
                            after(act, "pe", ph, f"o{t - 1}")
                        A(big2[0:T, :, :], ps[0:T, 0:4, 0:448], ACT.Copy).then_inc(act_step, 1)
                    after(act, "pe", ph, "o_turned")
                    A(yT[:, :], ps[:, 0, 0:TOK], ACT.Copy).then_inc(act_step, 1)
                elif kind == "gated":
                    A(sm[:, 0, 0:E2], rows[:, R_GATE, 0:E2], ACT.Exp, scale=-1.0).then_inc(act_step, 1)
                    after(act, "dve", ph, "shift")
                    A(sm[:, 9, :], sm[:, 8, :], ACT.Exp).then_inc(act_step, 1)
                    after(act, "pe", ph, "qk_turned")
                    A(big2[0:HD2, 0:2, :], ps[0:HD2, 0:2, 0:TOK], ACT.Copy).then_inc(act_step, 1)
                    for t in range(NT):
                        after(act, "dve", ph, f"shift{t}")
                        A(big2[0:T, 2, 0:T], z[:, t, 0:T], ACT.Exp).then_inc(act_step, 1)
                        after(act, "pe", ph, f"t{t}")
                        A(big2[0:T, 2, T:2 * T], ps[0:T, 3, 0:T], ACT.Copy).then_inc(act_step, 1)
                    after(act, "pe", ph, "a_turned")
                    A(big2[0:HD2, 0, :], ps[0:HD2, 0, 0:TOK], ACT.Copy).then_inc(act_step, 1)

        @block.vector
        def _(dve):
            V = nc.vector
            TT, TS, STT = V.tensor_tensor, V.tensor_scalar, V.scalar_tensor_tensor

            def self_dve(dve, ph):
                V = nc.vector
                TT, TS, STT = V.tensor_tensor, V.tensor_scalar, V.scalar_tensor_tensor
                after(dve, "pe", ph, "qk")
                TS(qnf[:, :], ps[:, 4, 0:TOK], fb[:, 0:1], float(DH) ** -0.5, ALU.add, ALU.mult).then_inc(dve_step, 1)
                TS(keep[:, :], ps[:, 5, 0:TOK], fb[:, 1:2], None, ALU.add).then_inc(dve_step, 1)
                after(dve, "pe", ph, "v")
                TT(z[:, :, :], ps[0:T, 3, :].rearrange("p (t d) -> p t d", d=D),
                   rows[:, R_FBV, :].unsqueeze(1).broadcast_to([T, NT, D]), ALU.add).then_inc(dve_step, 1)
                after(dve, "dve", ph, "v")
                for t in range(NT):
                    if t:
                        after(dve, "pe", ph, f"s{t - 1}")
                    TT(big0.rearrange("p a c -> p (a c)").rearrange("p (h k) -> p h k", h=H),
                       keep[:, t * T:(t + 1) * T].unsqueeze(1).broadcast_to([P, H, T]),
                       cst[:, C_BM:C_BM + H].unsqueeze(2).broadcast_to([P, H, T]), ALU.mult).then_inc(dve_step, 1)
                    after(dve, "pe", ph, f"s{t}")
                    s4 = ps[0:T, 0:4, 0:448].rearrange("p a (h k) -> p a h k", k=T)
                    V.reduce_max(sumh[:, 0, :].rearrange("p (a h) -> p a h", a=4), s4, AX.X).then_inc(dve_step, 1)
                    after(dve, "dve", ph, f"max{t}")
                    if t:
                        after(dve, "pe", ph, f"t{t - 1}")
                    for c in range(4):
                        last = TT(big1[0:T, c, :].rearrange("p (h k) -> p h k", k=T), s4[:, c, :, :],
                                  sumh[:, 0, 4 * c:4 * c + 4].unsqueeze(2).broadcast_to([T, 4, T]), ALU.subtract)
                    last.then_inc(dve_step, 1)
                    after(dve, "act", ph, f"exp{t}")
                    V.reduce_sum(sumh[:, 1, :], big1[0:T, :, :].rearrange("p a c -> p (a c)").rearrange("p (h k) -> p h k", k=T), AX.X)\
                        .then_inc(dve_step, 1)
                    after(dve, "dve", ph, f"sum{t}")
                    V.reciprocal(sumh[:, 2, :], sumh[:, 1, :]).then_inc(dve_step, 1)
                    after(dve, "dve", ph, f"recip{t}")
                    after(dve, "pe", ph, f"o{t}")
                    TT(hbuf[:, t, :].rearrange("p (h d) -> p h d", d=DH), ps[0:T, 4 + t % 2, 0:D].rearrange("p (h d) -> p h d", d=DH),
                       sumh[:, 2, :].unsqueeze(2).broadcast_to([T, H, DH]), ALU.mult).then_inc(dve_step, 1)
                TT(y[:, :, :], y[:, :, :], rows[:, R_FBO, :].unsqueeze(1).broadcast_to([T, NT, D]), ALU.add).then_inc(dve_step, 1)
                after(dve, "dve", ph, "hb")
                after(dve, "pe", ph, "proj")
                TT(hbuf[:, :, :], ps[0:T, 3, :].rearrange("p (t d) -> p t d", d=D), y[:, :, :], ALU.add).then_inc(dve_step, 1)
                after(dve, "dve", ph, "h")

            def gated_dve(dve, ph, top2):
                V = nc.vector
                TT, TS, STT = V.tensor_tensor, V.tensor_scalar, V.scalar_tensor_tensor

                def did(step):
                    after(dve, "dve", ph, step)

                def v(i):
                    return sm[:, i, :].rearrange("p (t e) -> p t e", e=E2)

                def one(i):
                    return s1[:, i, :].unsqueeze(2).broadcast_to([T, NT, E2])

                TT(sim2[:, 0, :], sim[:, :], sim[:, :], ALU.mult).then_inc(dve_step, 1)
                TT(z[:, :, :], y[:, :, :], y[:, :, :], ALU.mult).then_inc(dve_step, 1)
                did("y2")
                V.reduce_sum(s1[:, 10, :], z[:, :, :], AX.X).then_inc(dve_step, 1)
                did("y2_sum")
                TS(s1[:, 0, :], s1[:, 10, :], 1e-24, None, ALU.max).then_inc(dve_step, 1)
                after(dve, "pe", ph, "sim2")
                TS(sim2[:, 1, :], ps[:, 1, 0:E2], 1e-24, None, ALU.max).then_inc(dve_step, 1)
                after(dve, "pool", ph, "sim_norm")
                TT(sim2[:, 3, :], sim[:, :], sim2[:, 2, :], ALU.mult).then_inc(dve_step, 1)
                after(dve, "act", ph, "gate_exp")
                TS(sm[:, 1, 0:E2], sm[:, 0, 0:E2], 1.0, None, ALU.add).then_inc(dve_step, 1)
                did("gate1")
                V.reciprocal(sm[:, 2, 0:E2], sm[:, 1, 0:E2]).then_inc(dve_step, 1)
                after(dve, "pe", ph, "logits")
                after(dve, "pool", ph, "y_norm")
                did("gate")
                TT(v(0), ps[0:T, 2, 0:NT * E2].rearrange("p (t e) -> p t e", e=E2), one(1), ALU.mult).then_inc(dve_step, 1)
                did("cos")
                TT(v(1), v(0), sm[:, 2, 0:E2].unsqueeze(1).broadcast_to([T, NT, E2]), ALU.subtract).then_inc(dve_step, 1)
                did("logits")
                TS(v(10), v(1), 0.0, None, ALU.is_gt).then_inc(dve_step, 1)
                did("pos")
                V.reduce_max(s1[:, 6, :], v(10), AX.X).then_inc(dve_step, 1)
                TS(v(11), v(1), 0.0, None, ALU.max).then_inc(dve_step, 1)
                did("gated")
                V.reduce_max(s1[:, 7, :], v(11), AX.X).then_inc(dve_step, 1)
                top2(ph, v(1), E2)
                TT(v(12), v(4), v(7), ALU.add).then_inc(dve_step, 1)
                TS(s1[:, 8, :], s1[:, 6, :], -1.0, 1.0, ALU.mult, ALU.add).then_inc(dve_step, 1)
                did("none")
                TT(v(13), v(12), one(8), ALU.mult).then_inc(dve_step, 1)
                did("fallback")
                TT(v(14), v(13), v(10), ALU.add).then_inc(dve_step, 1)
                TT(v(8), v(11), one(7), ALU.subtract).then_inc(dve_step, 1)
                after(dve, "act", ph, "exp")
                TT(v(12), v(9), v(14), ALU.mult).then_inc(dve_step, 1)
                did("em")
                V.reduce_sum(s1[:, 9, :], v(12), AX.X).then_inc(dve_step, 1)
                did("sum")
                V.reciprocal(s1[:, 10, :], s1[:, 9, :]).then_inc(dve_step, 1)
                did("recip")
                TT(v(15), v(12), one(10), ALU.mult).then_inc(dve_step, 1)
                did("rw")
                for i in range(PAIRS):
                    t, p = divmod(i, E2 // 2)
                    w = t * E2 + 2 * p
                    after(dve, "pe", ph, f"p{i}")
                    if p == 0:
                        TS(qkv[:, t, :], ps[0:T, 4 + i % 2, 0:192], sm[:, 15, w:w + 1], None, ALU.mult).then_inc(dve_step, 1)
                    else:
                        did(f"p{i - 1}b")
                        STT(qkv[:, t, :], ps[0:T, 4 + i % 2, 0:192], sm[:, 15, w:w + 1], qkv[:, t, :], ALU.mult, ALU.add)\
                            .then_inc(dve_step, 1)
                    did(f"p{i}a")
                    STT(qkv[:, t, :], ps[0:T, 4 + i % 2, 192:384], sm[:, 15, w + 1:w + 2], qkv[:, t, :], ALU.mult, ALU.add)\
                        .then_inc(dve_step, 1)
                for t in range(NT):
                    after(dve, "pe", ph, f"s{t}")
                    STT(z[:, t, 0:T], ps[0:T, 2, 0:T], float(HD2) ** -0.5, cst[0:T, C_CAU:C_CAU + T], ALU.mult, ALU.add).then_inc(dve_step, 1)
                    did(f"mask{t}")
                    V.reduce_max(s1[:, 2, t:t + 1], z[:, t, 0:T], AX.X).then_inc(dve_step, 1)
                    did(f"max{t}")
                    TS(z[:, t, 0:T], z[:, t, 0:T], s1[:, 2, t:t + 1], None, ALU.subtract).then_inc(dve_step, 1)
                    after(dve, "act", ph, f"exp{t}")
                    V.reduce_sum(s1[:, 3, t:t + 1], big2[0:T, 2, 0:T], AX.X).then_inc(dve_step, 1)
                    did(f"sum{t}")
                    V.reciprocal(s1[:, 4, t:t + 1], s1[:, 3, t:t + 1]).then_inc(dve_step, 1)
                    did(f"recip{t}")
                    after(dve, "pe", ph, f"o{t}")
                    TS(hbuf[:, t, 0:HD2], ps[0:T, 4, 0:HD2], s1[:, 4, t:t + 1], None, ALU.mult).then_inc(dve_step, 1)
                for i in range(FOURS):
                    t, p = divmod(i, E2 // 4)
                    after(dve, "pe", ph, f"f{i}")
                    for k in range(4):
                        w = t * E2 + 4 * p + k
                        STT(x[:, t, :], ps[0:T, 4 + i % 2, k * D:(k + 1) * D], sm[:, 15, w:w + 1], x[:, t, :],
                            ALU.mult, ALU.add).then_inc(dve_step, 1)
                        did(f"f{i}_{k}")

            def side(item):
                kind, g, i = item
                bk = bank(item)
                if kind == "K":
                    dve.wait_ge(khi_done, KS * g + i + 1)
                    if g >= 2 and i == 0:
                        dve.wait_ge(kq_in[g % 2], 16 * 12 * (g // 2))
                    STT(klo[:, g % 2, i * KP:(i + 1) * KP], ps[:, bk, 0:KP], xb[:, g // B, 0:1],
                        khi[:, g % 2, i * KP:(i + 1) * KP], ALU.add, ALU.subtract).then_inc(klo_done, 1)
                elif kind == "S":
                    c, k = divmod(i, KS)
                    dve.wait_ge(aux_filled, place[item] + 1)
                    V.reduce_max(mx_part[:, g % 2, c, k:k + 1], ps[:, bk, 0:KP], AX.X).then_inc(smax_done, 1)
                    if i == CH * KS - 1:
                        dve.wait_ge(smax_done, CH * KS * (g + 1))
                        V.reduce_max(mx[:, g % 2, 0:CH], mx_part[:, g % 2, :, :], AX.X).then_inc(mx_done, 1)

            def mask_by_query(g):
                dve.wait_ge(mask_in[g % 2], 16 * ((masks_before(g) + 1) // 2))
                if g >= 2:
                    dve.wait_ge(smax_done, CH * KS * (g - 1))
                if g // B == 1:
                    V.tensor_copy(mask_q[0:S, g % 2, :], mask_u8[:, g % 2, :]).then_inc(maskq_done, 1)
                else:
                    STT(mask_q[0:S, g % 2, :], tri_u8[:, :], 0.5, mask_u8[:, g % 2, :], ALU.is_lt, ALU.is_ge)\
                        .then_inc(maskq_done, 1)

            def masks_by_key(l):
                for b in range(B):
                    if l == 1:
                        last = V.tensor_copy(mask_t[0:KK, b, :, :], maskT_u8[0:KK, b, :, :])
                    else:
                        last = STT(mask_t[0:KK, b, :, :], triT_u8[0:KK, :, :], 0.5,
                                   padT_u8[0:KK, b, :].unsqueeze(2).broadcast_to([KK, KT, S]), ALU.is_lt, ALU.is_ge)
                last.then_inc(maskt_done, 1)

            def combine(g):
                dve.wait_ge(pv_done, KT * (g + 1))
                if g:
                    dve.wait_ge(o_done, g)
                pv = ps[:, BANK_PV + g % 2, 0:2 * T].rearrange("p (r h s) -> p r h s", r=2, h=2)
                TS(oc_t[:, :, :], pv[:, :, 0, :], cst[:, C_SEL:C_SEL + 1], None, ALU.mult).then_inc(oc_half, 1)
                dve.wait_ge(oc_half, g + 1)
                STT(oc[:, :, :], pv[:, :, 1, :], cst[:, C_SEL + 1:C_SEL + 2], oc_t[:, :, :], ALU.mult, ALU.add)\
                    .then_inc(oc_done, 1)

            def normalise(g):
                dve.wait_ge(den_done, g + 1)
                b = g % B
                V.reciprocal(rden[:, :, :].rearrange("p r s -> p (r s)"), ps[:, BANK_PV + g % 2, 256:256 + 2 * S])\
                    .then_inc(rden_done, 1)
                dve.wait_ge(rden_done, g + 1)
                TT(o_all[:, :, b * S:(b + 1) * S], oc[:, :, :], rden[:, :, :], ALU.mult).then_inc(o_done, 1)

            def attention(l):
                for g in range(l * B, (l + 1) * B):
                    if g % B == 0:
                        for item in head_items(g):
                            side(item)
                    for kt, slot in enumerate(aux_slots(g)):
                        if kt == 3 and g % B:
                            normalise(g - 1)
                        for item in slot:
                            side(item)
                        if kt == KT - 1 and g + 2 < G and (g + 2) // B in MASKED:
                            mask_by_query(g + 2)
                    combine(g)
                normalise((l + 1) * B - 1)

            def top2(ph, p, n_e):
                def v(i):
                    return sm[:, i, 0:NT * n_e].rearrange("p (t e) -> p t e", e=n_e)

                def one(i):
                    return s1[:, i, :].unsqueeze(2).broadcast_to([T, NT, n_e])

                rank = cst[0:T, C_RANK:C_RANK + n_e].unsqueeze(1).broadcast_to([T, NT, n_e])
                V.reduce_max(s1[:, 2, :], p, AX.X).then_inc(dve_step, 1)
                after(dve, "dve", ph, "v1")
                TT(v(3), p, one(2), ALU.is_equal).then_inc(dve_step, 1)
                after(dve, "dve", ph, "eq1")
                TT(v(5), v(3), rank, ALU.mult).then_inc(dve_step, 1)
                after(dve, "dve", ph, "sc1")
                V.reduce_max(s1[:, 3, :], v(5), AX.X).then_inc(dve_step, 1)
                after(dve, "dve", ph, "m1")
                TT(v(4), v(5), one(3), ALU.is_equal).then_inc(dve_step, 1)
                after(dve, "dve", ph, "oh1")
                STT(v(6), v(4), NEG, p, ALU.mult, ALU.add).then_inc(dve_step, 1)
                after(dve, "dve", ph, "p2")
                V.reduce_max(s1[:, 4, :], v(6), AX.X).then_inc(dve_step, 1)
                after(dve, "dve", ph, "v2")
                TT(v(3), v(6), one(4), ALU.is_equal).then_inc(dve_step, 1)
                after(dve, "dve", ph, "eq2")
                TT(v(5), v(3), rank, ALU.mult).then_inc(dve_step, 1)
                after(dve, "dve", ph, "sc2")
                V.reduce_max(s1[:, 5, :], v(5), AX.X).then_inc(dve_step, 1)
                after(dve, "dve", ph, "m2")
                TT(v(7), v(5), one(5), ALU.is_equal).then_inc(dve_step, 1)
                after(dve, "dve", ph, "oh2")

            def moe(ph, n):
                def v(i):
                    return sm[:, i, 0:NT * E].rearrange("p (t e) -> p t e", e=E)

                def one(i):
                    return s1[:, i, :].unsqueeze(2).broadcast_to([T, NT, E])

                def did(step):
                    after(dve, "dve", ph, step)

                lg = ps[0:T, 5, 0:NT * E].rearrange("p (t e) -> p t e", e=E)
                after(dve, "pe", ph, "gate")
                if n == 2:
                    TT(v(0), lg, rows[:, R_RB2, 0:E].unsqueeze(1).broadcast_to([T, NT, E]), ALU.add).then_inc(dve_step, 1)
                    did("logits")
                    top2(ph, v(0), E)
                    TT(s1[:, 7, :], s1[:, 4, :], s1[:, 2, :], ALU.subtract).then_inc(dve_step, 1)
                    after(dve, "act", ph, "exp")
                    TS(s1[:, 9, :], s1[:, 8, :], 1.0, None, ALU.add).then_inc(dve_step, 1)
                    did("plus")
                    V.reciprocal(s1[:, 6, :], s1[:, 9, :]).then_inc(dve_step, 1)
                    did("inv")
                    TT(s1[:, 1, :], s1[:, 8, :], s1[:, 6, :], ALU.mult).then_inc(dve_step, 1)
                    TT(v(9), v(4), one(6), ALU.mult).then_inc(dve_step, 1)
                    did("w1")
                    TT(v(10), v(7), one(1), ALU.mult).then_inc(dve_step, 1)
                    did("w2")
                    TT(v(8), v(9), v(10), ALU.add).then_inc(dve_step, 1)
                else:
                    V.tensor_copy(v(0), lg).then_inc(dve_step, 1)
                    did("logits")
                    V.reduce_max(s1[:, 0, :], v(0), AX.X).then_inc(dve_step, 1)
                    did("max")
                    TT(v(1), v(0), one(0), ALU.subtract).then_inc(dve_step, 1)
                    after(dve, "act", ph, "exp")
                    V.reduce_sum(s1[:, 1, :], v(2), AX.X).then_inc(dve_step, 1)
                    did("sum")
                    V.reciprocal(s1[:, 6, :], s1[:, 1, :]).then_inc(dve_step, 1)
                    did("recip")
                    TT(v(10), v(2), one(6), ALU.mult).then_inc(dve_step, 1)
                    did("probs")
                    top2(ph, v(10), E)
                    TT(v(9), v(4), v(7), ALU.add).then_inc(dve_step, 1)
                    STT(s1[:, 8, :], s1[:, 2, :], 1e-9 if n == 1 else 0.0, s1[:, 4, :], ALU.add, ALU.add).then_inc(dve_step, 1)
                    did("den")
                    V.reciprocal(s1[:, 9, :], s1[:, 8, :]).then_inc(dve_step, 1)
                    TT(v(11), v(9), v(10), ALU.mult).then_inc(dve_step, 1)
                    did("cp")
                    TT(v(8), v(11), one(9), ALU.mult).then_inc(dve_step, 1)
                did("W")
                if n != 1:
                    TT(x[:, :, :], x[:, :, :], (hbuf if n == 0 else y)[:, :, :], ALU.add).then_inc(dve_step, 1)
                    did("base")
                for e in range(E):
                    after(dve, "pe", ph, f"y{e}")
                    for t in range(NT):
                        last = STT(x[:, t, :], ps[0:T, 4 + e % 2, t * D:(t + 1) * D], sm[:, 8, t * E + e:t * E + e + 1],
                                   x[:, t, :], ALU.mult, ALU.add)
                    last.then_inc(dve_step, 1)
                    did(f"acc{e}")
                after(dve, "pe", ph, "b2")
                TT(x[:, :, :], ps[0:T, 4, :].rearrange("p (t d) -> p t d", d=D), x[:, :, :], ALU.add).then_inc(dve_step, 1)
                did("b2")

            V.memset(mask_q[:, :, :], 0.0)
            V.memset(mask_t[:, :, :, :], 0.0)
            V.memset(ones_b[:, :], 1.0)
            dve.wait_ge(kvw_in, 32)
            for item in FIRST_ITEMS:
                side(item)
            dve.wait_ge(const_in, 16 * N_CONST)
            V.tensor_copy(hot[:, :], hot_f)
            TS(id_mask[:, :], ident, MASK, None, ALU.mult)
            V.tensor_copy(id_b[:, :], ident)
            V.tensor_copy(blk_b[0:T, :], cst[0:T, C_BLK:C_BLK + T])
            V.tensor_copy(bm16[:, :], cst[:, C_BM:C_BM + H])
            V.tensor_copy(m4[:, :], cst[:, C_M4:C_M4 + HQ]).then_inc(consts_ready, 1)
            dve.wait_ge(consts_ready, 1)
            masks_by_key(1)
            dve.wait_ge(x_in, 16)

            for ph in program_order():
                kind, n = ph
                if kind == "ln":
                    src, dst = ln_io(n)
                    for t in range(NT):
                        last = V.bn_stats(st[:, t, :], src[:, t, :])
                    last.then_inc(dve_step, 1)
                    after(dve, "dve", ph, "stats")
                    for t in range(NT):
                        last = V.bn_aggr(mv[:, t, :], st[:, t, :])
                    last.then_inc(dve_step, 1)
                    after(dve, "dve", ph, "aggr")
                    TS(ve[:, :], mv[:, :, 1], 1e-5, None, ALU.add).then_inc(dve_step, 1)
                    after(dve, "pool", ph, "rstd")
                    for t in range(NT):
                        last = TS(dst[:, t, :], src[:, t, :], mv[:, t, 0:1], rstd[:, t:t + 1], ALU.subtract, ALU.mult)
                    last.then_inc(dve_step, 1)
                    after(dve, "dve", ph, "norm")
                elif kind == "affine":
                    w, b = (R_LN1W, R_LN1B) if n == 0 else (R_LN2W, R_LN2B)
                    TT(z[:, :, :], z[:, :, :], rows[:, w, :].unsqueeze(1).broadcast_to([T, NT, D]), ALU.mult).then_inc(dve_step, 1)
                    after(dve, "dve", ph, "mul")
                    TT(z[:, :, :], z[:, :, :], rows[:, b, :].unsqueeze(1).broadcast_to([T, NT, D]), ALU.add).then_inc(dve_step, 1)
                elif kind == "count":
                    after(dve, "pe", ph, "count")
                    TS(keep[:, :], ps[:, 5, 0:TOK], KV - 0.5, None, ALU.is_lt).then_inc(dve_step, 1)
                elif kind == "q":
                    after(dve, "pe", ph, "q")
                    scale = float(D) ** -0.5 if n == 2 else float(DH) ** -0.5
                    for quad in range(QUADS):
                        TS(qs[:, quad, :], ps[:, quad, 0:TOK], xb[:, n, 2 + quad:3 + quad], scale, ALU.add, ALU.mult)
                    TS(qnf[:, :], ps[:, 4, 0:TOK], xb[:, n, 1:2], scale, ALU.add, ALU.mult).then_inc(dve_step, 1)
                    after(dve, "dve", ph, "scaled")
                    if n == 2:
                        TT(qs[:, :, :], qs[:, :, :], keep[:, :].unsqueeze(1).broadcast_to([P, 4, TOK]), ALU.mult).then_inc(dve_step, 1)
                        TT(qn16[:, :], qnf[:, :], keep[:, :], ALU.mult).then_inc(dve_step, 1)
                    else:
                        V.tensor_copy(qn16[:, :], qnf[:, :]).then_inc(dve_step, 1)
                    after(dve, "act", ph, "hi_lo")
                    TT(qv[64:96, :, :], qs[64:96, :, :], qv_hi[64:96, :, :], ALU.subtract).then_inc(dve_step, 1)
                    attention(n)
                    if n == 1:
                        masks_by_key(2)
                elif kind == "out":
                    dve.wait_ge(o_done, B * (n + 1))
                    if n == 1:
                        TT(o_all[:, :, :], o_all[:, :, :], keep[:, :].unsqueeze(1).broadcast_to([P, 2, TOK]), ALU.mult).then_inc(dve_step, 1)
                    else:
                        TS(o_all[:, 0, :], o_all[:, 0, :], xb[:, n, 6:7], None, ALU.add)
                        TS(o_all[:, 1, :], o_all[:, 1, :], xb[:, n, 7:8], None, ALU.add).then_inc(dve_step, 1)
                    TT(x[:, :, :], x[:, :, :], rows[:, R_BO + n, :].unsqueeze(1).broadcast_to([T, NT, D]), ALU.add).then_inc(dve_step, 1)
                    after(dve, "dve", ph, "with_bo")
                    after(dve, "pe", ph, "projected")
                    TT(x[:, :, :], ps[0:T, 3, :].rearrange("p (t d) -> p t d", d=D), x[:, :, :], ALU.add).then_inc(dve_step, 1)
                    after(dve, "dve", ph, "added")
                elif kind == "moe":
                    moe(ph, n)
                elif kind == "self":
                    self_dve(dve, ph)
                elif kind == "gated":
                    gated_dve(dve, ph, top2)


def kernel(**inputs):
    from concourse.bass_utils import run_bass_kernel_spmd
    from concourse import bacc

    f = {k: np.asarray(v) for k, v in inputs.items()}
    f4 = np.float32

    def head_blocks(w):
        full = np.zeros((D, D), f4)
        for h in range(H):
            full[h * DH:(h + 1) * DH, h * DH:(h + 1) * DH] = w[h].T
        return full

    none = np.zeros(D, f4)
    layers = [
        (f["L0_xattn_Wq"], f["L0_xattn_Wk"], f["L0_xattn_Wv"], f["L0_xattn_Wo"],
         f["L0_xattn_bq"], f["L0_xattn_bk"], f["L0_xattn_bv"], f["L0_xattn_bo"]),
        (f["L1_xattn_W_Q"].T, f["L1_xattn_W_K"].T, f["L1_xattn_W_V"].T, f["L1_xattn_W_O"].T, none, none, none, none),
        (f["L2_xattn_Wq"].T, f["L2_xattn_Wk"].T, f["L2_xattn_Wv"].T, f["L2_xattn_Wo"].T,
         f["L2_xattn_bq"], f["L2_xattn_bk"], f["L2_xattn_bv"], f["L2_xattn_bo"]),
        (head_blocks(f["L3_xattn_wq"]), head_blocks(f["L3_xattn_wk"]), head_blocks(f["L3_xattn_wv"]), f["L3_xattn_wo"].T,
         f["L3_xattn_bq"].reshape(D), f["L3_xattn_bk"].reshape(D), f["L3_xattn_bv"].reshape(D), f["L3_xattn_bo"]),
    ]
    kvw = np.zeros((P, L, 256), f4)
    xw = np.zeros((L, P, 7 * D), f4)
    xb = np.zeros((P, L, 8), f4)
    rows = np.zeros((R_N, D), f4)
    for l, (wq, wk, wv, wo, bq, bk, bv, bo) in enumerate(layers):
        kvw[:, l, 0:D], kvw[:, l, D:] = wk, wv
        xw[l, :, 0:D] = wq
        xb[:, l, 0], xb[:, l, 1] = bk, bq
        for quad in range(QUADS):
            for blk in range(3):
                c = D * (1 + quad) + 32 * blk
                xw[l, :, c:c + 32] = wq[:, 32 * quad:32 * quad + 32]
                xb[32 * blk:32 * blk + 32, l, 2 + quad] = bq[32 * quad:32 * quad + 32]
        for t8 in range(8):
            r, j = divmod(t8, 4)
            xw[l, 32 * j:32 * j + 16, D * (5 + r):D * (6 + r)] = wo[16 * t8:16 * t8 + 16, :]
            xb[32 * j:32 * j + 16, l, 6 + r] = bv[16 * t8:16 * t8 + 16]
        rows[R_BO + l] = bo
    rows[R_LN1W], rows[R_LN1B] = f["L0_ffn_ln1_w"], f["L0_ffn_ln1_b"]
    rows[R_LN2W], rows[R_LN2B] = f["L0_ffn_ln2_w"], f["L0_ffn_ln2_b"]
    rows[R_FBO], rows[R_FBV] = f["L0_ffn_b_o"], f["L0_ffn_b_qkv"][2 * D:]
    rows[R_RB2, 0:E] = f["L3_ffn_rb2"]
    rows[R_GATE, 0:E2] = f["L2_ffn_gates"]

    p = np.arange(P)
    cst = np.zeros((P, C_W), f4)
    cst[:, C_ID:C_ID + P] = np.eye(P)
    for m in range(P):
        cst[m + 16 if m % 32 < 16 else m, C_PERM + m] = 1.0
    cst[:, C_BM:C_BM + H] = p[:, None] // DH == np.arange(H)
    cst[:, C_M4:C_M4 + HQ] = p[:, None] % 32 // DH == np.arange(HQ)
    cst[:, C_SEL:C_SEL + 2] = p[:, None] % 16 // DH == np.arange(2)
    q, k = np.arange(T)[:, None], np.arange(T)[None, :]
    cst[0:T, C_BLK:C_BLK + T] = np.where(q // S == k // S, 0.0, NEG)
    cst[0:T, C_CAU:C_CAU + T] = np.where((q // S == k // S) & (k <= q), 0.0, NEG)
    cst[:, C_RANK:C_RANK + E2] = E2 - np.arange(E2)
    cst[:, C_HOT:] = np.where(p[:, None] == np.tile(np.arange(S), H), MASK, 0.0)

    def by_key(m):
        m = m.reshape(m.shape[:-1] + (KT, KK))
        return np.moveaxis(m, -1, 0)

    mask = f["mask_BxSxS2_bf0"]
    tri = f["mask_SxS2_bk0"]
    pad = f["mask_BxS2_bk1"]

    def experts(w1, w2):
        w2 = w2.reshape(E, FC, P, D).transpose(0, 2, 1, 3).reshape(E, P, FC * D)
        return np.concatenate([w1, w2], axis=2)

    moe = np.concatenate([experts(f["L0_ffn_w1"], f["L0_ffn_w2"]),
                          experts(f["L1_ffn_w1"].transpose(0, 2, 1), f["L1_ffn_w2"].transpose(0, 2, 1)),
                          experts(f["L3_ffn_we1"], f["L3_ffn_we2"])])
    b1 = np.stack([f["L0_ffn_b1"], f["L1_ffn_b1"], f["L3_ffn_be1"]]).reshape(3, E, FC, P).transpose(3, 0, 1, 2)
    b2 = np.stack([f["L0_ffn_b2"], f["L1_ffn_b2"], f["L3_ffn_be2"]], axis=1)
    wg = np.stack([f["L0_ffn_w_gate"], f["L1_ffn_router_w"].T, f["L3_ffn_rw2"]], axis=1)
    qkv2 = np.concatenate([f["L2_ffn_q_proj"], f["L2_ffn_k_proj"], f["L2_ffn_v_proj"]], axis=2)
    arrays = {
        "x": f["x"].reshape(TOK, D), "ctxT": f["ctx_1024"].transpose(0, 2, 1), "kvw": kvw, "xw": xw, "xb": xb,
        "rows": rows, "cst": cst, "mask": mask.transpose(1, 0, 2), "pad": pad, "tri": tri,
        "maskT": by_key(mask).transpose(0, 1, 3, 2), "triT": by_key(tri).transpose(0, 2, 1), "padT": by_key(pad),
        "moe": moe, "b1": b1, "b2": b2, "wg": wg,
        "fw": np.concatenate([f["L0_ffn_w_qkv"], f["L0_ffn_w_o"]], axis=1),
        "fb": f["L0_ffn_b_qkv"][0:2 * D].reshape(2, D).T, "rw1": f["L3_ffn_rw1"], "rb1": f["L3_ffn_rb1"].reshape(D, 1),
        "sim": f["L2_ffn_sim_matrix"], "qkv2": qkv2.transpose(1, 0, 2).reshape(D, E2 * 192),
        "o2": f["L2_ffn_o_proj"].transpose(1, 0, 2).reshape(HD2, E2 * D),
    }
    nc = bacc.Bacc("TRN2", target_bir_lowering=False, num_devices=1)
    given, aps = {}, {}
    for name, arr in arrays.items():
        arr = np.ascontiguousarray(arr)
        given[f"in_{name}"] = arr
        aps[name] = nc.dram_tensor(f"in_{name}", arr.shape, mybir.dt.from_np(arr.dtype), kind="ExternalInput").ap()
    out = nc.dram_tensor("out", (TOK, D), F32, kind="ExternalOutput").ap()
    build(nc, aps, out)
    r = run_bass_kernel_spmd(nc, [given], core_ids=[0])
    return r.results[0]["out"].reshape(B, S, D)
```

```python
from contextlib import ExitStack

import concourse.bass as bass
from concourse import mybir
import numpy as np

F32 = mybir.dt.float32
F16 = mybir.dt.float16
BF16 = mybir.dt.bfloat16
U8 = mybir.dt.uint8
ALU = mybir.AluOpType
ACT = mybir.ActivationFunctionType
AX = mybir.AxisListType

P = 128
B, S, D = 8, 56, 128
H, DH = 16, 8
KV = 1500
KT = 12
KK = KV // KT
KPAD = 1504
L = 4
G = L * B
T = 2 * S
NT = B // 2
TOK = B * S
QUADS, HQ = 4, 4
HC = H * S
CH = HC // P
KS = 3
KP = KV // KS
E, F, FC = 8, 512, 4
SLOTS = 3
MASKED = (1, 2)
MASK = -32768.0
NEG = -(2.0 ** 100)
E2, HD2 = 16, 64

C_ID, C_PERM, C_BM, C_M4, C_SEL, C_BLK, C_CAU, C_RANK, C_HOT = 0, 128, 256, 272, 276, 278, 390, 502, 518
C_W = C_HOT + HC
R_LN1W, R_LN1B, R_LN2W, R_LN2B, R_BO, R_FBO, R_FBV, R_RB2, R_GATE = 0, 1, 2, 3, 4, 8, 9, 10, 11
R_N = 12


BEFORE, BETWEEN, HALFWAY = range(3)


def aux_slots(g):
    slots = [[] for _ in range(KT)]
    if (g + 1) % B:
        n = 0
        for s in range(10):
            for where in (BEFORE, HALFWAY) if s else (BEFORE, BETWEEN, HALFWAY):
                slots[s].append((where, ("S", g + 1, n)))
                n += 1
        slots[10] += [(BETWEEN, ("M", g + 1, 0)), (HALFWAY, ("M", g + 1, 1))]
    if g % B:
        slots[1].append((BETWEEN, ("D", g - 1, 0)))
    slots[3].append((BETWEEN, ("V", g, 1)))
    slots[6].append((BETWEEN, ("V", g, 2)))
    if g + 1 < G:
        slots[11].append((HALFWAY, ("V", g + 1, 0)))
    if g + 2 < G:
        for i, s in enumerate((5, 8, 10)):
            slots[s].append((BETWEEN if s < 10 else BEFORE, ("K", g + 2, i)))
    return [sorted(slot, key=lambda entry: entry[0]) for slot in slots]


def head_items(g):
    return [("S", g, n) for n in range(CH * KS)] + [("M", g, 0), ("M", g, 1)]


FIRST_ITEMS = [("K", 0, i) for i in range(KS)] + [("V", 0, 0)] + [("K", 1, i) for i in range(KS)]


def all_items():
    items = list(FIRST_ITEMS)
    for g in range(G):
        if g % B == 0:
            items += head_items(g)
        for slot in aux_slots(g):
            items += [item for _, item in slot]
        if g % B == B - 1:
            items.append(("D", g, 0))
    return items


TOP2 = ["v1", "eq1", "sc1", "m1", "oh1", "p2", "v2", "eq2", "sc2", "m2", "oh2"]
EP = E2 // 2


def phase_steps(phase):
    kind, n = phase
    if kind == "ln":
        return {"dve": ["stats", "aggr", "var", "norm"], "pool": ["rstd"]}
    if kind == "affine":
        return {"dve": ["mul", "add"]}
    if kind == "turn":
        return {"pe": ["turned"], "act": ["copied"]}
    if kind == "count":
        return {"pe": ["count"], "dve": ["keep"]}
    if kind == "q":
        return {"pe": ["qn", "q"], "act": ["hi", "hi_lo"],
                "dve": ["qnf"] * (n == 2) + ["q16", "scaled"] + ["kept"] * (n == 2) + ["lo"]}
    if kind == "out":
        return {"dve": ["biased", "with_bo", "added"], "pe": ["projected"]}
    if kind == "moe":
        pe = ["r1"] * (n == 2) + ["gate", "h0"]
        for e in range(E):
            pe += [f"h{e + 1}"] * (e + 1 < E) + [f"y{e}"]
        softmax = ["max", "shift", "sum", "recip", "probs"] * (n != 2)
        weigh = ["gap", "plus", "inv", "second", "w1", "w2", "W"] if n == 2 else ["chosen", "den", "inv", "cp", "W"]
        return {"pe": pe + ["w_turned", "b2"],
                "act": ["r1"] * (n == 2) + ["exp"] + [f"h{e}_{c}" for e in range(E) for c in range(FC)] + ["w_copied"],
                "dve": ["logits"] + softmax + TOP2 + weigh + ["base"] * (n != 1) + [f"acc{e}" for e in range(E)] + ["b2"]}
    if kind == "self":
        pe, dve = ["qk", "v", "s0"], ["q", "k", "v", "max0", "shift0"]
        for t in range(NT):
            pe += [f"s{t + 1}"] * (t + 1 < NT) + [f"t{t}_{c}" for c in range(4)] + [f"o{t}"]
            dve += [f"max{t + 1}", f"shift{t + 1}"] * (t + 1 < NT) + [f"recip{t}", f"o{t}"]
        return {"pe": pe + ["o_turned", "proj"], "dve": dve + ["hb", "h"], "pool": [f"kb{t}" for t in range(NT)],
                "act": [s for t in range(NT) for s in [f"exp{t}"] + [f"pt{t}_{c}" for c in range(4)]] + ["o_copied"]}
    assert kind == "gated"
    turns = [f"m{t}{half}" for t in range(NT) for half in "ab"]
    return {"pe": ["sim2", "logits"] + [f"p{p}_{t}" for p in range(EP) for t in range(NT)] + ["qk_turned", "s", "t", "o"]
            + turns[0:2] + [x for t in range(NT) for x in turns[2 * t + 2:2 * t + 4] + [f"f{t}"]],
            "act": ["gate_exp", "exp", "qk_copied", "s_exp", "pt"] + turns,
            "pool": ["sim_norm", "y_norm"],
            "dve": ["sim2", "y2", "y2_sum", "y2_max", "sim2_max", "sim_unit", "gate1", "gate", "cos", "logits", "pos", "any",
                    "gated", "gmax"] + TOP2 + ["two", "none", "fallback", "active", "shift", "em", "sum", "recip", "rw"]
            + [f"{k}{p}_{t}" for p in range(EP) for k in "ab" for t in range(NT)]
            + ["masked", "smax", "sshift", "ssum", "srecip", "o"] + [f"mix{t}" for t in range(NT)] + ["added"]}


def program_order():
    seq = []
    turn = ln = moe = 0
    for l in range(L):
        if l in MASKED:
            seq.append(("count", l))
        seq += [("ln", ln), ("turn", turn), ("q", l), ("out", l), ("ln", ln + 1)]
        ln, turn = ln + 2, turn + 1
        if l == 0:
            seq += [("ln", ln), ("affine", 0), ("turn", turn), ("self", 0), ("ln", ln + 1), ("affine", 1)]
            ln, turn = ln + 2, turn + 1
        seq.append(("turn", turn))
        turn += 1
        if l == 2:
            seq.append(("gated", 0))
        else:
            seq.append(("moe", moe))
            moe += 1
    return seq


def step_counts():
    n = {"pe": 0, "act": 0, "dve": 0, "pool": 0}
    at = {}
    for phase in program_order():
        for who, names in phase_steps(phase).items():
            for step in names:
                n[who] += 1
                at[(who, phase, step)] = n[who]
    return at


def build(nc, a, out):
    at = step_counts()
    items = all_items()
    place = {item: n for n, item in enumerate(items)}

    with ExitStack() as ctx:
        def sb(name, shape, dt):
            return ctx.enter_context(nc.sbuf_tensor(name, shape, dt))

        def sem(name):
            return ctx.enter_context(nc.semaphore(name))

        ps = ctx.enter_context(nc.psum_tensor("ps", [P, 8, 512], F32))
        BANK_PV, BANK_AUX, N_AUX = 4, 5, 3

        ctxT = sb("ctxT", [P, 3, KV], F32)
        khi = sb("khi", [P, 2, KV], F16)
        klo = sb("klo", [P, 2, KV], F16)
        kq = sb("kq", [P, 2, QUADS, KPAD], F16)
        v_aug = sb("v_aug", [P, 2, KT, 8, 32], F32)
        probs = sb("probs", [P, 2, HC], F32)
        qn = sb("qn", [P, 2, H, S], F16)
        qb = sb("qb", [P, 2, QUADS, HQ, S], F16)
        mx_part = sb("mx_part", [P, 2, CH, KS], F32)
        mx = sb("mx", [P, 2, 8], F32)
        oc_t = sb("oc_t", [P, 2, S], F32)
        oc = sb("oc", [P, 2, S], F32)
        rden = sb("rden", [P, 2, S], F32)
        o_all = sb("o_all", [P, 2, TOK], F32)
        mask_u8 = sb("mask_u8", [S, 2, KV], U8)
        tri_u8 = sb("tri_u8", [S, KV], U8)
        mask_q = sb("mask_q", [P, 2, KV], BF16)
        maskT_u8 = sb("maskT_u8", [P, B, KT, S], U8)
        triT_u8 = sb("triT_u8", [P, KT, S], U8)
        padT_u8 = sb("padT_u8", [P, B, KT], U8)
        mask_t = sb("mask_t", [P, B, KT, S], BF16)
        keep = sb("keep", [P, TOK], F32)
        weights = sb("weights", [P, 5120], F32)
        big1 = sb("big1", [P, 4, TOK], F32)
        big2 = sb("big2", [P, 4, TOK], F32)
        big3 = weights[:, 3072:3072 + 4 * TOK].rearrange("p (a c) -> p a c", a=4)
        big0 = probs[:, :, :].rearrange("p a c -> p (a c)").rearrange("p (a c) -> p a c", a=4)
        kvw = sb("kvw", [P, L, 256], F32)
        xw = sb("xw", [P, 7 * D], F32)
        xb = sb("xb", [P, L, 8], F32)
        rows = sb("rows", [T, R_N, D], F32)
        cst = sb("cst", [P, C_W - HC], F32)
        hot_f = big1[:, 0:2, :].rearrange("p a c -> p (a c)")
        hot = sb("hot", [P, HC], BF16)
        id_mask = sb("id_mask", [P, P], BF16)
        id_b = sb("id_b", [P, P], BF16)
        blk_b = sb("blk_b", [P, T], BF16)
        ones_b = sb("ones_b", [P, P], BF16)
        ones_f = sb("ones_f", [P, P], F32)
        bm16 = sb("bm16", [P, H], F16)
        m4 = sb("m4", [P, HQ], F16)
        x = sb("x", [T, NT, D], F32)
        y = sb("y", [T, NT, D], F32)
        z = sb("z", [T, NT, D], F32)
        v_self = sb("v_self", [T, NT, H, DH + 1], F32)
        hbuf = sb("hbuf", [T, NT, D], F32)
        yT = sb("yT", [P, TOK], F32)
        qnf = sb("qnf", [P, TOK], F32)
        qn16 = sb("qn16", [P, TOK], F16)
        st = sb("st", [T, NT, 6], F32)
        mv = sb("mv", [T, NT, 2], F32)
        ve = sb("ve", [T, NT], F32)
        rstd = sb("rstd", [T, NT], F32)
        mhalf = sb("mhalf", [P, NT * 8], F32)
        sm = sb("sm", [T, 16, NT * E2], F32)
        s1 = sb("s1", [T, 12, NT], F32)
        rw1 = sb("rw1", [P, D], F32)
        rb1 = sb("rb1", [P, 1], F32)
        b1 = sb("b1", [P, 3, E, FC], F32)
        b2 = sb("b2", [E, 3, D], F32)
        wg = sb("wg", [P, 3, E], F32)
        fw = sb("fw", [P, 4 * D], F32)
        fb = sb("fb", [P, 2], F32)
        sim = sb("sim", [P, E2], F32)
        sim2 = sb("sim2", [P, 4, E2], F32)
        sumh = sb("sumh", [T, 4, H], F32)

        ident = cst[:, C_ID:C_ID + P]
        perm = cst[:, C_PERM:C_PERM + P]

        qs = big1
        qv = big2[:, 0:2, :].rearrange("p a c -> p (a c)").bitcast(F16).rearrange("p (a c) -> p a c", a=4)
        qv_hi = big2[:, 2:4, :].rearrange("p a c -> p (a c)").bitcast(F16).rearrange("p (a c) -> p a c", a=4)

        ctx_in = [sem(f"ctx_in{i}") for i in range(3)]
        const_in = sem("const_in")
        kvw_in = sem("kvw_in")
        x_in = sem("x_in")
        xw_in = sem("xw_in")
        weights_in = [sem(f"weights_in{i}") for i in range(SLOTS)]
        gated_in = sem("gated_in")
        mask_in = [sem(f"mask_in{i}") for i in range(2)]
        consts_ready = sem("consts_ready")
        pool_ready = sem("pool_ready")
        aux_filled = sem("aux_filled")
        khi_done = sem("khi_done")
        klo_done = sem("klo_done")
        v_done = sem("v_done")
        smax_done = sem("smax_done")
        mx_done = sem("mx_done")
        mrow_done = sem("mrow_done")
        kq_in = [sem(f"kq_in{i}") for i in range(2)]
        qn_done = sem("qn_done")
        qb_done = sem("qb_done")
        maskq_done = sem("maskq_done")
        maskt_done = sem("maskt_done")
        scores_done = sem("scores_done")
        exp_done = sem("exp_done")
        pv_done = sem("pv_done")
        oc_half = sem("oc_half")
        oc_done = sem("oc_done")
        rden_done = sem("rden_done")
        o_done = sem("o_done")
        out_done = sem("out_done")
        steps = {w: sem(f"{w}_step") for w in ("pe", "act", "dve", "pool")}
        pe_step, act_step, dve_step, pool_step = (steps[w] for w in ("pe", "act", "dve", "pool"))

        block = ctx.enter_context(nc.Block())

        def after(eng, who, phase, step):
            eng.wait_ge(steps[who], at[(who, phase, step)])

        def bank(item):
            return BANK_AUX + place[item] % N_AUX

        def masks_before(g):
            return sum(1 for k in range(g + 1) if k // B in MASKED)

        def weights_count(mi, e):
            per = [len([k for k in range(E) if k % SLOTS == s]) for s in range(SLOTS)]
            return 16 * (mi * per[e % SLOTS] + e // SLOTS + 1)

        def prior(ph, kind):
            seq = program_order()
            return [p for p in seq[:seq.index(ph)] if p[0] == kind][-1]

        def turn_sources():
            seq, out_ = program_order(), []
            for i, p in enumerate(seq):
                if p[0] == "turn":
                    q = seq[i - 1]
                    out_.append(("z" if q[0] == "affine" else "y", q))
            return out_

        mixed = (big0[0:T, :, :].rearrange("p a c -> p (a c)")[:, 0:E2 * HD2], weights[0:T, 4096:5120])
        mixed_t = ((o_all[:, 0, :], o_all[:, 1, :]), (yT[:, :], qnf[:, :]))
        s_buf = big0[0:T, 3, :]
        hbuf_T = keep
        qkv = big1[0:T, :, :].rearrange("p a c -> p (a c)")[:, 0:768].rearrange("p (t c) -> p t c", t=NT)
        N_FILLS = 7
        N_CONST = 15

        def ln_io(n):
            lns = [(x, y), (x, y), (y, z), (hbuf, z)] + [(x, y)] * 6
            return lns[n]

        @block.sync
        def _(sp):
            sp.dma_start(kvw[:, :, :], a["kvw"]).then_inc(kvw_in, 16)
            sp.dma_start(ctxT[:, 0, :], a["ctxT"][0]).then_inc(ctx_in[0], 16)
            sp.dma_start(xb[:, :, :], a["xb"]).then_inc(kvw_in, 16)
            sp.dma_start(cst[:, :], a["cst"][:, 0:C_W - HC]).then_inc(const_in, 16)
            sp.dma_start(x[:, :, :], a["x"].rearrange("(t p) d -> p t d", p=T)).then_inc(x_in, 16)
            sp.dma_start(ctxT[:, 1, :], a["ctxT"][1]).then_inc(ctx_in[1], 16)
            sp.dma_start(hot_f, a["cst"][:, C_W - HC:C_W]).then_inc(const_in, 16)
            sp.dma_start(ctxT[:, 2, :], a["ctxT"][2]).then_inc(ctx_in[2], 16)
            sp.dma_start(rows[:, :, :], a["rows"].rearrange("r d -> (r d)").partition_broadcast(T)
                         .rearrange("p (r d) -> p r d", d=D)).then_inc(const_in, 16)
            sp.dma_start(rw1[:, :], a["rw1"]).then_inc(const_in, 16)
            sp.dma_start(rb1[:, :], a["rb1"]).then_inc(const_in, 16)
            sp.dma_start(b1[:, :, :, :], a["b1"]).then_inc(const_in, 16)
            sp.dma_start(b2[:, :, :], a["b2"]).then_inc(const_in, 16)
            sp.dma_start(wg[:, :, :], a["wg"]).then_inc(const_in, 16)
            sp.dma_start(fw[:, :], a["fw"]).then_inc(const_in, 16)
            sp.dma_start(fb[:, :], a["fb"]).then_inc(const_in, 16)
            sp.dma_start(sim[:, :], a["sim"]).then_inc(const_in, 16)
            sp.dma_start(tri_u8[:, :], a["tri"]).then_inc(const_in, 16)
            sp.dma_start(maskT_u8[0:KK, :, :, :], a["maskT"]).then_inc(const_in, 16)
            sp.dma_start(triT_u8[0:KK, :, :], a["triT"]).then_inc(const_in, 16)
            sp.dma_start(padT_u8[0:KK, :, :], a["padT"]).then_inc(const_in, 16)

            def spread_keys(g):
                sp.wait_ge(klo_done, KS * (g + 1))
                if g >= 2:
                    sp.wait_ge(scores_done, KT * (g - 1))
                else:
                    sp.wait_ge(pool_ready, N_FILLS)
                for quad in range(QUADS):
                    r = slice(32 * quad, 32 * quad + 32)
                    for blk, part in enumerate((khi, klo, khi)):
                        sp.dma_start(kq[32 * blk:32 * blk + 32, g % 2, quad, 0:KV], part[r, g % 2, :])\
                            .then_inc(kq_in[g % 2], 16)

            def load_mask(g):
                if masks_before(g) > 2:
                    sp.wait_ge(maskq_done, masks_before(g) - 2)
                b = g % B
                src = a["mask"][:, b, :] if g // B == 1 else a["pad"][b, :].partition_broadcast(S)
                sp.dma_start(mask_u8[:, g % 2, :], src).then_inc(mask_in[g % 2], 16)

            spread_keys(0)
            spread_keys(1)
            for l in range(L):
                if l:
                    after(sp, "pe", ("out", l - 1), "projected")
                sp.dma_start(xw[:, :], a["xw"][l]).then_inc(xw_in, 16)
                mi = {0: 0, 1: 1, 3: 2}.get(l)
                if l:
                    former = ("gated", 0) if l == 3 else ("moe", l - 1)
                    after(sp, "pe", former, f"f{NT - 1}" if l == 3 else "b2")
                if mi is None:
                    sp.dma_start(weights[:, 0:3072], a["qkv2"]).then_inc(gated_in, 16)
                    sp.dma_start(weights[:, 3072:4096], a["o2"]).then_inc(gated_in, 16)
                else:
                    for e in range(SLOTS):
                        sp.dma_start(weights[:, e * 1024:(e + 1) * 1024], a["moe"][mi * E + e])\
                            .then_inc(weights_in[e], 16)
                for g in range(l * B, (l + 1) * B):
                    if g + 3 < G:
                        sp.wait_ge(v_done, 3 * (g + 1))
                        sp.dma_start(ctxT[:, g % 3, :], a["ctxT"][(g + 3) % B]).then_inc(ctx_in[g % 3], 16)
                    if g + 3 < G and (g + 3) // B in MASKED:
                        load_mask(g + 3)
                    if g + 2 < G:
                        spread_keys(g + 2)
                if mi is not None:
                    for e in range(SLOTS, E):
                        after(sp, "pe", ("moe", mi), f"y{e - SLOTS}")
                        k = e % SLOTS
                        sp.dma_start(weights[:, k * 1024:(k + 1) * 1024], a["moe"][mi * E + e])\
                            .then_inc(weights_in[k], 16)
            after(sp, "dve", ("moe", 2), "b2")
            sp.dma_start(out.rearrange("(t p) d -> p t d", p=T), x[:, :, :]).then_inc(out_done, 16)
            sp.wait_ge(out_done, 16)

        @block.gpsimd
        def _(pool):
            fills = [(mhalf[:, :], -0.5), (kq[:, :, :, KV:KPAD], 0.0), (kq[96:128, :, :, 0:KV], 0.0),
                     (kq[96:97, :, :, 0:KV], 1.0), (v_aug[:, :, :, :, :], 1.0), (qb[96:128, :, :, :, :], 0.0),
                     (ones_f[:, :], 1.0)]
            for n, (dst, value) in enumerate(fills):
                if n:
                    pool.wait_ge(pool_ready, n)
                nc.gpsimd.memset(dst, value).then_inc(pool_ready, 1)

            def rsqrt(ph):
                after(pool, "dve", ph, "var")
                pool.wait_ge(pool_ready, N_FILLS)
                nc.gpsimd.tensor_tensor(rstd[:, :], ve[:, :], mhalf[0:T, 0:NT], ALU.pow).then_inc(pool_step, 1)

            for ph in program_order():
                kind, n = ph
                if kind == "ln":
                    rsqrt(ph)
                elif kind == "gated":
                    after(pool, "dve", ph, "sim2_max")
                    nc.gpsimd.tensor_tensor(sim2[:, 2, :], sim2[:, 1, :], mhalf[:, 0:E2], ALU.pow).then_inc(pool_step, 1)
                    after(pool, "dve", ph, "y2_max")
                    nc.gpsimd.tensor_tensor(s1[:, 1, :], s1[:, 0, :], mhalf[0:T, 0:NT], ALU.pow).then_inc(pool_step, 1)
                elif kind == "self":
                    after(pool, "dve", ph, "k")
                    for t in range(NT):
                        if t:
                            after(pool, "pe", ph, f"s{t - 1}")
                        nc.gpsimd.tensor_tensor(big3.rearrange("p a c -> p (a c)").rearrange("p (h k) -> p h k", h=H),
                                                keep[:, t * T:(t + 1) * T].unsqueeze(1).broadcast_to([P, H, T]),
                                                cst[:, C_BM:C_BM + H].unsqueeze(2).broadcast_to([P, H, T]), ALU.mult)\
                            .then_inc(pool_step, 1)
                elif kind == "q":
                    for b in range(B):
                        g = n * B + b
                        if b == 0:
                            pool.wait_ge(consts_ready, 1)
                            after(pool, "dve", ph, "q16")
                        if g >= 2:
                            pool.wait_ge(smax_done, CH * KS * (g - 1))
                        src = qn16[:, b * S:(b + 1) * S].unsqueeze(1).broadcast_to([P, H, S])
                        nc.gpsimd.tensor_tensor(qn[:, g % 2, :, :], src,
                                                bm16[:, :].unsqueeze(2).broadcast_to([P, H, S]), ALU.mult)\
                            .then_inc(qn_done, 1)
                        if g >= 2:
                            pool.wait_ge(scores_done, KT * (g - 1))
                        if b == 0:
                            after(pool, "dve", ph, "lo")
                            after(pool, "act", ph, "hi")
                        src = qv[0:96, :, b * S:(b + 1) * S].unsqueeze(2).broadcast_to([96, QUADS, HQ, S])
                        sel = m4[0:96, :].unsqueeze(1).unsqueeze(3).broadcast_to([96, QUADS, HQ, S])
                        nc.gpsimd.tensor_tensor(qb[0:96, g % 2, :, :, :], src, sel, ALU.mult).then_inc(qb_done, 1)

        @block.tensor
        def _(pe):
            mm = nc.tensor.matmul

            def gated_pe(pe, ph):
                after(pe, "dve", ph, "sim2")
                after(pe, "act", prior(ph, "turn"), "copied")
                mm(ps[:, 1, 0:E2], ones_f[:, :], sim2[:, 0, :], start=True, stop=True).then_inc(pe_step, 1)
                after(pe, "dve", ph, "sim_unit")
                for t in range(NT):
                    last = mm(ps[0:T, 2, t * E2:(t + 1) * E2], yT[:, t * T:(t + 1) * T], sim2[:, 3, :], start=True, stop=True)
                last.then_inc(pe_step, 1)
                pe.wait_ge(gated_in, 32)
                after(pe, "dve", ph, "cos")
                for p in range(EP):
                    for t in range(NT):
                        if p >= 2:
                            after(pe, "dve", ph, f"b{p - 2}_{t}")
                        mm(ps[0:T, 4 * (p % 2) + t, 0:384], yT[:, t * T:(t + 1) * T], weights[:, p * 384:(p + 1) * 384],
                           start=True, stop=True).then_inc(pe_step, 1)
                after(pe, "dve", ph, f"b{EP - 1}_{NT - 1}")
                for t in range(NT):
                    nc.tensor.transpose(ps[0:HD2, 0, t * T:(t + 1) * T], qkv[:, t, 0:64], ident[0:T, 0:T])
                    last = nc.tensor.transpose(ps[0:HD2, 1, t * T:(t + 1) * T], qkv[:, t, 64:128], ident[0:T, 0:T])
                last.then_inc(pe_step, 1)
                after(pe, "act", ph, "qk_copied")
                for t in range(NT):
                    cols = slice(t * T, (t + 1) * T)
                    last = mm(ps[0:T, 2, cols], big2[0:HD2, 0, cols], big2[0:HD2, 1, cols], start=True, stop=True)
                last.then_inc(pe_step, 1)
                after(pe, "act", ph, "s_exp")
                for t in range(NT):
                    last = nc.tensor.transpose(ps[0:T, 3, t * T:(t + 1) * T], big2[0:T, 2, t * T:(t + 1) * T], ident[0:T, 0:T])
                last.then_inc(pe_step, 1)
                after(pe, "act", ph, "pt")
                for t in range(NT):
                    last = mm(ps[0:T, 4, t * HD2:(t + 1) * HD2], big2[0:T, 3, t * T:(t + 1) * T], qkv[:, t, 128:192],
                              start=True, stop=True)
                last.then_inc(pe_step, 1)

                def turn_mixed(t):
                    after(pe, "dve", ph, f"mix{t}")
                    for half in range(2):
                        if t >= 2:
                            after(pe, "act", ph, f"m{t - 2}{'ab'[half]}")
                        for c in range(4):
                            src = mixed[t % 2][:, (4 * half + c) * P:(4 * half + c + 1) * P]
                            last = nc.tensor.transpose(ps[:, 2 * (t % 2) + half, c * T:(c + 1) * T], src, ident[0:T, 0:T])
                        last.then_inc(pe_step, 1)

                turn_mixed(0)
                for t in range(NT):
                    if t + 1 < NT:
                        turn_mixed(t + 1)
                    after(pe, "act", ph, f"m{t}b")
                    for c in range(EP):
                        last = mm(ps[0:T, 5, t * D:(t + 1) * D], mixed_t[t % 2][c // 4][:, (c % 4) * T:(c % 4 + 1) * T],
                                  weights[:, 3072 + c * D:3072 + (c + 1) * D], start=c == 0, stop=c == EP - 1)
                    last.then_inc(pe_step, 1)

            def wait_evacuated(item):
                kind, g, i = item
                if kind == "K":
                    pe.wait_ge(khi_done, KS * g + i + 1)
                    pe.wait_ge(klo_done, KS * g + i + 1)
                elif kind == "V":
                    pe.wait_ge(v_done, 3 * g + i + 1)
                elif kind == "S":
                    pe.wait_ge(smax_done, CH * KS * g + i + 1)
                elif kind == "D":
                    pe.wait_ge(rden_done, g + 1)
                else:
                    pe.wait_ge(mrow_done, 2 * g + i + 1)

            def side(item):
                kind, g, i = item
                l, bk = g // B, bank(item)
                if place[item] >= N_AUX:
                    wait_evacuated(items[place[item] - N_AUX])
                if kind == "K":
                    if i == 0:
                        pe.wait_ge(ctx_in[g % 3], 16 * (g // 3 + 1))
                    last = mm(ps[:, bk, 0:KP], kvw[:, l, 0:D], ctxT[:, g % 3, i * KP:(i + 1) * KP], start=True, stop=True)
                elif kind == "V":
                    for j in range(4):
                        kt = 4 * i + j
                        last = mm(ps[0:KK, bk, j * D:(j + 1) * D], ctxT[:, g % 3, kt * KK:(kt + 1) * KK],
                                  kvw[:, l, D:2 * D], start=True, stop=True)
                elif kind == "S":
                    c, k = divmod(i, KS)
                    if i == 0:
                        pe.wait_ge(qn_done, g + 1)
                        if l in MASKED:
                            pe.wait_ge(maskq_done, masks_before(g))
                    cols = slice(c * P, (c + 1) * P)
                    q2 = qn[:, g % 2, :, :].rearrange("p h s -> p (h s)")
                    masked = l in MASKED
                    last = mm(ps[:, bk, 0:KP], q2[:, cols], khi[:, g % 2, k * KP:(k + 1) * KP], start=True, stop=not masked)
                    if masked:
                        last = mm(ps[:, bk, 0:KP], hot[:, cols], mask_q[:, g % 2, k * KP:(k + 1) * KP], start=False, stop=True)
                elif kind == "D":
                    pe.wait_ge(oc_done, g + 1)
                    last = mm(ps[:, bk, 0:2 * S], perm, oc[:, :, :].rearrange("p r s -> p (r s)"), start=True, stop=True)
                else:
                    if i == 0:
                        pe.wait_ge(mx_done, g + 1)
                    for j, c in enumerate(range(4 * i, min(4 * i + 4, CH))):
                        last = mm(ps[0:1, bk, j * P:(j + 1) * P], mx[:, g % 2, c:c + 1], ident, start=True, stop=True)
                last.then_inc(aux_filled, 1)

            def scores(g, kt):
                n = g * KT + kt
                if kt == 0:
                    pe.wait_ge(kq_in[g % 2], 16 * 12 * (g // 2 + 1))
                    pe.wait_ge(qb_done, g + 1)
                    pe.wait_ge(mrow_done, 2 * (g + 1))
                if n >= 2:
                    pe.wait_ge(exp_done, n - 1)
                masked = g // B in MASKED
                for quad in range(QUADS):
                    dst = ps[:, 2 * (kt % 2) + quad // 2, (quad % 2) * 224:(quad % 2 + 1) * 224]
                    last = mm(dst, kq[:, g % 2, quad, kt * KK:kt * KK + P],
                              qb[:, g % 2, quad, :, :].rearrange("p h s -> p (h s)"), start=True, stop=not masked)
                    if masked:
                        mt = mask_t[:, g % B, kt, :].unsqueeze(1).broadcast_to([P, HQ, S])
                        last = mm(dst.rearrange("p (h s) -> p h s", s=S), id_mask[:, :], mt, start=False, stop=True)
                last.then_inc(scores_done, 1)

            def values(g, kt, r):
                n = g * KT + kt
                if kt % 4 == 0 and r == 0:
                    pe.wait_ge(v_done, 3 * g + kt // 4 + 1)
                if kt == 0 and r == 0 and g:
                    pe.wait_ge(oc_done, g)
                if r == 0:
                    pe.wait_ge(exp_done, n + 1)
                for j in range(4):
                    t8 = 4 * r + j
                    last = mm(ps[32 * j:32 * j + 32, BANK_PV, r * T:(r + 1) * T],
                              v_aug[0:KK, g % 2, kt, t8, :], probs[0:KK, kt % 2, t8 * T:(t8 + 1) * T],
                              start=(kt == 0 and r == 0), stop=(kt == KT - 1), skip_group_check=True)
                if r:
                    last.then_inc(pv_done, 1)

            def attention(l):
                for g in range(l * B, (l + 1) * B):
                    if g % B == 0:
                        for item in head_items(g):
                            side(item)
                        scores(g, 0)
                    for kt, slot in enumerate(aux_slots(g)):
                        for where, item in slot:
                            if where == BEFORE:
                                side(item)
                        if kt + 1 < KT:
                            scores(g, kt + 1)
                        elif (g + 1) % B:
                            scores(g + 1, 0)
                        for where, item in slot:
                            if where == BETWEEN:
                                side(item)
                        values(g, kt, 0)
                        for where, item in slot:
                            if where == HALFWAY:
                                side(item)
                        values(g, kt, 1)
                side(("D", (l + 1) * B - 1, 0))

            pe.wait_ge(kvw_in, 32)
            for item in FIRST_ITEMS:
                side(item)
            pe.wait_ge(const_in, 16 * N_CONST)
            pe.wait_ge(consts_ready, 1)
            pe.wait_ge(pool_ready, N_FILLS)
            src_of_turn = turn_sources()
            for ph in program_order():
                kind, n = ph
                if kind == "turn":
                    src, before = src_of_turn[n]
                    after(pe, "dve", before, "add" if before[0] == "affine" else "norm")
                    for t in range(NT):
                        last = nc.tensor.transpose(ps[:, 0, t * T:(t + 1) * T], (y if src == "y" else z)[:, t, :], ident[0:T, 0:T])
                    last.then_inc(pe_step, 1)
                elif kind == "count":
                    pe.wait_ge(consts_ready, 1)
                    pe.wait_ge(maskt_done, MASKED.index(n) + 1)
                    after(pe, "dve", ("moe", n - 1), "b2")
                    for kt in range(KT):
                        last = mm(ps[:, 5, 0:TOK].rearrange("p (b s) -> p b s", s=S), ones_b[0:KK, :], mask_t[0:KK, :, kt, :], start=kt == 0, stop=kt == KT - 1)
                    last.then_inc(pe_step, 1)
                elif kind == "q":
                    pe.wait_ge(xw_in, 16 * (n + 1))
                    after(pe, "act", prior(ph, "turn"), "copied")
                    mm(ps[:, 4, 0:TOK], xw[:, 0:D], yT[:, :], start=True, stop=True).then_inc(pe_step, 1)
                    for quad in range(QUADS):
                        last = mm(ps[:, quad, 0:TOK], xw[:, D * (1 + quad):D * (2 + quad)], yT[:, :], start=True, stop=True)
                    last.then_inc(pe_step, 1)
                    attention(n)
                elif kind == "out":
                    after(pe, "dve", ph, "biased")
                    for t in range(NT):
                        for r in range(2):
                            last = mm(ps[0:T, 3, t * D:(t + 1) * D], o_all[:, r, t * T:(t + 1) * T],
                                      xw[:, D * (5 + r):D * (6 + r)], start=r == 0, stop=r == 1)
                    last.then_inc(pe_step, 1)
                elif kind == "moe":
                    after(pe, "act", prior(ph, "turn"), "copied")
                    rT = yT
                    if n == 2:
                        mm(ps[:, 1, 0:TOK], rw1[:, :], yT[:, :], start=True, stop=True).then_inc(pe_step, 1)
                        after(pe, "act", ph, "r1")
                        rT = hbuf_T
                    for t in range(NT):
                        last = mm(ps[0:T, 5, t * E:(t + 1) * E], rT[:, t * T:(t + 1) * T], wg[:, n, :], start=True, stop=True)
                    last.then_inc(pe_step, 1)

                    def hidden(e):
                        pe.wait_ge(weights_in[e % SLOTS], weights_count(n, e))
                        for c in range(FC):
                            if e:
                                after(pe, "act", ph, f"h{e - 1}_{c}")
                            w = (e % SLOTS) * 1024 + c * P
                            last = mm(ps[:, c, 0:TOK], weights[:, w:w + P], yT[:, :], start=True, stop=True)
                        last.then_inc(pe_step, 1)

                    def down(e):
                        after(pe, "act", ph, f"h{e}_{FC - 1}")
                        if e >= 2:
                            after(pe, "dve", ph, f"acc{e - 2}")
                        else:
                            after(pe, "dve", ph, "logits")
                        hT = (big0, big1)[e % 2]
                        for t in range(NT):
                            for c in range(FC):
                                w = (e % SLOTS) * 1024 + F + c * D
                                last = mm(ps[0:T, 4 + e % 2, t * D:(t + 1) * D], hT[:, c, t * T:(t + 1) * T],
                                          weights[:, w:w + D], start=c == 0, stop=c == FC - 1)
                        last.then_inc(pe_step, 1)

                    hidden(0)
                    for e in range(E):
                        if e + 1 < E:
                            hidden(e + 1)
                        down(e)
                    after(pe, "dve", ph, "W")
                    after(pe, "act", ph, f"h{E - 1}_{FC - 1}")
                    for t in range(NT):
                        last = nc.tensor.transpose(ps[0:E, 0, t * T:(t + 1) * T], sm[:, 8, t * E:(t + 1) * E], ident[0:T, 0:T])
                    last.then_inc(pe_step, 1)
                    after(pe, "act", ph, "w_copied")
                    after(pe, "dve", ph, f"acc{E - 2}")
                    for t in range(NT):
                        last = mm(ps[0:T, 4, t * D:(t + 1) * D], keep[0:E, t * T:(t + 1) * T], b2[:, n, :], start=True, stop=True)
                    last.then_inc(pe_step, 1)
                elif kind == "self":
                    after(pe, "act", prior(ph, "turn"), "copied")
                    mm(ps[:, 4, 0:TOK], fw[:, 0:D], yT[:, :], start=True, stop=True)
                    mm(ps[:, 5, 0:TOK], fw[:, D:2 * D], yT[:, :], start=True, stop=True).then_inc(pe_step, 1)
                    for t in range(NT):
                        last = mm(ps[0:T, 3, t * D:(t + 1) * D], yT[:, t * T:(t + 1) * T], fw[:, 2 * D:3 * D], start=True, stop=True)
                    last.then_inc(pe_step, 1)
                    def self_scores(t):
                        after(pe, "pool", ph, f"kb{t}")
                        after(pe, "dve", ph, f"shift{t - 1}" if t else "v")
                        for c in range(4):
                            mm(ps[0:T, c, 0:448], qnf[:, t * T:(t + 1) * T], big3[:, c, :], start=True, stop=False)
                            last = mm(ps[0:T, c, 0:448].rearrange("p (h k) -> p h k", k=T), id_b[0:T, 0:T],
                                      blk_b[0:T, :].unsqueeze(1).broadcast_to([T, 4, T]), start=False, stop=True)
                        last.then_inc(pe_step, 1)

                    self_scores(0)
                    for t in range(NT):
                        if t + 1 < NT:
                            self_scores(t + 1)
                        after(pe, "act", ph, f"exp{t}")
                        for c in range(4):
                            i = 4 * t + c
                            if i >= 3:
                                after(pe, "act", ph, f"pt{(i - 3) // 4}_{(i - 3) % 4}")
                            for j in range(4):
                                last = nc.tensor.transpose(ps[0:T, 4 + i % 3, j * T:(j + 1) * T],
                                                           (big0, big1)[t % 2][0:T, c, j * T:(j + 1) * T], ident[0:T, 0:T])
                            last.then_inc(pe_step, 1)
                        if t:
                            after(pe, "dve", ph, f"o{t - 1}")
                        for h in range(H):
                            if h % 4 == 0:
                                after(pe, "act", ph, f"pt{t}_{h // 4}")
                            last = mm(ps[0:T, 7, h * 9:(h + 1) * 9], big2[0:T, h // 4, (h % 4) * T:(h % 4 + 1) * T],
                                      v_self[:, t, h, :], start=True, stop=True)
                        last.then_inc(pe_step, 1)
                    after(pe, "dve", ph, f"o{NT - 1}")
                    for t in range(NT):
                        last = nc.tensor.transpose(ps[:, 0, t * T:(t + 1) * T], hbuf[:, t, :], ident[0:T, 0:T])
                    last.then_inc(pe_step, 1)
                    after(pe, "act", ph, "o_copied")
                    for t in range(NT):
                        last = mm(ps[0:T, 3, t * D:(t + 1) * D], yT[:, t * T:(t + 1) * T], fw[:, 3 * D:4 * D], start=True, stop=True)
                    last.then_inc(pe_step, 1)
                elif kind == "gated":
                    gated_pe(pe, ph)

        @block.scalar
        def _(act):
            A = nc.scalar.activation

            def side(item):
                kind, g, i = item
                bk = bank(item)
                if kind in "SD":
                    return
                act.wait_ge(aux_filled, place[item] + 1)
                if kind == "K":
                    if g >= 2 and i == 0:
                        act.wait_ge(kq_in[g % 2], 16 * 12 * (g // 2))
                    A(khi[:, g % 2, i * KP:(i + 1) * KP], ps[:, bk, 0:KP], ACT.Identity,
                      bias=xb[:, g // B, 0:1]).then_inc(khi_done, 1)
                elif kind == "V":
                    if g >= 2 and i == 0:
                        act.wait_ge(pv_done, KT * (g - 1))
                    dst = v_aug[0:KK, g % 2, 4 * i:4 * i + 4, :, 0:16].rearrange("p k t c -> p (k t) c")
                    A(dst, ps[0:KK, bk, :].rearrange("p (k c) -> p k c", c=16), ACT.Copy).then_inc(v_done, 1)
                else:
                    n = 512 if i == 0 else HC - 512
                    row = qb[96:97, g % 2, :, :, :].rearrange("p a h s -> p (a h s)")
                    if i == 0 and g >= 2:
                        act.wait_ge(scores_done, KT * (g - 1))
                    A(row[:, i * 512:i * 512 + n], ps[0:1, bk, 0:n], ACT.Copy, scale=-1.0).then_inc(mrow_done, 1)

            def attention(l):
                for g in range(l * B, (l + 1) * B):
                    if g % B == 0:
                        for item in head_items(g):
                            side(item)
                    for kt, slot in enumerate(aux_slots(g)):
                        n = g * KT + kt
                        act.wait_ge(scores_done, n + 1)
                        if n >= 2:
                            act.wait_ge(pv_done, n - 1)
                        A(probs[0:KK, kt % 2, :].rearrange("p (a c) -> p a c", a=2),
                          ps[0:KK, 2 * (kt % 2):2 * (kt % 2) + 2, 0:448], ACT.Exp).then_inc(exp_done, 1)
                        for _, item in slot:
                            side(item)

            act.wait_ge(kvw_in, 32)
            act.wait_ge(pool_ready, N_FILLS)
            for item in FIRST_ITEMS:
                side(item)
            for ph in program_order():
                kind, n = ph
                if kind == "turn":
                    after(act, "pe", ph, "turned")
                    A(yT[:, :], ps[:, 0, 0:TOK], ACT.Copy).then_inc(act_step, 1)
                elif kind == "q":
                    after(act, "dve", ph, "kept" if n == 2 else "scaled")
                    A(qv[0:64, :, :], qs[0:64, :, :], ACT.Copy).then_inc(act_step, 1)
                    A(qv_hi[64:96, :, :], qs[64:96, :, :], ACT.Copy).then_inc(act_step, 1)
                    attention(n)
                elif kind == "moe":
                    func = (ACT.Gelu_apprx_tanh, ACT.Relu, ACT.Silu)[n]
                    if n == 2:
                        act.wait_ge(const_in, 16 * N_CONST)
                        after(act, "pe", ph, "r1")
                        A(hbuf_T[:, :], ps[:, 1, 0:TOK], ACT.Silu, bias=rb1[:, 0:1]).then_inc(act_step, 1)
                        after(act, "dve", ph, "gap")
                        A(s1[:, 8, :], s1[:, 7, :], ACT.Exp).then_inc(act_step, 1)
                    else:
                        after(act, "dve", ph, "shift")
                        A(sm[:, 2, 0:32], sm[:, 1, 0:32], ACT.Exp).then_inc(act_step, 1)
                    act.wait_ge(const_in, 16 * N_CONST)
                    for e in range(E):
                        after(act, "pe", ph, f"h{e}")
                        if e >= 2:
                            after(act, "pe", ph, f"y{e - 2}")
                        for c in range(FC):
                            A((big0, big1)[e % 2][:, c, :], ps[:, c, 0:TOK], func, bias=b1[:, n, e, c:c + 1])\
                                .then_inc(act_step, 1)
                    after(act, "pe", ph, "w_turned")
                    A(keep[0:E, :], ps[0:E, 0, 0:TOK], ACT.Copy).then_inc(act_step, 1)
                elif kind == "self":
                    for t in range(NT):
                        after(act, "dve", ph, f"shift{t}")
                        big = (big0, big1)[t % 2]
                        A(big[0:T, :, :], big[0:T, :, :], ACT.Exp).then_inc(act_step, 1)
                        if t:
                            after(act, "pe", ph, f"o{t - 1}")
                        for c in range(4):
                            after(act, "pe", ph, f"t{t}_{c}")
                            A(big2[0:T, c, :], ps[0:T, 4 + (4 * t + c) % 3, 0:448], ACT.Copy).then_inc(act_step, 1)
                    after(act, "pe", ph, "o_turned")
                    A(yT[:, :], ps[:, 0, 0:TOK], ACT.Copy).then_inc(act_step, 1)
                elif kind == "gated":
                    A(sm[:, 0, 0:E2], rows[:, R_GATE, 0:E2], ACT.Exp, scale=-1.0).then_inc(act_step, 1)
                    after(act, "dve", ph, "shift")
                    A(sm[:, 9, :], sm[:, 8, :], ACT.Exp).then_inc(act_step, 1)
                    after(act, "pe", ph, "qk_turned")
                    A(big2[0:HD2, 0:2, :], ps[0:HD2, 0:2, 0:TOK], ACT.Copy).then_inc(act_step, 1)
                    after(act, "dve", ph, "sshift")
                    A(big2[0:T, 2, :], s_buf, ACT.Exp).then_inc(act_step, 1)
                    after(act, "pe", ph, "t")
                    A(big2[0:T, 3, :], ps[0:T, 3, 0:TOK], ACT.Copy).then_inc(act_step, 1)
                    for t in range(NT):
                        for half in range(2):
                            after(act, "pe", ph, f"m{t}{'ab'[half]}")
                            if t >= 2:
                                after(act, "pe", ph, f"f{t - 2}")
                            A(mixed_t[t % 2][half], ps[:, 2 * (t % 2) + half, 0:TOK], ACT.Copy).then_inc(act_step, 1)

        @block.vector
        def _(dve):
            V = nc.vector
            TT, TS, STT = V.tensor_tensor, V.tensor_scalar, V.scalar_tensor_tensor

            def self_dve(dve, ph):
                V = nc.vector
                TT, TS, STT = V.tensor_tensor, V.tensor_scalar, V.scalar_tensor_tensor
                after(dve, "pe", ph, "qk")
                TS(qnf[:, :], ps[:, 4, 0:TOK], fb[:, 0:1], float(DH) ** -0.5, ALU.add, ALU.mult).then_inc(dve_step, 1)
                TS(keep[:, :], ps[:, 5, 0:TOK], fb[:, 1:2], None, ALU.add).then_inc(dve_step, 1)
                after(dve, "pe", ph, "v")
                V.memset(v_self[:, :, :, DH], 1.0)
                TT(v_self[:, :, :, 0:DH], ps[0:T, 3, :].rearrange("p (t h d) -> p t h d", h=H, d=DH),
                   rows[:, R_FBV, :].rearrange("p (h d) -> p h d", d=DH).unsqueeze(1).broadcast_to([T, NT, H, DH]), ALU.add)\
                    .then_inc(dve_step, 1)

                def shift(t):
                    after(dve, "pe", ph, f"s{t}")
                    s4 = ps[0:T, 0:4, 0:448].rearrange("p a (h k) -> p a h k", k=T)
                    V.reduce_max(sumh[:, t % 2, :].rearrange("p (a h) -> p a h", a=4), s4, AX.X).then_inc(dve_step, 1)
                    after(dve, "dve", ph, f"max{t}")
                    if t >= 2:
                        after(dve, "pe", ph, f"t{t - 2}_3")
                    for c in range(4):
                        last = TT((big0, big1)[t % 2][0:T, c, :].rearrange("p (h k) -> p h k", k=T), s4[:, c, :, :],
                                  sumh[:, t % 2, 4 * c:4 * c + 4].unsqueeze(2).broadcast_to([T, 4, T]), ALU.subtract)
                    last.then_inc(dve_step, 1)

                shift(0)
                for t in range(NT):
                    if t + 1 < NT:
                        shift(t + 1)
                    after(dve, "pe", ph, f"o{t}")
                    o = ps[0:T, 7, 0:H * (DH + 1)].rearrange("p (h d) -> p h d", d=DH + 1)
                    V.reciprocal(sumh[:, 2, :], o[:, :, DH]).then_inc(dve_step, 1)
                    after(dve, "dve", ph, f"recip{t}")
                    TT(hbuf[:, t, :].rearrange("p (h d) -> p h d", d=DH), o[:, :, 0:DH],
                       sumh[:, 2, :].unsqueeze(2).broadcast_to([T, H, DH]), ALU.mult).then_inc(dve_step, 1)
                TT(y[:, :, :], y[:, :, :], rows[:, R_FBO, :].unsqueeze(1).broadcast_to([T, NT, D]), ALU.add).then_inc(dve_step, 1)
                after(dve, "dve", ph, "hb")
                after(dve, "pe", ph, "proj")
                TT(hbuf[:, :, :], ps[0:T, 3, :].rearrange("p (t d) -> p t d", d=D), y[:, :, :], ALU.add).then_inc(dve_step, 1)
                after(dve, "dve", ph, "h")

            def gated_dve(dve, ph, top2):
                V = nc.vector
                TT, TS, STT = V.tensor_tensor, V.tensor_scalar, V.scalar_tensor_tensor

                def did(step):
                    after(dve, "dve", ph, step)

                def v(i):
                    return sm[:, i, :].rearrange("p (t e) -> p t e", e=E2)

                def one(i):
                    return s1[:, i, :].unsqueeze(2).broadcast_to([T, NT, E2])

                TT(sim2[:, 0, :], sim[:, :], sim[:, :], ALU.mult).then_inc(dve_step, 1)
                TT(z[:, :, :], y[:, :, :], y[:, :, :], ALU.mult).then_inc(dve_step, 1)
                did("y2")
                V.reduce_sum(s1[:, 10, :], z[:, :, :], AX.X).then_inc(dve_step, 1)
                did("y2_sum")
                TS(s1[:, 0, :], s1[:, 10, :], 1e-24, None, ALU.max).then_inc(dve_step, 1)
                after(dve, "pe", ph, "sim2")
                TS(sim2[:, 1, :], ps[:, 1, 0:E2], 1e-24, None, ALU.max).then_inc(dve_step, 1)
                after(dve, "pool", ph, "sim_norm")
                TT(sim2[:, 3, :], sim[:, :], sim2[:, 2, :], ALU.mult).then_inc(dve_step, 1)
                after(dve, "act", ph, "gate_exp")
                TS(sm[:, 1, 0:E2], sm[:, 0, 0:E2], 1.0, None, ALU.add).then_inc(dve_step, 1)
                did("gate1")
                V.reciprocal(sm[:, 2, 0:E2], sm[:, 1, 0:E2]).then_inc(dve_step, 1)
                after(dve, "pe", ph, "logits")
                after(dve, "pool", ph, "y_norm")
                did("gate")
                TT(v(0), ps[0:T, 2, 0:NT * E2].rearrange("p (t e) -> p t e", e=E2), one(1), ALU.mult).then_inc(dve_step, 1)
                did("cos")
                TT(v(1), v(0), sm[:, 2, 0:E2].unsqueeze(1).broadcast_to([T, NT, E2]), ALU.subtract).then_inc(dve_step, 1)
                did("logits")
                TS(v(10), v(1), 0.0, None, ALU.is_gt).then_inc(dve_step, 1)
                did("pos")
                V.reduce_max(s1[:, 6, :], v(10), AX.X).then_inc(dve_step, 1)
                TS(v(11), v(1), 0.0, None, ALU.max).then_inc(dve_step, 1)
                did("gated")
                V.reduce_max(s1[:, 7, :], v(11), AX.X).then_inc(dve_step, 1)
                top2(ph, v(1), E2)
                TT(v(12), v(4), v(7), ALU.add).then_inc(dve_step, 1)
                TS(s1[:, 8, :], s1[:, 6, :], -1.0, 1.0, ALU.mult, ALU.add).then_inc(dve_step, 1)
                did("none")
                TT(v(13), v(12), one(8), ALU.mult).then_inc(dve_step, 1)
                did("fallback")
                TT(v(14), v(13), v(10), ALU.add).then_inc(dve_step, 1)
                TT(v(8), v(11), one(7), ALU.subtract).then_inc(dve_step, 1)
                after(dve, "act", ph, "exp")
                TT(v(12), v(9), v(14), ALU.mult).then_inc(dve_step, 1)
                did("em")
                V.reduce_sum(s1[:, 9, :], v(12), AX.X).then_inc(dve_step, 1)
                did("sum")
                V.reciprocal(s1[:, 10, :], s1[:, 9, :]).then_inc(dve_step, 1)
                did("recip")
                TT(v(15), v(12), one(10), ALU.mult).then_inc(dve_step, 1)
                did("rw")
                for p in range(EP):
                    for k in range(2):
                        for t in range(NT):
                            w = sm[:, 15, t * E2 + 2 * p + k:t * E2 + 2 * p + k + 1]
                            part = ps[0:T, 4 * (p % 2) + t, 192 * k:192 * (k + 1)]
                            after(dve, "pe", ph, f"p{p}_{t}")
                            if p == 0 and k == 0:
                                TS(qkv[:, t, :], part, w, None, ALU.mult).then_inc(dve_step, 1)
                            else:
                                did(f"a{p}_{t}" if k else f"b{p - 1}_{t}")
                                STT(qkv[:, t, :], part, w, qkv[:, t, :], ALU.mult, ALU.add).then_inc(dve_step, 1)
                after(dve, "pe", ph, "s")
                s3 = s_buf.rearrange("p (t k) -> p t k", t=NT)
                STT(s3, ps[0:T, 2, 0:TOK].rearrange("p (t k) -> p t k", t=NT), float(HD2) ** -0.5,
                    cst[0:T, C_CAU:C_CAU + T].unsqueeze(1).broadcast_to([T, NT, T]), ALU.mult, ALU.add).then_inc(dve_step, 1)
                did("masked")
                V.reduce_max(s1[:, 2, :], s3, AX.X).then_inc(dve_step, 1)
                did("smax")
                TT(s3, s3, s1[:, 2, :].unsqueeze(2).broadcast_to([T, NT, T]), ALU.subtract).then_inc(dve_step, 1)
                after(dve, "act", ph, "s_exp")
                V.reduce_sum(s1[:, 3, :], big2[0:T, 2, :].rearrange("p (t k) -> p t k", t=NT), AX.X).then_inc(dve_step, 1)
                did("ssum")
                V.reciprocal(s1[:, 4, :], s1[:, 3, :]).then_inc(dve_step, 1)
                did("srecip")
                after(dve, "pe", ph, "o")
                TT(hbuf[:, :, 0:HD2], ps[0:T, 4, 0:NT * HD2].rearrange("p (t d) -> p t d", d=HD2),
                   s1[:, 4, :].unsqueeze(2).broadcast_to([T, NT, HD2]), ALU.mult).then_inc(dve_step, 1)
                did("o")
                for t in range(NT):
                    if t >= 2:
                        after(dve, "pe", ph, f"m{t - 2}b")
                    TT(mixed[t % 2].rearrange("p (e d) -> p e d", d=HD2), hbuf[:, t, 0:HD2].unsqueeze(1).broadcast_to([T, E2, HD2]),
                       sm[:, 15, t * E2:(t + 1) * E2].unsqueeze(2).broadcast_to([T, E2, HD2]), ALU.mult).then_inc(dve_step, 1)
                after(dve, "pe", ph, f"f{NT - 1}")
                TT(x[:, :, :], ps[0:T, 5, :].rearrange("p (t d) -> p t d", d=D), x[:, :, :], ALU.add).then_inc(dve_step, 1)
                did("added")

            def side(item):
                kind, g, i = item
                bk = bank(item)
                if kind == "K":
                    dve.wait_ge(khi_done, KS * g + i + 1)
                    if g >= 2 and i == 0:
                        dve.wait_ge(kq_in[g % 2], 16 * 12 * (g // 2))
                    STT(klo[:, g % 2, i * KP:(i + 1) * KP], ps[:, bk, 0:KP], xb[:, g // B, 0:1],
                        khi[:, g % 2, i * KP:(i + 1) * KP], ALU.add, ALU.subtract).then_inc(klo_done, 1)
                elif kind == "D":
                    dve.wait_ge(aux_filled, place[item] + 1)
                    V.reciprocal(rden[:, :, :].rearrange("p r s -> p (r s)"), ps[:, bk, 0:2 * S]).then_inc(rden_done, 1)
                    dve.wait_ge(rden_done, g + 1)
                    TT(o_all[:, :, (g % B) * S:(g % B + 1) * S], oc[:, :, :], rden[:, :, :], ALU.mult).then_inc(o_done, 1)
                elif kind == "S":
                    c, k = divmod(i, KS)
                    dve.wait_ge(aux_filled, place[item] + 1)
                    V.reduce_max(mx_part[:, g % 2, c, k:k + 1], ps[:, bk, 0:KP], AX.X).then_inc(smax_done, 1)
                    if i == CH * KS - 1:
                        dve.wait_ge(smax_done, CH * KS * (g + 1))
                        V.reduce_max(mx[:, g % 2, 0:CH], mx_part[:, g % 2, :, :], AX.X).then_inc(mx_done, 1)

            def mask_by_query(g):
                dve.wait_ge(mask_in[g % 2], 16 * ((masks_before(g) + 1) // 2))
                if g >= 2:
                    dve.wait_ge(smax_done, CH * KS * (g - 1))
                if g // B == 1:
                    V.tensor_copy(mask_q[0:S, g % 2, :], mask_u8[:, g % 2, :]).then_inc(maskq_done, 1)
                else:
                    STT(mask_q[0:S, g % 2, :], tri_u8[:, :], 0.5, mask_u8[:, g % 2, :], ALU.is_lt, ALU.is_ge)\
                        .then_inc(maskq_done, 1)

            def masks_by_key(l):
                for b in range(B):
                    if l == 1:
                        last = V.tensor_copy(mask_t[0:KK, b, :, :], maskT_u8[0:KK, b, :, :])
                    else:
                        last = STT(mask_t[0:KK, b, :, :], triT_u8[0:KK, :, :], 0.5,
                                   padT_u8[0:KK, b, :].unsqueeze(2).broadcast_to([KK, KT, S]), ALU.is_lt, ALU.is_ge)
                last.then_inc(maskt_done, 1)

            def combine(g):
                dve.wait_ge(pv_done, KT * (g + 1))
                if g:
                    dve.wait_ge(o_done, g)
                pv = ps[:, BANK_PV, 0:2 * T].rearrange("p (r h s) -> p r h s", r=2, h=2)
                TS(oc_t[:, :, :], pv[:, :, 0, :], cst[:, C_SEL:C_SEL + 1], None, ALU.mult).then_inc(oc_half, 1)
                dve.wait_ge(oc_half, g + 1)
                STT(oc[:, :, :], pv[:, :, 1, :], cst[:, C_SEL + 1:C_SEL + 2], oc_t[:, :, :], ALU.mult, ALU.add)\
                    .then_inc(oc_done, 1)

            def attention(l):
                for g in range(l * B, (l + 1) * B):
                    if g % B == 0:
                        for item in head_items(g):
                            side(item)
                    for kt, slot in enumerate(aux_slots(g)):
                        for _, item in slot:
                            side(item)
                        if kt == KT - 1 and g + 2 < G and (g + 2) // B in MASKED:
                            mask_by_query(g + 2)
                    combine(g)
                side(("D", (l + 1) * B - 1, 0))

            def top2(ph, p, n_e):
                def v(i):
                    return sm[:, i, 0:NT * n_e].rearrange("p (t e) -> p t e", e=n_e)

                def one(i):
                    return s1[:, i, :].unsqueeze(2).broadcast_to([T, NT, n_e])

                rank = cst[0:T, C_RANK:C_RANK + n_e].unsqueeze(1).broadcast_to([T, NT, n_e])
                V.reduce_max(s1[:, 2, :], p, AX.X).then_inc(dve_step, 1)
                after(dve, "dve", ph, "v1")
                TT(v(3), p, one(2), ALU.is_equal).then_inc(dve_step, 1)
                after(dve, "dve", ph, "eq1")
                TT(v(5), v(3), rank, ALU.mult).then_inc(dve_step, 1)
                after(dve, "dve", ph, "sc1")
                V.reduce_max(s1[:, 3, :], v(5), AX.X).then_inc(dve_step, 1)
                after(dve, "dve", ph, "m1")
                TT(v(4), v(5), one(3), ALU.is_equal).then_inc(dve_step, 1)
                after(dve, "dve", ph, "oh1")
                STT(v(6), v(4), NEG, p, ALU.mult, ALU.add).then_inc(dve_step, 1)
                after(dve, "dve", ph, "p2")
                V.reduce_max(s1[:, 4, :], v(6), AX.X).then_inc(dve_step, 1)
                after(dve, "dve", ph, "v2")
                TT(v(3), v(6), one(4), ALU.is_equal).then_inc(dve_step, 1)
                after(dve, "dve", ph, "eq2")
                TT(v(5), v(3), rank, ALU.mult).then_inc(dve_step, 1)
                after(dve, "dve", ph, "sc2")
                V.reduce_max(s1[:, 5, :], v(5), AX.X).then_inc(dve_step, 1)
                after(dve, "dve", ph, "m2")
                TT(v(7), v(5), one(5), ALU.is_equal).then_inc(dve_step, 1)
                after(dve, "dve", ph, "oh2")

            def moe(ph, n):
                def v(i):
                    return sm[:, i, 0:NT * E].rearrange("p (t e) -> p t e", e=E)

                def one(i):
                    return s1[:, i, :].unsqueeze(2).broadcast_to([T, NT, E])

                def did(step):
                    after(dve, "dve", ph, step)

                lg = ps[0:T, 5, 0:NT * E].rearrange("p (t e) -> p t e", e=E)
                after(dve, "pe", ph, "gate")
                if n == 2:
                    TT(v(0), lg, rows[:, R_RB2, 0:E].unsqueeze(1).broadcast_to([T, NT, E]), ALU.add).then_inc(dve_step, 1)
                    did("logits")
                    top2(ph, v(0), E)
                    TT(s1[:, 7, :], s1[:, 4, :], s1[:, 2, :], ALU.subtract).then_inc(dve_step, 1)
                    after(dve, "act", ph, "exp")
                    TS(s1[:, 9, :], s1[:, 8, :], 1.0, None, ALU.add).then_inc(dve_step, 1)
                    did("plus")
                    V.reciprocal(s1[:, 6, :], s1[:, 9, :]).then_inc(dve_step, 1)
                    did("inv")
                    TT(s1[:, 1, :], s1[:, 8, :], s1[:, 6, :], ALU.mult).then_inc(dve_step, 1)
                    TT(v(9), v(4), one(6), ALU.mult).then_inc(dve_step, 1)
                    did("w1")
                    TT(v(10), v(7), one(1), ALU.mult).then_inc(dve_step, 1)
                    did("w2")
                    TT(v(8), v(9), v(10), ALU.add).then_inc(dve_step, 1)
                else:
                    V.tensor_copy(v(0), lg).then_inc(dve_step, 1)
                    did("logits")
                    V.reduce_max(s1[:, 0, :], v(0), AX.X).then_inc(dve_step, 1)
                    did("max")
                    TT(v(1), v(0), one(0), ALU.subtract).then_inc(dve_step, 1)
                    after(dve, "act", ph, "exp")
                    V.reduce_sum(s1[:, 1, :], v(2), AX.X).then_inc(dve_step, 1)
                    did("sum")
                    V.reciprocal(s1[:, 6, :], s1[:, 1, :]).then_inc(dve_step, 1)
                    did("recip")
                    TT(v(10), v(2), one(6), ALU.mult).then_inc(dve_step, 1)
                    did("probs")
                    top2(ph, v(10), E)
                    TT(v(9), v(4), v(7), ALU.add).then_inc(dve_step, 1)
                    STT(s1[:, 8, :], s1[:, 2, :], 1e-9 if n == 1 else 0.0, s1[:, 4, :], ALU.add, ALU.add).then_inc(dve_step, 1)
                    did("den")
                    V.reciprocal(s1[:, 9, :], s1[:, 8, :]).then_inc(dve_step, 1)
                    TT(v(11), v(9), v(10), ALU.mult).then_inc(dve_step, 1)
                    did("cp")
                    TT(v(8), v(11), one(9), ALU.mult).then_inc(dve_step, 1)
                did("W")
                if n != 1:
                    TT(x[:, :, :], x[:, :, :], (hbuf if n == 0 else y)[:, :, :], ALU.add).then_inc(dve_step, 1)
                    did("base")
                for e in range(E):
                    after(dve, "pe", ph, f"y{e}")
                    for t in range(NT):
                        last = STT(x[:, t, :], ps[0:T, 4 + e % 2, t * D:(t + 1) * D], sm[:, 8, t * E + e:t * E + e + 1],
                                   x[:, t, :], ALU.mult, ALU.add)
                    last.then_inc(dve_step, 1)
                    did(f"acc{e}")
                after(dve, "pe", ph, "b2")
                TT(x[:, :, :], ps[0:T, 4, :].rearrange("p (t d) -> p t d", d=D), x[:, :, :], ALU.add).then_inc(dve_step, 1)
                did("b2")

            V.memset(mask_q[:, :, :], 0.0)
            V.memset(mask_t[:, :, :, :], 0.0)
            V.memset(ones_b[:, :], 1.0)
            dve.wait_ge(kvw_in, 32)
            for item in FIRST_ITEMS:
                side(item)
            dve.wait_ge(const_in, 16 * N_CONST)
            V.tensor_copy(hot[:, :], hot_f)
            TS(id_mask[:, :], ident, MASK, None, ALU.mult)
            V.tensor_copy(id_b[:, :], ident)
            V.tensor_copy(blk_b[0:T, :], cst[0:T, C_BLK:C_BLK + T])
            V.tensor_copy(bm16[:, :], cst[:, C_BM:C_BM + H])
            V.tensor_copy(m4[:, :], cst[:, C_M4:C_M4 + HQ]).then_inc(consts_ready, 1)
            dve.wait_ge(consts_ready, 1)
            masks_by_key(1)
            dve.wait_ge(x_in, 16)

            for ph in program_order():
                kind, n = ph
                if kind == "ln":
                    src, dst = ln_io(n)
                    for t in range(NT):
                        last = V.bn_stats(st[:, t, :], src[:, t, :])
                    last.then_inc(dve_step, 1)
                    after(dve, "dve", ph, "stats")
                    for t in range(NT):
                        last = V.bn_aggr(mv[:, t, :], st[:, t, :])
                    last.then_inc(dve_step, 1)
                    after(dve, "dve", ph, "aggr")
                    TS(ve[:, :], mv[:, :, 1], 1e-5, None, ALU.add).then_inc(dve_step, 1)
                    after(dve, "pool", ph, "rstd")
                    for t in range(NT):
                        last = TS(dst[:, t, :], src[:, t, :], mv[:, t, 0:1], rstd[:, t:t + 1], ALU.subtract, ALU.mult)
                    last.then_inc(dve_step, 1)
                    after(dve, "dve", ph, "norm")
                elif kind == "affine":
                    w, b = (R_LN1W, R_LN1B) if n == 0 else (R_LN2W, R_LN2B)
                    TT(z[:, :, :], z[:, :, :], rows[:, w, :].unsqueeze(1).broadcast_to([T, NT, D]), ALU.mult).then_inc(dve_step, 1)
                    after(dve, "dve", ph, "mul")
                    TT(z[:, :, :], z[:, :, :], rows[:, b, :].unsqueeze(1).broadcast_to([T, NT, D]), ALU.add).then_inc(dve_step, 1)
                elif kind == "count":
                    after(dve, "pe", ph, "count")
                    TS(keep[:, :], ps[:, 5, 0:TOK], KV - 0.5, None, ALU.is_lt).then_inc(dve_step, 1)
                elif kind == "q":
                    after(dve, "pe", ph, "qn")
                    scale = float(D) ** -0.5 if n == 2 else float(DH) ** -0.5
                    if n == 2:
                        TS(qnf[:, :], ps[:, 4, 0:TOK], xb[:, n, 1:2], scale, ALU.add, ALU.mult).then_inc(dve_step, 1)
                        after(dve, "dve", ph, "qnf")
                        TT(qn16[:, :], qnf[:, :], keep[:, :], ALU.mult).then_inc(dve_step, 1)
                    else:
                        TS(qn16[:, :], ps[:, 4, 0:TOK], xb[:, n, 1:2], scale, ALU.add, ALU.mult).then_inc(dve_step, 1)
                    after(dve, "pe", ph, "q")
                    for quad in range(QUADS):
                        last = TS(qs[:, quad, :], ps[:, quad, 0:TOK], xb[:, n, 2 + quad:3 + quad], scale, ALU.add, ALU.mult)
                    last.then_inc(dve_step, 1)
                    if n == 2:
                        after(dve, "dve", ph, "scaled")
                        TT(qs[:, :, :], qs[:, :, :], keep[:, :].unsqueeze(1).broadcast_to([P, 4, TOK]), ALU.mult).then_inc(dve_step, 1)
                    after(dve, "act", ph, "hi_lo")
                    TT(qv[64:96, :, :], qs[64:96, :, :], qv_hi[64:96, :, :], ALU.subtract).then_inc(dve_step, 1)
                    attention(n)
                    if n == 1:
                        masks_by_key(2)
                elif kind == "out":
                    dve.wait_ge(o_done, B * (n + 1))
                    if n == 1:
                        TT(o_all[:, :, :], o_all[:, :, :], keep[:, :].unsqueeze(1).broadcast_to([P, 2, TOK]), ALU.mult).then_inc(dve_step, 1)
                    else:
                        TS(o_all[:, 0, :], o_all[:, 0, :], xb[:, n, 6:7], None, ALU.add)
                        TS(o_all[:, 1, :], o_all[:, 1, :], xb[:, n, 7:8], None, ALU.add).then_inc(dve_step, 1)
                    TT(x[:, :, :], x[:, :, :], rows[:, R_BO + n, :].unsqueeze(1).broadcast_to([T, NT, D]), ALU.add).then_inc(dve_step, 1)
                    after(dve, "dve", ph, "with_bo")
                    after(dve, "pe", ph, "projected")
                    TT(x[:, :, :], ps[0:T, 3, :].rearrange("p (t d) -> p t d", d=D), x[:, :, :], ALU.add).then_inc(dve_step, 1)
                    after(dve, "dve", ph, "added")
                elif kind == "moe":
                    moe(ph, n)
                elif kind == "self":
                    self_dve(dve, ph)
                elif kind == "gated":
                    gated_dve(dve, ph, top2)


def kernel(**inputs):
    from concourse.bass_utils import run_bass_kernel_spmd
    from concourse import bacc

    f = {k: np.asarray(v) for k, v in inputs.items()}
    f4 = np.float32

    def head_blocks(w):
        full = np.zeros((D, D), f4)
        for h in range(H):
            full[h * DH:(h + 1) * DH, h * DH:(h + 1) * DH] = w[h].T
        return full

    none = np.zeros(D, f4)
    layers = [
        (f["L0_xattn_Wq"], f["L0_xattn_Wk"], f["L0_xattn_Wv"], f["L0_xattn_Wo"],
         f["L0_xattn_bq"], f["L0_xattn_bk"], f["L0_xattn_bv"], f["L0_xattn_bo"]),
        (f["L1_xattn_W_Q"].T, f["L1_xattn_W_K"].T, f["L1_xattn_W_V"].T, f["L1_xattn_W_O"].T, none, none, none, none),
        (f["L2_xattn_Wq"].T, f["L2_xattn_Wk"].T, f["L2_xattn_Wv"].T, f["L2_xattn_Wo"].T,
         f["L2_xattn_bq"], f["L2_xattn_bk"], f["L2_xattn_bv"], f["L2_xattn_bo"]),
        (head_blocks(f["L3_xattn_wq"]), head_blocks(f["L3_xattn_wk"]), head_blocks(f["L3_xattn_wv"]), f["L3_xattn_wo"].T,
         f["L3_xattn_bq"].reshape(D), f["L3_xattn_bk"].reshape(D), f["L3_xattn_bv"].reshape(D), f["L3_xattn_bo"]),
    ]
    kvw = np.zeros((P, L, 256), f4)
    xw = np.zeros((L, P, 7 * D), f4)
    xb = np.zeros((P, L, 8), f4)
    rows = np.zeros((R_N, D), f4)
    for l, (wq, wk, wv, wo, bq, bk, bv, bo) in enumerate(layers):
        kvw[:, l, 0:D], kvw[:, l, D:] = wk, wv
        xw[l, :, 0:D] = wq
        xb[:, l, 0], xb[:, l, 1] = bk, bq
        for quad in range(QUADS):
            for blk in range(3):
                c = D * (1 + quad) + 32 * blk
                xw[l, :, c:c + 32] = wq[:, 32 * quad:32 * quad + 32]
                xb[32 * blk:32 * blk + 32, l, 2 + quad] = bq[32 * quad:32 * quad + 32]
        for t8 in range(8):
            r, j = divmod(t8, 4)
            xw[l, 32 * j:32 * j + 16, D * (5 + r):D * (6 + r)] = wo[16 * t8:16 * t8 + 16, :]
            xb[32 * j:32 * j + 16, l, 6 + r] = bv[16 * t8:16 * t8 + 16]
        rows[R_BO + l] = bo
    rows[R_LN1W], rows[R_LN1B] = f["L0_ffn_ln1_w"], f["L0_ffn_ln1_b"]
    rows[R_LN2W], rows[R_LN2B] = f["L0_ffn_ln2_w"], f["L0_ffn_ln2_b"]
    rows[R_FBO], rows[R_FBV] = f["L0_ffn_b_o"], f["L0_ffn_b_qkv"][2 * D:]
    rows[R_RB2, 0:E] = f["L3_ffn_rb2"]
    rows[R_GATE, 0:E2] = f["L2_ffn_gates"]

    p = np.arange(P)
    cst = np.zeros((P, C_W), f4)
    cst[:, C_ID:C_ID + P] = np.eye(P)
    for m in range(P):
        cst[m + 16 if m % 32 < 16 else m, C_PERM + m] = 1.0
    cst[:, C_BM:C_BM + H] = p[:, None] // DH == np.arange(H)
    cst[:, C_M4:C_M4 + HQ] = p[:, None] % 32 // DH == np.arange(HQ)
    cst[:, C_SEL:C_SEL + 2] = p[:, None] % 16 // DH == np.arange(2)
    q, k = np.arange(T)[:, None], np.arange(T)[None, :]
    cst[0:T, C_BLK:C_BLK + T] = np.where(q // S == k // S, 0.0, NEG)
    cst[0:T, C_CAU:C_CAU + T] = np.where((q // S == k // S) & (k <= q), 0.0, NEG)
    cst[:, C_RANK:C_RANK + E2] = E2 - np.arange(E2)
    cst[:, C_HOT:] = np.where(p[:, None] == np.tile(np.arange(S), H), MASK, 0.0)

    def by_key(m):
        m = m.reshape(m.shape[:-1] + (KT, KK))
        return np.moveaxis(m, -1, 0)

    mask = f["mask_BxSxS2_bf0"]
    tri = f["mask_SxS2_bk0"]
    pad = f["mask_BxS2_bk1"]

    def experts(w1, w2):
        w2 = w2.reshape(E, FC, P, D).transpose(0, 2, 1, 3).reshape(E, P, FC * D)
        return np.concatenate([w1, w2], axis=2)

    moe = np.concatenate([experts(f["L0_ffn_w1"], f["L0_ffn_w2"]),
                          experts(f["L1_ffn_w1"].transpose(0, 2, 1), f["L1_ffn_w2"].transpose(0, 2, 1)),
                          experts(f["L3_ffn_we1"], f["L3_ffn_we2"])])
    b1 = np.stack([f["L0_ffn_b1"], f["L1_ffn_b1"], f["L3_ffn_be1"]]).reshape(3, E, FC, P).transpose(3, 0, 1, 2)
    b2 = np.stack([f["L0_ffn_b2"], f["L1_ffn_b2"], f["L3_ffn_be2"]], axis=1)
    wg = np.stack([f["L0_ffn_w_gate"], f["L1_ffn_router_w"].T, f["L3_ffn_rw2"]], axis=1)
    qkv2 = np.concatenate([f["L2_ffn_q_proj"], f["L2_ffn_k_proj"], f["L2_ffn_v_proj"]], axis=2)
    arrays = {
        "x": f["x"].reshape(TOK, D), "ctxT": f["ctx_1024"].transpose(0, 2, 1), "kvw": kvw, "xw": xw, "xb": xb,
        "rows": rows, "cst": cst, "mask": mask.transpose(1, 0, 2), "pad": pad, "tri": tri,
        "maskT": by_key(mask).transpose(0, 1, 3, 2), "triT": by_key(tri).transpose(0, 2, 1), "padT": by_key(pad),
        "moe": moe, "b1": b1, "b2": b2, "wg": wg,
        "fw": np.concatenate([f["L0_ffn_w_qkv"], f["L0_ffn_w_o"]], axis=1),
        "fb": f["L0_ffn_b_qkv"][0:2 * D].reshape(2, D).T, "rw1": f["L3_ffn_rw1"], "rb1": f["L3_ffn_rb1"].reshape(D, 1),
        "sim": f["L2_ffn_sim_matrix"], "qkv2": qkv2.transpose(1, 0, 2).reshape(D, E2 * 192),
        "o2": f["L2_ffn_o_proj"].reshape(EP, P, D).transpose(1, 0, 2).reshape(P, EP * D),
    }
    nc = bacc.Bacc("TRN2", target_bir_lowering=False, num_devices=1)
    given, aps = {}, {}
    for name, arr in arrays.items():
        arr = np.ascontiguousarray(arr)
        given[f"in_{name}"] = arr
        aps[name] = nc.dram_tensor(f"in_{name}", arr.shape, mybir.dt.from_np(arr.dtype), kind="ExternalInput").ap()
    out = nc.dram_tensor("out", (TOK, D), F32, kind="ExternalOutput").ap()
    build(nc, aps, out)
    r = run_bass_kernel_spmd(nc, [given], core_ids=[0])
    return r.results[0]["out"].reshape(B, S, D)
```

```python
from contextlib import ExitStack

import concourse.bass as bass
from concourse import mybir
import numpy as np

F32 = mybir.dt.float32
F16 = mybir.dt.float16
BF16 = mybir.dt.bfloat16
U8 = mybir.dt.uint8
ALU = mybir.AluOpType
ACT = mybir.ActivationFunctionType
AX = mybir.AxisListType

P = 128
B, S, D = 8, 56, 128
H, DH = 16, 8
KV = 1500
KT = 12
KK = KV // KT
KPAD = 1504
L = 4
G = L * B
T = 2 * S
NT = B // 2
TOK = B * S
QUADS, HQ = 4, 4
HC = H * S
KS = 3
KP = KV // KS
E, F, FC = 8, 512, 4
SLOTS = 3
MASKED = (1, 2)
MASK = -32768.0
NEG = -(2.0 ** 100)
E2, HD2 = 16, 64

C_ID, C_PERM, C_BM, C_M4, C_SEL, C_BLK, C_CAU, C_RANK, C_W = 0, 128, 256, 272, 276, 278, 390, 502, 518
R_BO, R_FBO, R_FBV, R_RB2, R_GATE, R_N = 0, 4, 5, 6, 7, 8


BEFORE, BETWEEN, HALFWAY = range(3)


def chunk(g):
    return 2 * S if g // B in MASKED else P


def chunks(g):
    return HC // chunk(g)


def maxima_before(g):
    return sum(KS * chunks(k) for k in range(g))


def aux_slots(g):
    slots = [[] for _ in range(KT)]
    if (g + 1) % B:
        n, total = 0, KS * chunks(g + 1)
        for s in range(10):
            for where in (BEFORE, BETWEEN, HALFWAY) if s in (3, 5, 7, 4)[0:total - 20] else (BEFORE, HALFWAY):
                slots[s].append((where, ("S", g + 1, n)))
                n += 1
        assert n == total
        slots[10] += [(BETWEEN, ("M", g + 1, 0)), (BETWEEN, ("M", g + 1, 1))]
    if g % B:
        slots[1].append((BETWEEN, ("D", g - 1, 0)))
    if g % B:
        slots[2].append((BETWEEN, ("V", g, 1)))
        slots[5].append((BETWEEN, ("V", g, 2)))
    if (g + 1) % B:
        slots[11].append((BEFORE, ("V", g + 1, 0)))
    if g + 2 < G:
        for i, s in enumerate((6, 8, 10)):
            slots[s].append((BETWEEN if s < 10 else BEFORE, ("K", g + 2, i)))
    return [sorted(slot, key=lambda entry: entry[0]) for slot in slots]


def head_items(g):
    items = []
    for n in range(chunks(g) * KS):
        items.append(("S", g, n))
        if n in (6, 10, 14):
            items.append(("V", g, (n - 6) // 4))
    return items + [("M", g, 0), ("M", g, 1)]


FIRST_ITEMS = [("K", g, i) for g in range(2) for i in range(KS)]


def all_items():
    items = list(FIRST_ITEMS)
    for g in range(G):
        if g % B == 0:
            items += head_items(g)
        for slot in aux_slots(g):
            items += [item for _, item in slot]
        if g % B == B - 1:
            items.append(("D", g, 0))
    return items


TOP2 = ["v1", "eq1", "sc1", "m1", "oh1", "p2", "v2", "eq2", "sc2", "m2", "oh2"]
EP = E2 // 2
W_TURN = 2
AFFINE = (1, 2)
OWN_STATS = (0, 2)


def tiles(step):
    return [f"{step}{t}" for t in range(NT)]


def with_stats(step):
    steps = [step + "0"]
    for t in range(1, NT):
        steps += [f"{step}{t}", f"stats{t - 1}"]
    return steps + [f"stats{NT - 1}"]


def phase_steps(phase):
    kind, n = phase
    if kind == "ln":
        return {"dve": tiles("stats") * (n in OWN_STATS) + ["aggr", "var"] + tiles("norm"), "pool": ["rstd"]}
    if kind == "turn":
        return {"pe": ["turned"], "act": ["copied"]}
    if kind == "count":
        return {"pe": ["count"], "dve": ["keep"]}
    if kind == "q":
        return {"pe": ["qn", "q"], "act": ["scaled", "hi0", "hi_lo0", "hi1", "hi_lo1"],
                "pool": ["kept0"] * (n == 2) + ["lo0"] + ["kept1"] * (n == 2) + ["lo1"],
                "dve": ["sbias"] + ["qnf"] * (n == 2) + ["q16", "with_bo"]}
    if kind == "out":
        return {"dve": with_stats("added"), "pe": tiles("projected")}
    if kind == "moe":
        pe = ["r1"] * (n == 2) + ["gate", "h0"]
        for e in range(E - 1):
            pe += [f"h{e + 1}", f"y{e}"] + ["w_turned"] * (e == W_TURN) + ["b2"] * (e == W_TURN + 1)
        softmax = ["max", "shift", "sum", "recip", "probs"] * (n != 2)
        weigh = ["gap", "plus", "inv", "second", "w1", "w2", "W"] if n == 2 else ["chosen", "den", "inv", "cp", "W"]
        act = []
        for e in range(E):
            act += [f"h{e}_{c}" for c in range(FC)] + ["w_copied"] * (e == W_TURN + 1)
        acc = []
        for e in range(E - 1):
            acc += [f"acc{e}"] + ["b2"] * (e == W_TURN + 1)
        return {"pe": pe + tiles(f"y{E - 1}_"),
                "act": ["r1"] * (n == 2) + ["exp"] + act,
                "dve": ["logits"] + softmax + TOP2 + weigh + ["base"] * (n != 1) + acc
                + (tiles if n == 2 else with_stats)(f"acc{E - 1}_")}
    if kind == "self":
        def s(t):
            return [f"s{t}_{c}" for c in range(4)]

        def shift(t):
            return [f"{step}{t}_{c}" for c in range(4) for step in ("max", "shift")]
        pe, dve = ["qk", "v"] + s(0), ["q", "k", "v"] + shift(0)
        for t in range(NT):
            pe += s(t + 1) * (t + 1 < NT) + [f"t{t}_{c}" for c in range(4)] + [f"o{t}"]
            dve += shift(t + 1) * (t + 1 < NT) + [f"recip{t}", f"o{t}"]
        return {"pe": pe + ["o_turned"] + tiles("proj"), "dve": dve + ["hb"] + with_stats("h"), "pool": [f"kb{t}_{c}" for t in range(NT) for c in range(4)],
                "act": [f"{step}{t}_{c}" for t in range(NT) for step in ("exp", "pt") for c in range(4)] + ["o_copied"]}
    if kind == "sim":
        return {"pe": ["sim2"], "pool": ["sim_norm"], "dve": ["sim2", "sim2_max"]}
    assert kind == "gated"
    turns = [f"m{t}{half}" for t in range(NT) for half in "ab"]
    return {"pe": ["logits"] + [f"p{p}_{t}" for p in range(EP) for t in range(NT)] + ["qk_turned", "s", "t", "o"]
            + turns[0:2] + [x for t in range(NT) for x in turns[2 * t + 2:2 * t + 4] + [f"f{t}"]],
            "act": ["gate_exp", "exp", "qk_copied", "s_exp", "pt"] + turns,
            "pool": ["y_norm"],
            "dve": ["sim_unit", "y2", "y2_sum", "y2_max", "gate1", "gate", "cos", "logits", "pos", "any",
                    "gated", "gmax"] + TOP2 + ["two", "none", "fallback", "active", "shift", "em", "sum", "recip", "rw"]
            + [f"{k}{p}_{t}" for p in range(EP) for k in "ab" for t in range(NT)]
            + ["masked", "smax", "sshift", "ssum", "srecip", "o"] + tiles("mix") + with_stats("added")}


def program_order():
    seq = []
    turn = ln = moe = 0
    for l in range(L):
        seq += [("ln", ln)] + [("count", l)] * (l in MASKED) + [("sim", 0)] * (l == 2) + [("turn", turn), ("q", l), ("out", l), ("ln", ln + 1)]
        ln, turn = ln + 2, turn + 1
        if l == 0:
            seq += [("ln", ln), ("turn", turn), ("self", 0), ("ln", ln + 1)]
            ln, turn = ln + 2, turn + 1
        seq.append(("turn", turn))
        turn += 1
        if l == 2:
            seq.append(("gated", 0))
        else:
            seq.append(("moe", moe))
            moe += 1
    return seq


def step_counts():
    n = {"pe": 0, "act": 0, "dve": 0, "pool": 0}
    at = {}
    for phase in program_order():
        for who, names in phase_steps(phase).items():
            for step in names:
                n[who] += 1
                at[(who, phase, step)] = n[who]
    return at


def build(nc, a, out):
    at = step_counts()
    items = all_items()
    place = {item: n for n, item in enumerate(items)}

    with ExitStack() as ctx:
        def sb(name, shape, dt):
            return ctx.enter_context(nc.sbuf_tensor(name, shape, dt))

        def sem(name):
            return ctx.enter_context(nc.semaphore(name))

        ps = ctx.enter_context(nc.psum_tensor("ps", [P, 8, 512], F32))
        BANK_PV, BANK_AUX, N_AUX = 4, 5, 3
        TILE_BANKS = (5, 6, 7, 0)

        ctxT = sb("ctxT", [P, 3, KV], F32)
        khi = sb("khi", [P, 2, KV], F16)
        klo = sb("klo", [P, 2, KV], F16)
        kq = sb("kq", [P, 2, QUADS, KPAD], F16)
        v_aug = sb("v_aug", [P, 2, KT, 8, 32], F32)
        probs = sb("probs", [P, 2, HC], F32)
        qn = sb("qn", [P, 2, H, S], F16)
        qb = sb("qb", [P, 2, QUADS, HQ, S], F16)
        mx_part = sb("mx_part", [P, 2, 8, KS], F32)
        mx = sb("mx", [P, 2, 8], F16)
        masked_scores = sb("masked_scores", [T, 2, KP], F32)
        oc_t = sb("oc_t", [P, 2, S], F32)
        oc = sb("oc", [P, 2, S], F32)
        rden = sb("rden", [P, 2, S], F32)
        o_all = sb("o_all", [P, 2, TOK], F32)
        mask_u8 = sb("mask_u8", [T, 2, KV], U8)
        tri_u8 = sb("tri_u8", [T, KV], U8)
        mask_q = sb("mask_q", [T, 2, KV], BF16)
        maskT_u8 = sb("maskT_u8", [P, B, KT, S], U8)
        triT_u8 = sb("triT_u8", [P, KT, S], U8)
        padT_u8 = sb("padT_u8", [P, B, KT], U8)
        mask_t = sb("mask_t", [P, B, KT, S], BF16)
        keep = sb("keep", [P, TOK], F32)
        weights = sb("weights", [P, 5120], F32)
        big1 = sb("big1", [P, 4, TOK], F32)
        big2 = sb("big2", [P, 4, TOK], F32)
        big3 = weights[:, 3072:3072 + 4 * TOK].rearrange("p (a c) -> p a c", a=4)
        big0 = probs[:, :, :].rearrange("p a c -> p (a c)").rearrange("p (a c) -> p a c", a=4)
        kvw = sb("kvw", [P, L, 256], F32)
        xw = sb("xw", [P, 7 * D], F32)
        xb = sb("xb", [P, L, 8], F32)
        rows = sb("rows", [T, R_N, D], F32)
        cst = sb("cst", [P, C_W], F32)
        id16 = sb("id16", [P, P], F16)
        id_mask = sb("id_mask", [P, P], BF16)
        id_b = sb("id_b", [P, P], BF16)
        blk_b = sb("blk_b", [P, T], BF16)
        ones_b = sb("ones_b", [P, P], BF16)
        ones_f = sb("ones_f", [P, P], F32)
        bm16 = sb("bm16", [P, H], F16)
        m4 = sb("m4", [P, HQ], F16)
        x = sb("x", [T, NT, D], F32)
        y = sb("y", [T, NT, D], F32)
        z = sb("z", [T, NT, D], F32)
        v_self = sb("v_self", [T, NT, H, DH + 1], F32)
        hbuf = sb("hbuf", [T, NT, D], F32)
        yT = sb("yT", [P, TOK], F32)
        qnf = sb("qnf", [P, TOK], F32)
        qn16 = sb("qn16", [P, TOK], F16)
        st = sb("st", [T, NT, 6], F32)
        mv = sb("mv", [T, NT, 2], F32)
        ve = sb("ve", [T, NT], F32)
        rstd = sb("rstd", [T, NT], F32)
        mhalf = sb("mhalf", [P, NT * 8], F32)
        sm = sb("sm", [T, 16, NT * E2], F32)
        s1 = sb("s1", [T, 12, NT], F32)
        rw1 = sb("rw1", [P, D], F32)
        rb1 = sb("rb1", [P, 1], F32)
        b1 = sb("b1", [P, 3, E, FC], F32)
        b2 = sb("b2", [E, 3, D], F32)
        wg = sb("wg", [P, 3, E], F32)
        fw = sb("fw", [P, 4 * D], F32)
        fb = sb("fb", [P, 6], F32)
        sim = sb("sim", [P, E2], F32)
        sim2 = sb("sim2", [P, 4, E2], F32)
        sumh = sb("sumh", [T, 4, H], F32)
        sbias = sb("sbias", [P, 4], F32)

        ident = cst[:, C_ID:C_ID + P]
        perm = cst[:, C_PERM:C_PERM + P]

        qs = big1
        qv = big2[:, 0:2, :].rearrange("p a c -> p (a c)").bitcast(F16).rearrange("p (a c) -> p a c", a=4)
        qv_hi = big2[:, 2:4, :].rearrange("p a c -> p (a c)").bitcast(F16).rearrange("p (a c) -> p a c", a=4)

        ctx_in = [sem(f"ctx_in{i}") for i in range(3)]
        cst_in = sem("cst_in")
        const_in = sem("const_in")
        kvw_in = sem("kvw_in")
        x_in = sem("x_in")
        xw_in = sem("xw_in")
        weights_in = [sem(f"weights_in{i}") for i in range(SLOTS)]
        gated_in = sem("gated_in")
        mask_in = [sem(f"mask_in{i}") for i in range(2)]
        consts_ready = sem("consts_ready")
        pool_ready = sem("pool_ready")
        fills_done = sem("fills_done")
        aux_filled = sem("aux_filled")
        khi_done = sem("khi_done")
        klo_done = sem("klo_done")
        v_done = sem("v_done")
        smax_done = sem("smax_done")
        mx_done = sem("mx_done")
        mrow_done = sem("mrow_done")
        kq_in = [sem(f"kq_in{i}") for i in range(2)]
        first_qn_done = sem("first_qn_done")
        qn_done = sem("qn_done")
        qb_done = sem("qb_done")
        maskq_half = sem("maskq_half")
        maskq_done = sem("maskq_done")
        mask_rows_done = sem("mask_rows_done")
        maskt_done = sem("maskt_done")
        scores_done = sem("scores_done")
        exp_done = sem("exp_done")
        pv_done = sem("pv_done")
        oc_half = sem("oc_half")
        oc_done = sem("oc_done")
        rden_done = sem("rden_done")
        o_half = sem("o_half")
        o_done = sem("o_done")
        out_done = sem("out_done")
        steps = {w: sem(f"{w}_step") for w in ("pe", "act", "dve", "pool")}
        pe_step, act_step, dve_step, pool_step = (steps[w] for w in ("pe", "act", "dve", "pool"))

        block = ctx.enter_context(nc.Block())

        def after(eng, who, phase, step):
            eng.wait_ge(steps[who], at[(who, phase, step)])

        def bank(item):
            return BANK_AUX + place[item] % N_AUX

        def q_scale(l):
            return float(D) ** -0.5 if l == 2 else float(DH) ** -0.5

        def masks_before(g):
            return sum(1 for k in range(g + 1) if k // B in MASKED)

        def weights_count(mi, e):
            per = [len([k for k in range(E) if k % SLOTS == s]) for s in range(SLOTS)]
            return 16 * (mi * per[e % SLOTS] + e // SLOTS + 1)

        def prior(ph, kind):
            seq = program_order()
            return [p for p in seq[:seq.index(ph)] if p[0] == kind][-1]

        def prior_of(ph):
            seq = program_order()
            return seq[seq.index(ph) - 1]

        def turn_sources():
            seq, out_ = program_order(), []
            for i, p in enumerate(seq):
                if p[0] == "turn":
                    q = [r for r in seq[:i] if r[0] not in ("count", "sim")][-1]
                    out_.append((ln_io(q[1])[1], q))
            return out_

        mixed = (big0[0:T, :, :].rearrange("p a c -> p (a c)")[:, 0:E2 * HD2], weights[0:T, 4096:5120])
        mixed_t = ((o_all[:, 0, :], o_all[:, 1, :]), (yT[:, :], qnf[:, :]))
        s_buf = big0[0:T, 3, :]
        hbuf_T = keep
        qkv = big1[0:T, :, :].rearrange("p a c -> p (a c)")[:, 0:768].rearrange("p (t c) -> p t c", t=NT)
        N_FILLS = 5
        N_CONST = 14

        def ln_io(n):
            lns = [(x, y), (x, y), (y, z), (hbuf, z)] + [(x, y)] * 6
            return lns[n]

        @block.sync
        def _(sp):
            sp.dma_start(x[:, :, :], a["x"].rearrange("(t p) d -> p t d", p=T)).then_inc(x_in, 16)
            sp.dma_start(kvw[:, :, :], a["kvw"]).then_inc(kvw_in, 16)
            sp.dma_start(ctxT[:, 0, :], a["ctxT"][0]).then_inc(ctx_in[0], 16)
            sp.dma_start(xb[:, :, :], a["xb"]).then_inc(kvw_in, 16)
            sp.dma_start(cst[:, :], a["cst"]).then_inc(cst_in, 16)
            sp.dma_start(ctxT[:, 1, :], a["ctxT"][1]).then_inc(ctx_in[1], 16)
            sp.dma_start(xw[:, :], a["xw"][0]).then_inc(xw_in, 16)

            def load_constants():
                sp.dma_start(rows[:, :, :], a["rows"].rearrange("r d -> (r d)").partition_broadcast(T)
                             .rearrange("p (r d) -> p r d", d=D)).then_inc(const_in, 16)
                sp.dma_start(ctxT[:, 2, :], a["ctxT"][2]).then_inc(ctx_in[2], 16)
                for dst, src in ((rw1[:, :], "rw1"), (rb1[:, :], "rb1"), (b1[:, :, :, :], "b1"), (b2[:, :, :], "b2"),
                                 (wg[:, :, :], "wg"), (fw[:, :], "fw"), (fb[:, :], "fb"), (sim[:, :], "sim"),
                                 (tri_u8[0:S, :], "tri"), (tri_u8[S:T, :], "tri"), (maskT_u8[0:KK, :, :, :], "maskT"),
                                 (triT_u8[0:KK, :, :], "triT"), (padT_u8[0:KK, :, :], "padT")):
                    sp.dma_start(dst, a[src]).then_inc(const_in, 16)

            def spread_keys(g):
                sp.wait_ge(klo_done, KS * (g + 1))
                if g >= 2:
                    sp.wait_ge(scores_done, KT * (g - 1))
                for quad in range(QUADS):
                    r = slice(32 * quad, 32 * quad + 32)
                    for blk, part in enumerate((khi, klo, khi)):
                        sp.dma_start(kq[32 * blk:32 * blk + 32, g % 2, quad, 0:KV], part[r, g % 2, :])\
                            .then_inc(kq_in[g % 2], 16)

            def load_mask(g):
                if masks_before(g) > 2:
                    sp.wait_ge(maskq_done, masks_before(g) - 2)
                b = g % B
                src = a["mask"][:, b, :] if g // B == 1 else a["pad"][b, :].partition_broadcast(S)
                for half in range(2):
                    sp.dma_start(mask_u8[half * S:(half + 1) * S, g % 2, :], src).then_inc(mask_in[g % 2], 16)

            spread_keys(0)
            load_constants()
            spread_keys(1)
            for l in range(L):
                if l:
                    after(sp, "pe", ("out", l - 1), f"projected{NT - 1}")
                    sp.dma_start(xw[:, :], a["xw"][l]).then_inc(xw_in, 16)
                mi = {0: 0, 1: 1, 3: 2}.get(l)
                if l:
                    former = ("gated", 0) if l == 3 else ("moe", l - 1)
                    after(sp, "pe", former, f"f{NT - 1}" if l == 3 else f"y{E - 1}_{NT - 1}")
                if mi is None:
                    sp.dma_start(weights[:, 0:3072], a["qkv2"]).then_inc(gated_in, 16)
                    sp.dma_start(weights[:, 3072:4096], a["o2"]).then_inc(gated_in, 16)
                else:
                    for e in range(SLOTS):
                        sp.dma_start(weights[:, e * 1024:(e + 1) * 1024], a["moe"][mi * E + e])\
                            .then_inc(weights_in[e], 16)
                for g in range(l * B, (l + 1) * B):
                    if g + 3 < G:
                        sp.wait_ge(v_done, 3 * (g + 1))
                        sp.dma_start(ctxT[:, g % 3, :], a["ctxT"][(g + 3) % B]).then_inc(ctx_in[g % 3], 16)
                    if g + 3 < G and (g + 3) // B in MASKED:
                        load_mask(g + 3)
                    if g + 2 < G:
                        spread_keys(g + 2)
                if mi is not None:
                    for e in range(SLOTS, E):
                        after(sp, "pe", ("moe", mi), f"y{e - SLOTS}")
                        k = e % SLOTS
                        sp.dma_start(weights[:, k * 1024:(k + 1) * 1024], a["moe"][mi * E + e])\
                            .then_inc(weights_in[k], 16)
            after(sp, "dve", ("moe", 2), f"acc{E - 1}_{NT - 1}")
            sp.dma_start(out.rearrange("(t p) d -> p t d", p=T), x[:, :, :]).then_inc(out_done, 16)
            sp.wait_ge(out_done, 16)

        @block.gpsimd
        def _(pool):
            fills = [(mhalf[:, :], -0.5), (kq[:, :, :, KV:KPAD], 0.0), (kq[96:128, 0, :, 0:KV], 1.0),
                     (kq[96:128, 1, :, 0:KV], 1.0), (ones_f[:, :], 1.0)]

            def fill(numbers):
                for n in numbers:
                    if n:
                        pool.wait_ge(pool_ready, n)
                    nc.gpsimd.memset(*fills[n]).then_inc(pool_ready, 1)

            def rsqrt(ph):
                after(pool, "dve", ph, "var")
                pool.wait_ge(pool_ready, 3 if ph == ("ln", 0) else N_FILLS)
                nc.gpsimd.tensor_tensor(rstd[:, :], ve[:, :], mhalf[0:T, 0:NT], ALU.pow).then_inc(pool_step, 1)

            fill(range(3))
            for ph in program_order():
                kind, n = ph
                if kind == "ln":
                    rsqrt(ph)
                    if n == 0:
                        after(pool, "pool", ph, "rstd")
                        fill(range(3, N_FILLS))
                elif kind == "sim":
                    after(pool, "dve", ph, "sim2_max")
                    nc.gpsimd.tensor_tensor(sim2[:, 2, :], sim2[:, 1, :], mhalf[:, 0:E2], ALU.pow).then_inc(pool_step, 1)
                elif kind == "gated":
                    after(pool, "dve", ph, "y2_max")
                    nc.gpsimd.tensor_tensor(s1[:, 1, :], s1[:, 0, :], mhalf[0:T, 0:NT], ALU.pow).then_inc(pool_step, 1)
                elif kind == "self":
                    after(pool, "dve", ph, "k")
                    for t in range(NT):
                        for c in range(4):
                            if t:
                                after(pool, "pe", ph, f"s{t - 1}_{c}")
                            nc.gpsimd.tensor_tensor(big3[:, c, :].rearrange("p (h k) -> p h k", h=4),
                                                    keep[:, t * T:(t + 1) * T].unsqueeze(1).broadcast_to([P, 4, T]),
                                                    cst[:, C_BM + 4 * c:C_BM + 4 * c + 4].unsqueeze(2).broadcast_to([P, 4, T]),
                                                    ALU.mult).then_inc(pool_step, 1)
                elif kind == "q":
                    def low_parts(part):
                        cols = (slice(0, S), slice(S, TOK))[part]
                        if n == 2:
                            after(pool, "act", ph, "scaled")
                            width = cols.stop - cols.start
                            nc.gpsimd.tensor_tensor(qs[:, :, cols], qs[:, :, cols],
                                                    keep[:, cols].unsqueeze(1).broadcast_to([P, QUADS, width]), ALU.mult)\
                                .then_inc(pool_step, 1)
                        after(pool, "act", ph, f"hi_lo{part}")
                        nc.gpsimd.tensor_tensor(qv[64:96, :, cols], qs[64:96, :, cols], qv_hi[64:96, :, cols], ALU.subtract)\
                            .then_inc(pool_step, 1)
                        after(pool, "pool", ph, f"lo{part}")

                    for b in range(B):
                        g = n * B + b
                        if b == 0:
                            pool.wait_ge(consts_ready, 1)
                            after(pool, "dve", ph, "q16")
                        else:
                            if g >= 2:
                                pool.wait_ge(smax_done, maxima_before(g - 1))
                            src = qn16[:, b * S:(b + 1) * S].unsqueeze(1).broadcast_to([P, H, S])
                            nc.gpsimd.tensor_tensor(qn[:, g % 2, :, :], src,
                                                    bm16[:, :].unsqueeze(2).broadcast_to([P, H, S]), ALU.mult)\
                                .then_inc(qn_done, 1)
                            pool.wait_ge(qn_done, n * (B - 1) + b)
                        if b < 2:
                            low_parts(b)
                        if g >= 2:
                            pool.wait_ge(scores_done, KT * (g - 1))
                        src = qv[0:96, :, b * S:(b + 1) * S].unsqueeze(2).broadcast_to([96, QUADS, HQ, S])
                        sel = m4[0:96, :].unsqueeze(1).unsqueeze(3).broadcast_to([96, QUADS, HQ, S])
                        nc.gpsimd.tensor_tensor(qb[0:96, g % 2, :, :, :], src, sel, ALU.mult).then_inc(qb_done, 1)

        @block.tensor
        def _(pe):
            mm = nc.tensor.matmul

            def gated_pe(pe, ph):
                after(pe, "act", prior(ph, "turn"), "copied")
                after(pe, "dve", ph, "sim_unit")
                for t in range(NT):
                    last = mm(ps[0:T, 2, t * E2:(t + 1) * E2], yT[:, t * T:(t + 1) * T], sim2[:, 3, :], start=True, stop=True)
                last.then_inc(pe_step, 1)
                pe.wait_ge(gated_in, 32)
                after(pe, "dve", ph, "cos")
                for p in range(EP):
                    for t in range(NT):
                        if p >= 2:
                            after(pe, "dve", ph, f"b{p - 2}_{t}")
                        mm(ps[0:T, 4 * (p % 2) + t, 0:384], yT[:, t * T:(t + 1) * T], weights[:, p * 384:(p + 1) * 384],
                           start=True, stop=True).then_inc(pe_step, 1)
                after(pe, "dve", ph, f"b{EP - 1}_{NT - 1}")
                for t in range(NT):
                    nc.tensor.transpose(ps[0:HD2, 0, t * T:(t + 1) * T], qkv[:, t, 0:64], ident[0:T, 0:T])
                    last = nc.tensor.transpose(ps[0:HD2, 1, t * T:(t + 1) * T], qkv[:, t, 64:128], ident[0:T, 0:T])
                last.then_inc(pe_step, 1)
                after(pe, "act", ph, "qk_copied")
                for t in range(NT):
                    cols = slice(t * T, (t + 1) * T)
                    last = mm(ps[0:T, 2, cols], big2[0:HD2, 0, cols], big2[0:HD2, 1, cols], start=True, stop=True)
                last.then_inc(pe_step, 1)
                after(pe, "act", ph, "s_exp")
                for t in range(NT):
                    last = nc.tensor.transpose(ps[0:T, 3, t * T:(t + 1) * T], big2[0:T, 2, t * T:(t + 1) * T], ident[0:T, 0:T])
                last.then_inc(pe_step, 1)
                after(pe, "act", ph, "pt")
                for t in range(NT):
                    last = mm(ps[0:T, 4, t * HD2:(t + 1) * HD2], big2[0:T, 3, t * T:(t + 1) * T], qkv[:, t, 128:192],
                              start=True, stop=True)
                last.then_inc(pe_step, 1)

                def turn_mixed(t):
                    after(pe, "dve", ph, f"mix{t}")
                    for half in range(2):
                        if t >= 2:
                            after(pe, "act", ph, f"m{t - 2}{'ab'[half]}")
                        for c in range(4):
                            src = mixed[t % 2][:, (4 * half + c) * P:(4 * half + c + 1) * P]
                            last = nc.tensor.transpose(ps[:, 2 * (t % 2) + half, c * T:(c + 1) * T], src, ident[0:T, 0:T])
                        last.then_inc(pe_step, 1)

                turn_mixed(0)
                for t in range(NT):
                    if t + 1 < NT:
                        turn_mixed(t + 1)
                    after(pe, "act", ph, f"m{t}b")
                    for c in range(EP):
                        last = mm(ps[0:T, TILE_BANKS[t], 0:D], mixed_t[t % 2][c // 4][:, (c % 4) * T:(c % 4 + 1) * T],
                                  weights[:, 3072 + c * D:3072 + (c + 1) * D], start=c == 0, stop=c == EP - 1)
                    last.then_inc(pe_step, 1)

            def wait_evacuated(item):
                kind, g, i = item
                if kind == "K":
                    pe.wait_ge(khi_done, KS * g + i + 1)
                    pe.wait_ge(klo_done, KS * g + i + 1)
                elif kind == "V":
                    pe.wait_ge(v_done, 3 * g + i + 1)
                elif kind == "S":
                    pe.wait_ge(smax_done, maxima_before(g) + i + 1)
                elif kind == "D":
                    pe.wait_ge(rden_done, g + 1)
                else:
                    pe.wait_ge(mrow_done, 2 * g + i + 1)

            def side(item):
                kind, g, i = item
                l, bk = g // B, bank(item)
                if place[item] >= N_AUX:
                    wait_evacuated(items[place[item] - N_AUX])
                if kind == "K":
                    if i == 0:
                        pe.wait_ge(ctx_in[g % 3], 16 * (g // 3 + 1))
                    last = mm(ps[:, bk, 0:KP], kvw[:, l, 0:D], ctxT[:, g % 3, i * KP:(i + 1) * KP], start=True, stop=True)
                elif kind == "V":
                    for j in range(4):
                        kt = 4 * i + j
                        last = mm(ps[0:KK, bk, j * D:(j + 1) * D], ctxT[:, g % 3, kt * KK:(kt + 1) * KK],
                                  kvw[:, l, D:2 * D], start=True, stop=True)
                elif kind == "S":
                    c, k = divmod(i, KS)
                    if i == 0:
                        if g % B == 0:
                            pe.wait_ge(first_qn_done, l + 1)
                        else:
                            pe.wait_ge(qn_done, l * (B - 1) + g % B)
                    q2 = qn[:, g % 2, :, :].rearrange("p h s -> p (h s)")
                    last = mm(ps[0:chunk(g), bk, 0:KP], q2[:, c * chunk(g):(c + 1) * chunk(g)],
                              khi[:, g % 2, k * KP:(k + 1) * KP], start=True, stop=True)
                elif kind == "D":
                    pe.wait_ge(oc_done, g + 1)
                    last = mm(ps[:, bk, 0:2 * S], perm, oc[:, :, :].rearrange("p r s -> p (r s)"), start=True, stop=True)
                else:
                    if i == 0:
                        pe.wait_ge(mx_done, g + 1)
                    w = chunk(g)
                    for j, c in enumerate(range(4 * i, min(4 * i + 4, chunks(g)))):
                        last = mm(ps[0:1, bk, j * w:(j + 1) * w], mx[0:w, g % 2, c:c + 1], id16[0:w, 0:w], start=True, stop=True)
                last.then_inc(aux_filled, 1)

            def scores(g, kt):
                n = g * KT + kt
                if kt == 0:
                    pe.wait_ge(kq_in[g % 2], 16 * 12 * (g // 2 + 1))
                    pe.wait_ge(qb_done, g + 1)
                    pe.wait_ge(mrow_done, 2 * (g + 1))
                if n >= 2:
                    pe.wait_ge(exp_done, n - 1)
                masked = g // B in MASKED
                for quad in range(QUADS):
                    dst = ps[:, 2 * (kt % 2) + quad // 2, (quad % 2) * 224:(quad % 2 + 1) * 224]
                    last = mm(dst, kq[:, g % 2, quad, kt * KK:kt * KK + P],
                              qb[:, g % 2, quad, :, :].rearrange("p h s -> p (h s)"), start=True, stop=not masked)
                    if masked:
                        mt = mask_t[:, g % B, kt, :].unsqueeze(1).broadcast_to([P, HQ, S])
                        last = mm(dst.rearrange("p (h s) -> p h s", s=S), id_mask[:, :], mt, start=False, stop=True)
                last.then_inc(scores_done, 1)

            def values(g, kt, r):
                n = g * KT + kt
                if kt % 4 == 0 and r == 0:
                    pe.wait_ge(v_done, 3 * g + kt // 4 + 1)
                if kt == 0 and r == 0 and g:
                    pe.wait_ge(oc_done, g)
                if r == 0:
                    pe.wait_ge(exp_done, n + 1)
                for j in range(4):
                    t8 = 4 * r + j
                    last = mm(ps[32 * j:32 * j + 32, BANK_PV, r * T:(r + 1) * T],
                              v_aug[0:KK, g % 2, kt, t8, :], probs[0:KK, kt % 2, t8 * T:(t8 + 1) * T],
                              start=(kt == 0 and r == 0), stop=(kt == KT - 1), skip_group_check=True)
                if r:
                    last.then_inc(pv_done, 1)

            def attention(l):
                for g in range(l * B, (l + 1) * B):
                    if g % B == 0:
                        for item in head_items(g)[N_AUX:]:
                            side(item)
                        scores(g, 0)
                    for kt, slot in enumerate(aux_slots(g)):
                        for where, item in slot:
                            if where == BEFORE:
                                side(item)
                        if kt + 1 < KT:
                            scores(g, kt + 1)
                        elif (g + 1) % B:
                            scores(g + 1, 0)
                        for where, item in slot:
                            if where == BETWEEN:
                                side(item)
                        values(g, kt, 0)
                        for where, item in slot:
                            if where == HALFWAY:
                                side(item)
                        values(g, kt, 1)
                side(("D", (l + 1) * B - 1, 0))

            pe.wait_ge(kvw_in, 32)
            for item in FIRST_ITEMS[0:KS]:
                side(item)
            pe.wait_ge(cst_in, 16)
            src_of_turn = turn_sources()
            for ph in program_order():
                kind, n = ph
                if kind == "turn":
                    src, before = src_of_turn[n]
                    for t in range(NT):
                        after(pe, "dve", before, f"norm{t}")
                        last = nc.tensor.transpose(ps[:, 0, t * T:(t + 1) * T], src[:, t, :], ident[0:T, 0:T])
                    last.then_inc(pe_step, 1)
                elif kind == "count":
                    pe.wait_ge(maskt_done, B * (MASKED.index(n) + 1))
                    after(pe, "dve", ("moe", 0) if n == 1 else ("moe", 1), f"acc{E - 1}_{NT - 1}")
                    for kt in range(KT):
                        last = mm(ps[:, 5, 0:TOK].rearrange("p (b s) -> p b s", s=S), ones_b[0:KK, :], mask_t[0:KK, :, kt, :], start=kt == 0, stop=kt == KT - 1)
                    last.then_inc(pe_step, 1)
                elif kind == "sim":
                    after(pe, "dve", ph, "sim2")
                    mm(ps[:, 6, 0:E2], ones_f[:, :], sim2[:, 0, :], start=True, stop=True).then_inc(pe_step, 1)
                elif kind == "q":
                    pe.wait_ge(xw_in, 16 * (n + 1))
                    after(pe, "act", prior(ph, "turn"), "copied")
                    mm(ps[:, 4, 0:TOK], xw[:, 0:D], yT[:, :], start=True, stop=True).then_inc(pe_step, 1)
                    if n == 0:
                        for item in FIRST_ITEMS[KS:]:
                            side(item)
                        pe.wait_ge(consts_ready, 1)
                        pe.wait_ge(pool_ready, N_FILLS)
                    for quad in range(QUADS):
                        if quad == 1:
                            for item in head_items(n * B)[0:N_AUX]:
                                side(item)
                        last = mm(ps[:, quad, 0:TOK], xw[:, D * (1 + quad):D * (2 + quad)], yT[:, :], start=True, stop=True)
                    last.then_inc(pe_step, 1)
                    attention(n)
                elif kind == "out":
                    pe.wait_ge(o_done, B * (n + 1))
                    for t in range(NT):
                        for r in range(2):
                            last = mm(ps[0:T, t, 0:D], o_all[:, r, t * T:(t + 1) * T],
                                      xw[:, D * (5 + r):D * (6 + r)], start=r == 0, stop=r == 1)
                        last.then_inc(pe_step, 1)
                elif kind == "moe":
                    pe.wait_ge(const_in, 16 * N_CONST)
                    after(pe, "act", prior(ph, "turn"), "copied")
                    rT = yT
                    if n == 2:
                        mm(ps[:, 1, 0:TOK], rw1[:, :], yT[:, :], start=True, stop=True).then_inc(pe_step, 1)
                        after(pe, "act", ph, "r1")
                        rT = hbuf_T
                    for t in range(NT):
                        last = mm(ps[0:T, 5, t * E:(t + 1) * E], rT[:, t * T:(t + 1) * T], wg[:, n, :], start=True, stop=True)
                    last.then_inc(pe_step, 1)

                    def hidden(e):
                        pe.wait_ge(weights_in[e % SLOTS], weights_count(n, e))
                        for c in range(FC):
                            if e:
                                after(pe, "act", ph, f"h{e - 1}_{c}")
                            w = (e % SLOTS) * 1024 + c * P
                            last = mm(ps[:, c, 0:TOK], weights[:, w:w + P], yT[:, :], start=True, stop=True)
                        last.then_inc(pe_step, 1)

                    def down(e):
                        after(pe, "act", ph, f"h{e}_{FC - 1}")
                        if e >= 2:
                            after(pe, "dve", ph, f"acc{e - 2}")
                        else:
                            after(pe, "dve", ph, "logits")
                        if e == E - 1:
                            after(pe, "dve", ph, "b2")
                        hT = (big0, big1)[e % 2]
                        for t in range(NT):
                            dst = ps[0:T, TILE_BANKS[t], 0:D] if e == E - 1 else ps[0:T, 4 + e % 2, t * D:(t + 1) * D]
                            for c in range(FC):
                                w = (e % SLOTS) * 1024 + F + c * D
                                last = mm(dst, hT[:, c, t * T:(t + 1) * T], weights[:, w:w + D], start=c == 0, stop=c == FC - 1)
                            if e == E - 1 or t == NT - 1:
                                last.then_inc(pe_step, 1)

                    hidden(0)
                    for e in range(E):
                        if e + 1 < E:
                            hidden(e + 1)
                        down(e)
                        if e == W_TURN:
                            after(pe, "dve", ph, "W")
                            for t in range(NT):
                                last = nc.tensor.transpose(ps[0:E, 6, t * T:(t + 1) * T], sm[:, 8, t * E:(t + 1) * E], ident[0:T, 0:T])
                            last.then_inc(pe_step, 1)
                        elif e == W_TURN + 1:
                            after(pe, "act", ph, "w_copied")
                            for t in range(NT):
                                last = mm(ps[0:T, 7, t * D:(t + 1) * D], keep[0:E, t * T:(t + 1) * T], b2[:, n, :], start=True, stop=True)
                            last.then_inc(pe_step, 1)
                elif kind == "self":
                    pe.wait_ge(const_in, 16 * N_CONST)
                    after(pe, "act", prior(ph, "turn"), "copied")
                    mm(ps[:, 4, 0:TOK], fw[:, 0:D], yT[:, :], start=True, stop=True)
                    mm(ps[:, 5, 0:TOK], fw[:, D:2 * D], yT[:, :], start=True, stop=True).then_inc(pe_step, 1)
                    for t in range(NT):
                        last = mm(ps[0:T, 3, t * D:(t + 1) * D], yT[:, t * T:(t + 1) * T], fw[:, 2 * D:3 * D], start=True, stop=True)
                    last.then_inc(pe_step, 1)
                    def self_scores(t):
                        for c in range(4):
                            after(pe, "dve", ph, f"shift{t - 1}_{c}" if t else "v")
                            after(pe, "pool", ph, f"kb{t}_{c}")
                            mm(ps[0:T, c, 0:448], qnf[:, t * T:(t + 1) * T], big3[:, c, :], start=True, stop=False)
                            last = mm(ps[0:T, c, 0:448].rearrange("p (h k) -> p h k", k=T), id_b[0:T, 0:T],
                                      blk_b[0:T, :].unsqueeze(1).broadcast_to([T, 4, T]), start=False, stop=True)
                            last.then_inc(pe_step, 1)

                    self_scores(0)
                    for t in range(NT):
                        if t + 1 < NT:
                            self_scores(t + 1)
                        for c in range(4):
                            after(pe, "act", ph, f"exp{t}_{c}")
                            i = 4 * t + c
                            if i >= 3:
                                after(pe, "act", ph, f"pt{(i - 3) // 4}_{(i - 3) % 4}")
                            for j in range(4):
                                last = nc.tensor.transpose(ps[0:T, 4 + i % 3, j * T:(j + 1) * T],
                                                           (big0, big1)[t % 2][0:T, c, j * T:(j + 1) * T], ident[0:T, 0:T])
                            last.then_inc(pe_step, 1)
                        if t:
                            after(pe, "dve", ph, f"o{t - 1}")
                        for h in range(H):
                            if h % 4 == 0:
                                after(pe, "act", ph, f"pt{t}_{h // 4}")
                            last = mm(ps[0:T, 7, h * 9:(h + 1) * 9], big2[0:T, h // 4, (h % 4) * T:(h % 4 + 1) * T],
                                      v_self[:, t, h, :], start=True, stop=True)
                        last.then_inc(pe_step, 1)
                    after(pe, "dve", ph, f"o{NT - 1}")
                    for t in range(NT):
                        last = nc.tensor.transpose(ps[:, 0, t * T:(t + 1) * T], hbuf[:, t, :], ident[0:T, 0:T])
                    last.then_inc(pe_step, 1)
                    after(pe, "act", ph, "o_copied")
                    for t in range(NT):
                        if t == NT - 1:
                            after(pe, "act", ph, f"pt{NT - 1}_3")
                        mm(ps[0:T, 1 + t, 0:D], yT[:, t * T:(t + 1) * T], fw[:, 3 * D:4 * D], start=True, stop=True).then_inc(pe_step, 1)
                elif kind == "gated":
                    gated_pe(pe, ph)

        @block.scalar
        def _(act):
            A = nc.scalar.activation

            def side(item):
                kind, g, i = item
                bk = bank(item)
                if kind in "SD":
                    return
                act.wait_ge(aux_filled, place[item] + 1)
                if kind == "K":
                    if g >= 2 and i == 0:
                        act.wait_ge(kq_in[g % 2], 16 * 12 * (g // 2))
                    A(khi[:, g % 2, i * KP:(i + 1) * KP], ps[:, bk, 0:KP], ACT.Identity,
                      bias=xb[:, g // B, 0:1]).then_inc(khi_done, 1)
                elif kind == "V":
                    if g >= 2 and i == 0:
                        act.wait_ge(pv_done, KT * (g - 1))
                    dst = v_aug[0:KK, g % 2, 4 * i:4 * i + 4, :, 0:16].rearrange("p k t c -> p (k t) c")
                    A(dst, ps[0:KK, bk, :].rearrange("p (k c) -> p k c", c=16), ACT.Copy).then_inc(v_done, 1)
                else:
                    first = 4 * chunk(g) * i
                    last = min(first + 4 * chunk(g), HC)
                    row = qb[96:97, g % 2, :, :, :].rearrange("p a h s -> p (a h s)")
                    if i == 0 and g >= 2:
                        act.wait_ge(scores_done, KT * (g - 1))
                    A(row[:, first:last], ps[0:1, bk, 0:last - first], ACT.Copy, scale=-1.0).then_inc(mrow_done, 1)

            def exp(n):
                k = n % 2
                act.wait_ge(scores_done, n + 1)
                if n >= 2:
                    act.wait_ge(pv_done, n - 1)
                A(probs[0:KK, k, :].rearrange("p (a c) -> p a c", a=2),
                  ps[0:KK, 2 * k:2 * k + 2, 0:448], ACT.Exp).then_inc(exp_done, 1)

            def attention(l):
                for g in range(l * B, (l + 1) * B):
                    if g % B == 0:
                        for item in head_items(g):
                            if item[0] == "M":
                                side(item)
                        exp(g * KT)
                    for kt, slot in enumerate(aux_slots(g)):
                        for where, item in slot:
                            if where == BEFORE:
                                side(item)
                        if kt + 1 < KT or (g + 1) % B:
                            exp(g * KT + kt + 1)
                        for where, item in slot:
                            if where != BEFORE:
                                side(item)

            act.wait_ge(kvw_in, 32)
            act.wait_ge(fills_done, 1)
            for item in FIRST_ITEMS[0:KS]:
                side(item)
            for ph in program_order():
                kind, n = ph
                if kind == "turn":
                    after(act, "pe", ph, "turned")
                    if n in AFFINE:
                        act.wait_ge(const_in, 16 * N_CONST)
                        k = 2 + 2 * AFFINE.index(n)
                        A(yT[:, :], ps[:, 0, 0:TOK], ACT.Identity, bias=fb[:, k + 1:k + 2], scale=fb[:, k:k + 1]).then_inc(act_step, 1)
                    else:
                        A(yT[:, :], ps[:, 0, 0:TOK], ACT.Copy).then_inc(act_step, 1)
                elif kind == "q":
                    if n == 0:
                        for item in FIRST_ITEMS[KS:]:
                            side(item)
                    after(act, "pe", ph, "q")
                    after(act, "dve", ph, "sbias")
                    for quad in range(QUADS):
                        last = A(qs[:, quad, :], ps[:, quad, 0:TOK], ACT.Identity, bias=sbias[:, quad:quad + 1], scale=q_scale(n))
                    last.then_inc(act_step, 1)
                    for part, cols in enumerate((slice(0, S), slice(S, TOK))):
                        if part:
                            for item in head_items(n * B):
                                if item[0] == "V":
                                    side(item)
                        after(act, *(("pool", ph, f"kept{part}") if n == 2 else ("act", ph, "scaled")))
                        A(qv[0:64, :, cols], qs[0:64, :, cols], ACT.Copy).then_inc(act_step, 1)
                        A(qv_hi[64:96, :, cols], qs[64:96, :, cols], ACT.Copy).then_inc(act_step, 1)
                    attention(n)
                elif kind == "moe":
                    func = (ACT.Gelu_apprx_tanh, ACT.Relu, ACT.Silu)[n]
                    if n == 2:
                        act.wait_ge(const_in, 16 * N_CONST)
                        after(act, "pe", ph, "r1")
                        A(hbuf_T[:, :], ps[:, 1, 0:TOK], ACT.Silu, bias=rb1[:, 0:1]).then_inc(act_step, 1)
                        after(act, "dve", ph, "gap")
                        A(s1[:, 8, :], s1[:, 7, :], ACT.Exp).then_inc(act_step, 1)
                    else:
                        after(act, "dve", ph, "shift")
                        A(sm[:, 2, 0:32], sm[:, 1, 0:32], ACT.Exp).then_inc(act_step, 1)
                    act.wait_ge(const_in, 16 * N_CONST)
                    for e in range(E):
                        after(act, "pe", ph, f"h{e}")
                        if e >= 2:
                            after(act, "pe", ph, f"y{e - 2}")
                        for c in range(FC):
                            A((big0, big1)[e % 2][:, c, :], ps[:, c, 0:TOK], func, bias=b1[:, n, e, c:c + 1])\
                                .then_inc(act_step, 1)
                        if e == W_TURN + 1:
                            after(act, "pe", ph, "w_turned")
                            A(keep[0:E, :], ps[0:E, 6, 0:TOK], ACT.Copy).then_inc(act_step, 1)
                elif kind == "self":
                    for t in range(NT):
                        big = (big0, big1)[t % 2]
                        for c in range(4):
                            after(act, "dve", ph, f"shift{t}_{c}")
                            A(big[0:T, c, :], big[0:T, c, :], ACT.Exp).then_inc(act_step, 1)
                        if t:
                            after(act, "pe", ph, f"o{t - 1}")
                        for c in range(4):
                            after(act, "pe", ph, f"t{t}_{c}")
                            A(big2[0:T, c, :], ps[0:T, 4 + (4 * t + c) % 3, 0:448], ACT.Copy).then_inc(act_step, 1)
                    after(act, "pe", ph, "o_turned")
                    A(yT[:, :], ps[:, 0, 0:TOK], ACT.Copy).then_inc(act_step, 1)
                elif kind == "gated":
                    A(sm[:, 0, 0:E2], rows[:, R_GATE, 0:E2], ACT.Exp, scale=-1.0).then_inc(act_step, 1)
                    after(act, "dve", ph, "shift")
                    A(sm[:, 9, :], sm[:, 8, :], ACT.Exp).then_inc(act_step, 1)
                    after(act, "pe", ph, "qk_turned")
                    A(big2[0:HD2, 0:2, :], ps[0:HD2, 0:2, 0:TOK], ACT.Copy).then_inc(act_step, 1)
                    after(act, "dve", ph, "sshift")
                    A(big2[0:T, 2, :], s_buf, ACT.Exp).then_inc(act_step, 1)
                    after(act, "pe", ph, "t")
                    A(big2[0:T, 3, :], ps[0:T, 3, 0:TOK], ACT.Copy).then_inc(act_step, 1)
                    for t in range(NT):
                        for half in range(2):
                            after(act, "pe", ph, f"m{t}{'ab'[half]}")
                            if t >= 2:
                                after(act, "pe", ph, f"f{t - 2}")
                            A(mixed_t[t % 2][half], ps[:, 2 * (t % 2) + half, 0:TOK], ACT.Copy).then_inc(act_step, 1)

        @block.vector
        def _(dve):
            V = nc.vector
            TT, TS, STT = V.tensor_tensor, V.tensor_scalar, V.scalar_tensor_tensor

            def self_dve(dve, ph):
                V = nc.vector
                TT, TS, STT = V.tensor_tensor, V.tensor_scalar, V.scalar_tensor_tensor
                after(dve, "pe", ph, "qk")
                TS(qnf[:, :], ps[:, 4, 0:TOK], fb[:, 0:1], float(DH) ** -0.5, ALU.add, ALU.mult).then_inc(dve_step, 1)
                TS(keep[:, :], ps[:, 5, 0:TOK], fb[:, 1:2], None, ALU.add).then_inc(dve_step, 1)
                after(dve, "pe", ph, "v")
                V.memset(v_self[:, :, :, DH], 1.0)
                TT(v_self[:, :, :, 0:DH], ps[0:T, 3, :].rearrange("p (t h d) -> p t h d", h=H, d=DH),
                   rows[:, R_FBV, :].rearrange("p (h d) -> p h d", d=DH).unsqueeze(1).broadcast_to([T, NT, H, DH]), ALU.add)\
                    .then_inc(dve_step, 1)

                def shift(t):
                    if t >= 2:
                        after(dve, "pe", ph, f"t{t - 2}_3")
                    for c in range(4):
                        after(dve, "pe", ph, f"s{t}_{c}")
                        scores = ps[0:T, c, 0:448].rearrange("p (h k) -> p h k", k=T)
                        V.reduce_max(sumh[:, t % 2, 4 * c:4 * c + 4], scores, AX.X).then_inc(dve_step, 1)
                        after(dve, "dve", ph, f"max{t}_{c}")
                        TT((big0, big1)[t % 2][0:T, c, :].rearrange("p (h k) -> p h k", k=T), scores,
                           sumh[:, t % 2, 4 * c:4 * c + 4].unsqueeze(2).broadcast_to([T, 4, T]), ALU.subtract).then_inc(dve_step, 1)

                shift(0)
                for t in range(NT):
                    if t + 1 < NT:
                        shift(t + 1)
                    after(dve, "pe", ph, f"o{t}")
                    o = ps[0:T, 7, 0:H * (DH + 1)].rearrange("p (h d) -> p h d", d=DH + 1)
                    V.reciprocal(sumh[:, 2, :], o[:, :, DH]).then_inc(dve_step, 1)
                    after(dve, "dve", ph, f"recip{t}")
                    TT(hbuf[:, t, :].rearrange("p (h d) -> p h d", d=DH), o[:, :, 0:DH],
                       sumh[:, 2, :].unsqueeze(2).broadcast_to([T, H, DH]), ALU.mult).then_inc(dve_step, 1)
                TT(y[:, :, :], y[:, :, :], rows[:, R_FBO, :].unsqueeze(1).broadcast_to([T, NT, D]), ALU.add).then_inc(dve_step, 1)
                after(dve, "dve", ph, "hb")
                add_and_take_stats(ph, "proj", "h", banks=range(1, NT + 1), base=y, total=hbuf)

            def gated_dve(dve, ph, top2):
                V = nc.vector
                TT, TS, STT = V.tensor_tensor, V.tensor_scalar, V.scalar_tensor_tensor

                def did(step):
                    after(dve, "dve", ph, step)

                def v(i):
                    return sm[:, i, :].rearrange("p (t e) -> p t e", e=E2)

                def one(i):
                    return s1[:, i, :].unsqueeze(2).broadcast_to([T, NT, E2])

                after(dve, "pool", ("sim", 0), "sim_norm")
                TT(sim2[:, 3, :], sim[:, :], sim2[:, 2, :], ALU.mult).then_inc(dve_step, 1)
                TT(z[:, :, :], y[:, :, :], y[:, :, :], ALU.mult).then_inc(dve_step, 1)
                did("y2")
                V.reduce_sum(s1[:, 10, :], z[:, :, :], AX.X).then_inc(dve_step, 1)
                did("y2_sum")
                TS(s1[:, 0, :], s1[:, 10, :], 1e-24, None, ALU.max).then_inc(dve_step, 1)
                after(dve, "act", ph, "gate_exp")
                TS(sm[:, 1, 0:E2], sm[:, 0, 0:E2], 1.0, None, ALU.add).then_inc(dve_step, 1)
                did("gate1")
                V.reciprocal(sm[:, 2, 0:E2], sm[:, 1, 0:E2]).then_inc(dve_step, 1)
                after(dve, "pe", ph, "logits")
                after(dve, "pool", ph, "y_norm")
                did("gate")
                TT(v(0), ps[0:T, 2, 0:NT * E2].rearrange("p (t e) -> p t e", e=E2), one(1), ALU.mult).then_inc(dve_step, 1)
                did("cos")
                TT(v(1), v(0), sm[:, 2, 0:E2].unsqueeze(1).broadcast_to([T, NT, E2]), ALU.subtract).then_inc(dve_step, 1)
                did("logits")
                TS(v(10), v(1), 0.0, None, ALU.is_gt).then_inc(dve_step, 1)
                did("pos")
                V.reduce_max(s1[:, 6, :], v(10), AX.X).then_inc(dve_step, 1)
                TS(v(11), v(1), 0.0, None, ALU.max).then_inc(dve_step, 1)
                did("gated")
                V.reduce_max(s1[:, 7, :], v(11), AX.X).then_inc(dve_step, 1)
                top2(ph, v(1), E2)
                TT(v(12), v(4), v(7), ALU.add).then_inc(dve_step, 1)
                TS(s1[:, 8, :], s1[:, 6, :], -1.0, 1.0, ALU.mult, ALU.add).then_inc(dve_step, 1)
                did("none")
                TT(v(13), v(12), one(8), ALU.mult).then_inc(dve_step, 1)
                did("fallback")
                TT(v(14), v(13), v(10), ALU.add).then_inc(dve_step, 1)
                TT(v(8), v(11), one(7), ALU.subtract).then_inc(dve_step, 1)
                after(dve, "act", ph, "exp")
                TT(v(12), v(9), v(14), ALU.mult).then_inc(dve_step, 1)
                did("em")
                V.reduce_sum(s1[:, 9, :], v(12), AX.X).then_inc(dve_step, 1)
                did("sum")
                V.reciprocal(s1[:, 10, :], s1[:, 9, :]).then_inc(dve_step, 1)
                did("recip")
                TT(v(15), v(12), one(10), ALU.mult).then_inc(dve_step, 1)
                did("rw")
                for p in range(EP):
                    for k in range(2):
                        for t in range(NT):
                            w = sm[:, 15, t * E2 + 2 * p + k:t * E2 + 2 * p + k + 1]
                            part = ps[0:T, 4 * (p % 2) + t, 192 * k:192 * (k + 1)]
                            after(dve, "pe", ph, f"p{p}_{t}")
                            if p == 0 and k == 0:
                                TS(qkv[:, t, :], part, w, None, ALU.mult).then_inc(dve_step, 1)
                            else:
                                did(f"a{p}_{t}" if k else f"b{p - 1}_{t}")
                                STT(qkv[:, t, :], part, w, qkv[:, t, :], ALU.mult, ALU.add).then_inc(dve_step, 1)
                after(dve, "pe", ph, "s")
                s3 = s_buf.rearrange("p (t k) -> p t k", t=NT)
                STT(s3, ps[0:T, 2, 0:TOK].rearrange("p (t k) -> p t k", t=NT), float(HD2) ** -0.5,
                    cst[0:T, C_CAU:C_CAU + T].unsqueeze(1).broadcast_to([T, NT, T]), ALU.mult, ALU.add).then_inc(dve_step, 1)
                did("masked")
                V.reduce_max(s1[:, 2, :], s3, AX.X).then_inc(dve_step, 1)
                did("smax")
                TT(s3, s3, s1[:, 2, :].unsqueeze(2).broadcast_to([T, NT, T]), ALU.subtract).then_inc(dve_step, 1)
                after(dve, "act", ph, "s_exp")
                V.reduce_sum(s1[:, 3, :], big2[0:T, 2, :].rearrange("p (t k) -> p t k", t=NT), AX.X).then_inc(dve_step, 1)
                did("ssum")
                V.reciprocal(s1[:, 4, :], s1[:, 3, :]).then_inc(dve_step, 1)
                did("srecip")
                after(dve, "pe", ph, "o")
                TT(hbuf[:, :, 0:HD2], ps[0:T, 4, 0:NT * HD2].rearrange("p (t d) -> p t d", d=HD2),
                   s1[:, 4, :].unsqueeze(2).broadcast_to([T, NT, HD2]), ALU.mult).then_inc(dve_step, 1)
                did("o")
                for t in range(NT):
                    if t >= 2:
                        after(dve, "pe", ph, f"m{t - 2}b")
                    TT(mixed[t % 2].rearrange("p (e d) -> p e d", d=HD2), hbuf[:, t, 0:HD2].unsqueeze(1).broadcast_to([T, E2, HD2]),
                       sm[:, 15, t * E2:(t + 1) * E2].unsqueeze(2).broadcast_to([T, E2, HD2]), ALU.mult).then_inc(dve_step, 1)
                add_and_take_stats(ph, "f", "added")

            def add_and_take_stats(ph, made, added, banks=TILE_BANKS, weight=None, take=True, base=x, total=x):
                for t in range(NT):
                    after(dve, "pe", ph, f"{made}{t}")
                    src = ps[0:T, banks[t], 0:D]
                    if weight is None:
                        TT(total[:, t, :], src, base[:, t, :], ALU.add).then_inc(dve_step, 1)
                    else:
                        STT(total[:, t, :], src, weight(t), base[:, t, :], ALU.mult, ALU.add).then_inc(dve_step, 1)
                    if t and take:
                        after(dve, "dve", ph, f"{added}{t - 1}")
                        V.bn_stats(st[:, t - 1, :], total[:, t - 1, :]).then_inc(dve_step, 1)
                after(dve, "dve", ph, f"{added}{NT - 1}")
                if take:
                    V.bn_stats(st[:, NT - 1, :], total[:, NT - 1, :]).then_inc(dve_step, 1)

            def side(item):
                kind, g, i = item
                bk = bank(item)
                if kind == "K":
                    dve.wait_ge(khi_done, KS * g + i + 1)
                    if g >= 2 and i == 0:
                        dve.wait_ge(kq_in[g % 2], 16 * 12 * (g // 2))
                    STT(klo[:, g % 2, i * KP:(i + 1) * KP], ps[:, bk, 0:KP], xb[:, g // B, 0:1],
                        khi[:, g % 2, i * KP:(i + 1) * KP], ALU.add, ALU.subtract).then_inc(klo_done, 1)
                elif kind == "D":
                    dve.wait_ge(aux_filled, place[item] + 1)
                    V.reciprocal(rden[:, :, :].rearrange("p r s -> p (r s)"), ps[:, bk, 0:2 * S]).then_inc(rden_done, 1)
                    dve.wait_ge(rden_done, g + 1)
                    cols = slice((g % B) * S, (g % B + 1) * S)
                    TT(o_all[:, :, cols], oc[:, :, :], rden[:, :, :], ALU.mult).then_inc(o_half, 1)
                    dve.wait_ge(o_half, g + 1)
                    if g // B == 1:
                        TT(o_all[:, :, cols], o_all[:, :, cols], keep[:, cols].unsqueeze(1).broadcast_to([P, 2, S]), ALU.mult)\
                            .then_inc(o_done, 1)
                    else:
                        TT(o_all[:, :, cols], o_all[:, :, cols], xb[:, g // B, 6:8].unsqueeze(2).broadcast_to([P, 2, S]), ALU.add)\
                            .then_inc(o_done, 1)
                elif kind == "S":
                    c, k = divmod(i, KS)
                    dve.wait_ge(aux_filled, place[item] + 1)
                    w, masked = chunk(g), g // B in MASKED
                    if masked:
                        if i == 0:
                            dve.wait_ge(maskq_done, masks_before(g))
                        if i >= 2:
                            dve.wait_ge(smax_done, maxima_before(g) + i - 1)
                        V.tensor_tensor_reduce(out=masked_scores[:, i % 2, :], in0=ps[0:w, bk, 0:KP],
                                               in1=mask_q[:, g % 2, k * KP:(k + 1) * KP], scale=1.0, scalar=NEG, op0=ALU.add,
                                               op1=ALU.max, accum_out=mx_part[0:w, g % 2, c, k:k + 1]).then_inc(smax_done, 1)
                    else:
                        V.reduce_max(mx_part[:, g % 2, c, k:k + 1], ps[:, bk, 0:KP], AX.X).then_inc(smax_done, 1)
                    if i == chunks(g) * KS - 1:
                        dve.wait_ge(smax_done, maxima_before(g + 1))
                        V.reduce_max(mx[0:w, g % 2, 0:chunks(g)], mx_part[0:w, g % 2, 0:chunks(g), :], AX.X).then_inc(mx_done, 1)

            def mask_by_query(g):
                dve.wait_ge(mask_in[g % 2], 32 * ((masks_before(g) + 1) // 2))
                if g // B == 1:
                    V.tensor_scalar(mask_q[:, g % 2, :], mask_u8[:, g % 2, :], MASK, None, ALU.mult).then_inc(maskq_done, 1)
                else:
                    dve.wait_ge(const_in, 16 * N_CONST)
                    STT(mask_q[:, g % 2, :], tri_u8[:, :], 0.5, mask_u8[:, g % 2, :], ALU.is_lt, ALU.is_ge).then_inc(maskq_half, 1)
                    dve.wait_ge(maskq_half, masks_before(g) - B)
                    TS(mask_q[:, g % 2, :], mask_q[:, g % 2, :], MASK, None, ALU.mult).then_inc(maskq_done, 1)

            def mask_by_key(l, b):
                if l == 1:
                    last = V.tensor_copy(mask_t[0:KK, b, :, :], maskT_u8[0:KK, b, :, :])
                else:
                    last = STT(mask_t[0:KK, b, :, :], triT_u8[0:KK, :, :], 0.5,
                               padT_u8[0:KK, b, :].unsqueeze(2).broadcast_to([KK, KT, S]), ALU.is_lt, ALU.is_ge)
                last.then_inc(maskt_done, 1)

            def combine(g):
                dve.wait_ge(pv_done, KT * (g + 1))
                if g:
                    dve.wait_ge(o_done, g)
                pv = ps[:, BANK_PV, 0:2 * T].rearrange("p (r h s) -> p r h s", r=2, h=2)
                TS(oc_t[:, :, :], pv[:, :, 0, :], cst[:, C_SEL:C_SEL + 1], None, ALU.mult).then_inc(oc_half, 1)
                dve.wait_ge(oc_half, g + 1)
                STT(oc[:, :, :], pv[:, :, 1, :], cst[:, C_SEL + 1:C_SEL + 2], oc_t[:, :, :], ALU.mult, ALU.add)\
                    .then_inc(oc_done, 1)

            def attention(l):
                for g in range(l * B, (l + 1) * B):
                    if g % B == 0:
                        for item in head_items(g):
                            side(item)
                    for kt, slot in enumerate(aux_slots(g)):
                        for _, item in slot:
                            side(item)
                        if kt == KT - 2 and g + 2 < G and (g + 2) // B in MASKED:
                            mask_by_query(g + 2)
                        if kt == 3 and g % B == 1:
                            dve.wait_ge(const_in, 16 * N_CONST)
                            TT(x[:, :, :], x[:, :, :], rows[:, R_BO + l, :].unsqueeze(1).broadcast_to([T, NT, D]), ALU.add)\
                                .then_inc(dve_step, 1)
                        if kt == 5 and l == 0:
                            if g == 0:
                                V.memset(mask_t[96:128, :, :, :], 0.0).then_inc(mask_rows_done, 1)
                                dve.wait_ge(mask_rows_done, 1)
                            dve.wait_ge(const_in, 16 * N_CONST)
                            mask_by_key(1, g)
                    combine(g)
                side(("D", (l + 1) * B - 1, 0))

            def top2(ph, p, n_e):
                def v(i):
                    return sm[:, i, 0:NT * n_e].rearrange("p (t e) -> p t e", e=n_e)

                def one(i):
                    return s1[:, i, :].unsqueeze(2).broadcast_to([T, NT, n_e])

                rank = cst[0:T, C_RANK:C_RANK + n_e].unsqueeze(1).broadcast_to([T, NT, n_e])
                V.reduce_max(s1[:, 2, :], p, AX.X).then_inc(dve_step, 1)
                after(dve, "dve", ph, "v1")
                TT(v(3), p, one(2), ALU.is_equal).then_inc(dve_step, 1)
                after(dve, "dve", ph, "eq1")
                TT(v(5), v(3), rank, ALU.mult).then_inc(dve_step, 1)
                after(dve, "dve", ph, "sc1")
                V.reduce_max(s1[:, 3, :], v(5), AX.X).then_inc(dve_step, 1)
                after(dve, "dve", ph, "m1")
                TT(v(4), v(5), one(3), ALU.is_equal).then_inc(dve_step, 1)
                after(dve, "dve", ph, "oh1")
                STT(v(6), v(4), NEG, p, ALU.mult, ALU.add).then_inc(dve_step, 1)
                after(dve, "dve", ph, "p2")
                V.reduce_max(s1[:, 4, :], v(6), AX.X).then_inc(dve_step, 1)
                after(dve, "dve", ph, "v2")
                TT(v(3), v(6), one(4), ALU.is_equal).then_inc(dve_step, 1)
                after(dve, "dve", ph, "eq2")
                TT(v(5), v(3), rank, ALU.mult).then_inc(dve_step, 1)
                after(dve, "dve", ph, "sc2")
                V.reduce_max(s1[:, 5, :], v(5), AX.X).then_inc(dve_step, 1)
                after(dve, "dve", ph, "m2")
                TT(v(7), v(5), one(5), ALU.is_equal).then_inc(dve_step, 1)
                after(dve, "dve", ph, "oh2")

            def moe(ph, n):
                def v(i):
                    return sm[:, i, 0:NT * E].rearrange("p (t e) -> p t e", e=E)

                def one(i):
                    return s1[:, i, :].unsqueeze(2).broadcast_to([T, NT, E])

                def did(step):
                    after(dve, "dve", ph, step)

                lg = ps[0:T, 5, 0:NT * E].rearrange("p (t e) -> p t e", e=E)
                after(dve, "pe", ph, "gate")
                if n == 2:
                    TT(v(0), lg, rows[:, R_RB2, 0:E].unsqueeze(1).broadcast_to([T, NT, E]), ALU.add).then_inc(dve_step, 1)
                    did("logits")
                    top2(ph, v(0), E)
                    TT(s1[:, 7, :], s1[:, 4, :], s1[:, 2, :], ALU.subtract).then_inc(dve_step, 1)
                    after(dve, "act", ph, "exp")
                    TS(s1[:, 9, :], s1[:, 8, :], 1.0, None, ALU.add).then_inc(dve_step, 1)
                    did("plus")
                    V.reciprocal(s1[:, 6, :], s1[:, 9, :]).then_inc(dve_step, 1)
                    did("inv")
                    TT(s1[:, 1, :], s1[:, 8, :], s1[:, 6, :], ALU.mult).then_inc(dve_step, 1)
                    TT(v(9), v(4), one(6), ALU.mult).then_inc(dve_step, 1)
                    did("w1")
                    TT(v(10), v(7), one(1), ALU.mult).then_inc(dve_step, 1)
                    did("w2")
                    TT(v(8), v(9), v(10), ALU.add).then_inc(dve_step, 1)
                else:
                    V.tensor_copy(v(0), lg).then_inc(dve_step, 1)
                    did("logits")
                    V.reduce_max(s1[:, 0, :], v(0), AX.X).then_inc(dve_step, 1)
                    did("max")
                    TT(v(1), v(0), one(0), ALU.subtract).then_inc(dve_step, 1)
                    after(dve, "act", ph, "exp")
                    V.reduce_sum(s1[:, 1, :], v(2), AX.X).then_inc(dve_step, 1)
                    did("sum")
                    V.reciprocal(s1[:, 6, :], s1[:, 1, :]).then_inc(dve_step, 1)
                    did("recip")
                    TT(v(10), v(2), one(6), ALU.mult).then_inc(dve_step, 1)
                    did("probs")
                    top2(ph, v(10), E)
                    TT(v(9), v(4), v(7), ALU.add).then_inc(dve_step, 1)
                    STT(s1[:, 8, :], s1[:, 2, :], 1e-9 if n == 1 else 0.0, s1[:, 4, :], ALU.add, ALU.add).then_inc(dve_step, 1)
                    did("den")
                    V.reciprocal(s1[:, 9, :], s1[:, 8, :]).then_inc(dve_step, 1)
                    TT(v(11), v(9), v(10), ALU.mult).then_inc(dve_step, 1)
                    did("cp")
                    TT(v(8), v(11), one(9), ALU.mult).then_inc(dve_step, 1)
                did("W")
                if n != 1:
                    TT(x[:, :, :], x[:, :, :], (hbuf if n == 0 else y)[:, :, :], ALU.add).then_inc(dve_step, 1)
                    did("base")
                for e in range(E - 1):
                    after(dve, "pe", ph, f"y{e}")
                    for t in range(NT):
                        last = STT(x[:, t, :], ps[0:T, 4 + e % 2, t * D:(t + 1) * D], sm[:, 8, t * E + e:t * E + e + 1],
                                   x[:, t, :], ALU.mult, ALU.add)
                    last.then_inc(dve_step, 1)
                    if n == 1:
                        mask_by_key(2, e)
                    did(f"acc{e}")
                    if e == W_TURN + 1:
                        after(dve, "pe", ph, "b2")
                        TT(x[:, :, :], ps[0:T, 7, :].rearrange("p (t d) -> p t d", d=D), x[:, :, :], ALU.add).then_inc(dve_step, 1)
                        did("b2")
                if n == 1:
                    mask_by_key(2, B - 1)
                add_and_take_stats(ph, f"y{E - 1}_", f"acc{E - 1}_", take=n != 2,
                                   weight=lambda t: sm[:, 8, t * E + E - 1:t * E + E])

            V.memset(v_aug[:, :, :, :, 16:32], 1.0)
            V.memset(ones_b[:, :], 1.0)
            V.memset(qb[96:128, :, :, :, :], 0.0).then_inc(fills_done, 1)
            dve.wait_ge(x_in, 16)

            for ph in program_order():
                kind, n = ph
                if kind == "ln":
                    src, dst = ln_io(n)
                    if n in OWN_STATS:
                        for t in range(NT):
                            V.bn_stats(st[:, t, :], src[:, t, :]).then_inc(dve_step, 1)
                        after(dve, "dve", ph, f"stats{NT - 1}")
                    else:
                        after(dve, "dve", prior_of(ph), f"stats{NT - 1}")
                    for t in range(NT):
                        last = V.bn_aggr(mv[:, t, :], st[:, t, :])
                    last.then_inc(dve_step, 1)
                    after(dve, "dve", ph, "aggr")
                    TS(ve[:, :], mv[:, :, 1], 1e-5, None, ALU.add).then_inc(dve_step, 1)
                    after(dve, "pool", ph, "rstd")
                    for t in range(NT):
                        TS(dst[:, t, :], src[:, t, :], mv[:, t, 0:1], rstd[:, t:t + 1], ALU.subtract, ALU.mult).then_inc(dve_step, 1)
                    after(dve, "dve", ph, f"norm{NT - 1}")
                    if n == 0:
                        dve.wait_ge(kvw_in, 32)
                        for item in FIRST_ITEMS[0:KS]:
                            side(item)
                        dve.wait_ge(cst_in, 16)
                        V.tensor_copy(id16[:, :], ident)
                        TS(id_mask[:, :], ident, MASK, None, ALU.mult)
                        V.tensor_copy(id_b[:, :], ident)
                        V.tensor_copy(blk_b[0:T, :], cst[0:T, C_BLK:C_BLK + T])
                        V.tensor_copy(bm16[:, :], cst[:, C_BM:C_BM + H])
                        V.tensor_copy(m4[:, :], cst[:, C_M4:C_M4 + HQ]).then_inc(consts_ready, 1)
                elif kind == "sim":
                    TT(sim2[:, 0, :], sim[:, :], sim[:, :], ALU.mult).then_inc(dve_step, 1)
                    after(dve, "pe", ph, "sim2")
                    TS(sim2[:, 1, :], ps[:, 6, 0:E2], 1e-24, None, ALU.max).then_inc(dve_step, 1)
                elif kind == "count":
                    after(dve, "pe", ph, "count")
                    TS(keep[:, :], ps[:, 5, 0:TOK], KV - 0.5, None, ALU.is_lt).then_inc(dve_step, 1)
                elif kind == "q":
                    TS(sbias[:, :], xb[:, n, 2:6], q_scale(n), None, ALU.mult).then_inc(dve_step, 1)
                    after(dve, "pe", ph, "qn")
                    scale = q_scale(n)
                    if n == 2:
                        TS(qnf[:, :], ps[:, 4, 0:TOK], xb[:, n, 1:2], scale, ALU.add, ALU.mult).then_inc(dve_step, 1)
                        after(dve, "dve", ph, "qnf")
                        TT(qn16[:, :], qnf[:, :], keep[:, :], ALU.mult).then_inc(dve_step, 1)
                    else:
                        TS(qn16[:, :], ps[:, 4, 0:TOK], xb[:, n, 1:2], scale, ALU.add, ALU.mult).then_inc(dve_step, 1)
                    after(dve, "dve", ph, "q16")
                    dve.wait_ge(consts_ready, 1)
                    TT(qn[:, 0, :, :], qn16[:, 0:S].unsqueeze(1).broadcast_to([P, H, S]),
                       bm16[:, :].unsqueeze(2).broadcast_to([P, H, S]), ALU.mult).then_inc(first_qn_done, 1)
                    if n == 0:
                        for item in FIRST_ITEMS[KS:]:
                            side(item)
                    attention(n)
                elif kind == "out":
                    add_and_take_stats(ph, "projected", "added", banks=range(NT))
                elif kind == "moe":
                    moe(ph, n)
                elif kind == "self":
                    self_dve(dve, ph)
                elif kind == "gated":
                    gated_dve(dve, ph, top2)


def kernel(**inputs):
    from concourse.bass_utils import run_bass_kernel_spmd
    from concourse import bacc

    f = {k: np.asarray(v) for k, v in inputs.items()}
    f4 = np.float32

    def head_blocks(w):
        full = np.zeros((D, D), f4)
        for h in range(H):
            full[h * DH:(h + 1) * DH, h * DH:(h + 1) * DH] = w[h].T
        return full

    none = np.zeros(D, f4)
    layers = [
        (f["L0_xattn_Wq"], f["L0_xattn_Wk"], f["L0_xattn_Wv"], f["L0_xattn_Wo"],
         f["L0_xattn_bq"], f["L0_xattn_bk"], f["L0_xattn_bv"], f["L0_xattn_bo"]),
        (f["L1_xattn_W_Q"].T, f["L1_xattn_W_K"].T, f["L1_xattn_W_V"].T, f["L1_xattn_W_O"].T, none, none, none, none),
        (f["L2_xattn_Wq"].T, f["L2_xattn_Wk"].T, f["L2_xattn_Wv"].T, f["L2_xattn_Wo"].T,
         f["L2_xattn_bq"], f["L2_xattn_bk"], f["L2_xattn_bv"], f["L2_xattn_bo"]),
        (head_blocks(f["L3_xattn_wq"]), head_blocks(f["L3_xattn_wk"]), head_blocks(f["L3_xattn_wv"]), f["L3_xattn_wo"].T,
         f["L3_xattn_bq"].reshape(D), f["L3_xattn_bk"].reshape(D), f["L3_xattn_bv"].reshape(D), f["L3_xattn_bo"]),
    ]
    kvw = np.zeros((P, L, 256), f4)
    xw = np.zeros((L, P, 7 * D), f4)
    xb = np.zeros((P, L, 8), f4)
    rows = np.zeros((R_N, D), f4)
    for l, (wq, wk, wv, wo, bq, bk, bv, bo) in enumerate(layers):
        kvw[:, l, 0:D], kvw[:, l, D:] = wk, wv
        xw[l, :, 0:D] = wq
        xb[:, l, 0], xb[:, l, 1] = bk, bq
        for quad in range(QUADS):
            for blk in range(3):
                c = D * (1 + quad) + 32 * blk
                xw[l, :, c:c + 32] = wq[:, 32 * quad:32 * quad + 32]
                xb[32 * blk:32 * blk + 32, l, 2 + quad] = bq[32 * quad:32 * quad + 32]
        for t8 in range(8):
            r, j = divmod(t8, 4)
            xw[l, 32 * j:32 * j + 16, D * (5 + r):D * (6 + r)] = wo[16 * t8:16 * t8 + 16, :]
            xb[32 * j:32 * j + 16, l, 6 + r] = bv[16 * t8:16 * t8 + 16]
        rows[R_BO + l] = bo
    rows[R_FBO], rows[R_FBV] = f["L0_ffn_b_o"], f["L0_ffn_b_qkv"][2 * D:]
    rows[R_RB2, 0:E] = f["L3_ffn_rb2"]
    rows[R_GATE, 0:E2] = f["L2_ffn_gates"]

    p = np.arange(P)
    cst = np.zeros((P, C_W), f4)
    cst[:, C_ID:C_ID + P] = np.eye(P)
    for m in range(P):
        cst[m + 16 if m % 32 < 16 else m, C_PERM + m] = 1.0
    cst[:, C_BM:C_BM + H] = p[:, None] // DH == np.arange(H)
    cst[:, C_M4:C_M4 + HQ] = p[:, None] % 32 // DH == np.arange(HQ)
    cst[:, C_SEL:C_SEL + 2] = p[:, None] % 16 // DH == np.arange(2)
    q, k = np.arange(T)[:, None], np.arange(T)[None, :]
    cst[0:T, C_BLK:C_BLK + T] = np.where(q // S == k // S, 0.0, NEG)
    cst[0:T, C_CAU:C_CAU + T] = np.where((q // S == k // S) & (k <= q), 0.0, NEG)
    cst[:, C_RANK:C_RANK + E2] = E2 - np.arange(E2)

    def by_key(m):
        m = m.reshape(m.shape[:-1] + (KT, KK))
        return np.moveaxis(m, -1, 0)

    mask = f["mask_BxSxS2_bf0"]
    tri = f["mask_SxS2_bk0"]
    pad = f["mask_BxS2_bk1"]

    def experts(w1, w2):
        w2 = w2.reshape(E, FC, P, D).transpose(0, 2, 1, 3).reshape(E, P, FC * D)
        return np.concatenate([w1, w2], axis=2)

    moe = np.concatenate([experts(f["L0_ffn_w1"], f["L0_ffn_w2"]),
                          experts(f["L1_ffn_w1"].transpose(0, 2, 1), f["L1_ffn_w2"].transpose(0, 2, 1)),
                          experts(f["L3_ffn_we1"], f["L3_ffn_we2"])])
    b1 = np.stack([f["L0_ffn_b1"], f["L1_ffn_b1"], f["L3_ffn_be1"]]).reshape(3, E, FC, P).transpose(3, 0, 1, 2)
    b2 = np.stack([f["L0_ffn_b2"], f["L1_ffn_b2"], f["L3_ffn_be2"]], axis=1)
    wg = np.stack([f["L0_ffn_w_gate"], f["L1_ffn_router_w"].T, f["L3_ffn_rw2"]], axis=1)
    qkv2 = np.concatenate([f["L2_ffn_q_proj"], f["L2_ffn_k_proj"], f["L2_ffn_v_proj"]], axis=2)
    arrays = {
        "x": f["x"].reshape(TOK, D), "ctxT": f["ctx_1024"].transpose(0, 2, 1), "kvw": kvw, "xw": xw, "xb": xb,
        "rows": rows, "cst": cst, "mask": mask.transpose(1, 0, 2), "pad": pad, "tri": tri,
        "maskT": by_key(mask).transpose(0, 1, 3, 2), "triT": by_key(tri).transpose(0, 2, 1), "padT": by_key(pad),
        "moe": moe, "b1": b1, "b2": b2, "wg": wg,
        "fw": np.concatenate([f["L0_ffn_w_qkv"], f["L0_ffn_w_o"]], axis=1),
        "fb": np.stack([f["L0_ffn_b_qkv"][0:D], f["L0_ffn_b_qkv"][D:2 * D], f["L0_ffn_ln1_w"], f["L0_ffn_ln1_b"],
                        f["L0_ffn_ln2_w"], f["L0_ffn_ln2_b"]], axis=1), "rw1": f["L3_ffn_rw1"], "rb1": f["L3_ffn_rb1"].reshape(D, 1),
        "sim": f["L2_ffn_sim_matrix"], "qkv2": qkv2.transpose(1, 0, 2).reshape(D, E2 * 192),
        "o2": f["L2_ffn_o_proj"].reshape(EP, P, D).transpose(1, 0, 2).reshape(P, EP * D),
    }
    nc = bacc.Bacc("TRN2", target_bir_lowering=False, num_devices=1)
    given, aps = {}, {}
    for name, arr in arrays.items():
        arr = np.ascontiguousarray(arr)
        given[f"in_{name}"] = arr
        aps[name] = nc.dram_tensor(f"in_{name}", arr.shape, mybir.dt.from_np(arr.dtype), kind="ExternalInput").ap()
    out = nc.dram_tensor("out", (TOK, D), F32, kind="ExternalOutput").ap()
    build(nc, aps, out)
    r = run_bass_kernel_spmd(nc, [given], core_ids=[0])
    return r.results[0]["out"].reshape(B, S, D)
```
